# Optimizing a Trainium2 kernel written in Bass

```python
import numpy as np
import jax
import jax.numpy as jnp

def _softmax(x, axis=-1):
    return jax.nn.softmax(x, axis=axis)

def _gelu(x):
    return jax.nn.gelu(x, approximate=True)

def _silu(x):
    return jax.nn.silu(x)

def _sigmoid(x):
    return jax.nn.sigmoid(x)

def _layernorm(x, axis=-1, eps=1e-05):
    m = jnp.mean(x, axis=axis, keepdims=True)
    v = jnp.var(x, axis=axis, keepdims=True)
    return (x - m) / jnp.sqrt(v + eps)

def _scatter_add(tgt, idx, src, axis=0):
    return tgt.at[idx].add(src)

def _segment_sum(src, seg, n):
    return jax.ops.segment_sum(src, seg, n)
kernel_name = 'mk_adaln_d2_jaxref_r8_13753b'

def setup_inputs(seed: int=0):
    np.random.seed(seed)
    _w = jnp.asarray

    def _L0_attn_setup():
        import jax, jax.numpy as jnp
        import numpy as np
        DIM = 256
        D_STATE = 128
        EXPAND = 2
        HEADDIM = 64
        CHUNK = 64
        NGROUPS = 1
        D_INNER = EXPAND * DIM
        NHEADS = D_INNER // HEADDIM
        D_PROJ = D_INNER * 2 + NGROUPS * D_STATE * 2 + NHEADS
        BATCH, SEQ = (2, 512)
        EPS = 1e-05

        def segsum(x):
            T = x.shape[-1]
            xx = jnp.broadcast_to(x[..., :, None], x.shape + (T,))
            keep = jnp.tril(jnp.ones((T, T), dtype=bool), -1)
            xx = jnp.where(keep, xx, 0.0)
            s = jnp.cumsum(xx, axis=-2)
            tri = jnp.tril(jnp.ones((T, T), dtype=bool), 0)
            return jnp.where(tri, s, -jnp.inf)

        def rms_norm(x, w):
            return x * jax.lax.rsqrt(jnp.mean(x * x, axis=-1, keepdims=True) + EPS) * w

        def layer_norm(x, w, b):
            mu = jnp.mean(x, axis=-1, keepdims=True)
            var = jnp.mean((x - mu) ** 2, axis=-1, keepdims=True)
            return (x - mu) * jax.lax.rsqrt(var + EPS) * w + b

        def ssd_chunked(x, A, B, C, chunk):
            b, s, h, p = x.shape
            n = B.shape[-1]
            if B.shape[2] < h:
                r = h // B.shape[2]
                B = jnp.repeat(B, r, axis=2)
                C = jnp.repeat(C, r, axis=2)
            c = s // chunk
            x = x.reshape(b, c, chunk, h, p)
            A = A.reshape(b, c, chunk, h).transpose(0, 3, 1, 2)
            B = B.reshape(b, c, chunk, h, n)
            C = C.reshape(b, c, chunk, h, n)
            L = jnp.exp(segsum(A))
            Y_diag = jnp.einsum('bclhn,bcshn,bhcls,bcshp->bclhp', C, B, L, x)
            A_cumsum = jnp.cumsum(A, axis=-1)
            decay_states = jnp.exp(A_cumsum[..., -1:] - A_cumsum)
            states = jnp.einsum('bclhn,bhcl,bclhp->bchpn', B, decay_states, x)
            A_chunk = jnp.pad(A_cumsum[..., -1], ((0, 0), (0, 0), (1, 0)))
            decay_chunk = jnp.exp(segsum(A_chunk))
            new_states = jnp.einsum('bhzc,bchpn->bzhpn', decay_chunk[:, :, :c, 1:c + 1], states)
            Y_off = jnp.einsum('bclhn,bchpn,bhcl->bclhp', C, new_states, jnp.exp(A_cumsum))
            return (Y_diag + Y_off).reshape(b, s, h, p)

        def mamba3_forward(u, in_proj_w, out_proj_w, D, dt_bias, A_log, bnorm_w, cnorm_w, ln_w, ln_b):
            b, s, _ = u.shape
            u_n = layer_norm(u, ln_w, ln_b)
            proj = jnp.einsum('bsd,ed->bse', u_n, in_proj_w)
            z = proj[..., :D_INNER]
            x = proj[..., D_INNER:2 * D_INNER]
            B = proj[..., 2 * D_INNER:2 * D_INNER + NGROUPS * D_STATE].reshape(b, s, NGROUPS, D_STATE)
            C = proj[..., 2 * D_INNER + NGROUPS * D_STATE:2 * D_INNER + 2 * NGROUPS * D_STATE].reshape(b, s, NGROUPS, D_STATE)
            dt = proj[..., -NHEADS:]
            B = rms_norm(B, bnorm_w)
            C = rms_norm(C, cnorm_w)
            x = x.reshape(b, s, NHEADS, HEADDIM)
            z = z.reshape(b, s, NHEADS, HEADDIM)
            dt_proc = jax.nn.softplus(dt + dt_bias)
            A = -jnp.exp(A_log)
            dA = dt_proc * A
            y = ssd_chunked(x, dA, B, C, CHUNK)
            y = y + x * D[None, None, :, None]
            y = y.reshape(b, s, D_INNER)
            z_flat = z.reshape(b, s, D_INNER)
            y = y * jax.nn.silu(z_flat)
            return u + jnp.einsum('bse,de->bsd', y, out_proj_w)
        key = jax.random.key(seed)
        ks = jax.random.split(key, 6)
        u = jax.random.normal(ks[0], (BATCH, SEQ, DIM), dtype=jnp.float32)
        in_proj_w = jax.random.normal(ks[1], (D_PROJ, DIM), dtype=jnp.float32) * 0.02
        out_proj_w = jax.random.normal(ks[2], (DIM, D_INNER), dtype=jnp.float32) * 0.02
        D = jnp.ones((NHEADS,), dtype=jnp.float32)
        dt_bias = jax.random.normal(ks[3], (NHEADS,), dtype=jnp.float32) * 0.1
        A_log = jnp.log(0.5 + jax.random.uniform(ks[4], (NHEADS,), dtype=jnp.float32) * 0.5)
        bnorm_w = jnp.ones((D_STATE,), dtype=jnp.float32)
        cnorm_w = jnp.ones((D_STATE,), dtype=jnp.float32)
        ln_w = jnp.ones((DIM,), dtype=jnp.float32)
        ln_b = jnp.zeros((DIM,), dtype=jnp.float32)
        return {'u': u, 'in_proj_w': in_proj_w, 'out_proj_w': out_proj_w, 'D': D, 'dt_bias': dt_bias, 'A_log': A_log, 'bnorm_w': bnorm_w, 'cnorm_w': cnorm_w, 'ln_w': ln_w, 'ln_b': ln_b}
    _L0_attn_in = _L0_attn_setup()

    def _L0_ffn_setup():
        import jax, jax.numpy as jnp
        import numpy as np
        E = 64
        K = 8
        H = 256
        I = 96
        CAP = 64

        def _moe(hidden_states, gate_w, wg, wu, wd):
            B, S, Hd = hidden_states.shape
            x = hidden_states.reshape(-1, Hd)
            T = x.shape[0]
            logits = x @ gate_w.T
            probs = jax.nn.softmax(logits.astype(jnp.float32), axis=-1)
            w, sel = jax.lax.top_k(probs, K)
            w = w / jnp.sum(w, axis=-1, keepdims=True)
            w = w.astype(x.dtype)
            eid = sel.reshape(-1)
            tok = jnp.repeat(jnp.arange(T), K)
            oh = jax.nn.one_hot(eid, E, dtype=jnp.int32)
            pos = jnp.sum(jnp.cumsum(oh, axis=0) * oh, axis=-1) - 1
            valid = pos < CAP
            slot = jnp.where(valid, pos, CAP)
            xin = jnp.zeros((E, CAP + 1, Hd), x.dtype).at[eid, slot].set(x[tok])
            inp = xin[:, :CAP]
            h = jax.nn.silu(jnp.einsum('ech,ehi->eci', inp, wg)) * jnp.einsum('ech,ehi->eci', inp, wu)
            out = jnp.einsum('eci,eih->ech', h, wd)
            out_pad = jnp.concatenate([out, jnp.zeros((E, 1, Hd), out.dtype)], axis=1)
            g = out_pad[eid, slot] * (w.reshape(-1) * valid.astype(w.dtype))[:, None]
            y = jnp.zeros((T, Hd), x.dtype).at[tok].add(g)
            return y.reshape(B, S, Hd)
        key = jax.random.key(seed)
        k1, k2, k3, k4, k5 = jax.random.split(key, 5)
        hidden_states = jax.random.normal(k1, (1, 256, H), dtype=jnp.float32)
        gate_w = jax.random.normal(k2, (E, H), dtype=jnp.float32) * 0.02
        wg = jax.random.normal(k3, (E, H, I), dtype=jnp.float32) * 0.02
        wu = jax.random.normal(k4, (E, H, I), dtype=jnp.float32) * 0.02
        wd = jax.random.normal(k5, (E, I, H), dtype=jnp.float32) * 0.02
        return {'hidden_states': hidden_states, 'gate_w': gate_w, 'wg': wg, 'wu': wu, 'wd': wd}
    _L0_ffn_in = _L0_ffn_setup()
    _L0_c = _w((lambda *s: np.random.randn(*s).astype(np.float32) * 0.05)(1, 256))
    _L0_wmod = _w((lambda *s: np.random.randn(*s).astype(np.float32) * 0.05)(256, 6 * 256) * 256 ** (-0.5))

    def _L1_attn_setup():
        import jax, jax.numpy as jnp
        import numpy as np
        B, T, HID = (2, 256, 256)
        H, D, QC = (16, 128, 64)
        RD, THETA = (64, 10000.0)
        WIN = 64
        G, INTER = (4, 256)
        EPS = 1e-06

        def _rope_cache(t):
            inv = 1.0 / THETA ** (jnp.arange(0, RD, 2, dtype=jnp.float32) / RD)
            ang = jnp.arange(t, dtype=jnp.float32)[:, None] * inv[None, :]
            return (jnp.cos(ang), jnp.sin(ang))

        def _apply_partial_rope(x, cos, sin):
            x_rot, x_pass = (x[..., :RD], x[..., RD:])
            x1, x2 = (x_rot[..., :RD // 2], x_rot[..., RD // 2:])
            r1 = x1 * cos - x2 * sin
            r2 = x1 * sin + x2 * cos
            return jnp.concatenate([r1, r2, x_pass], axis=-1)

        def _rmsnorm(x, w):
            return x * jax.lax.rsqrt(jnp.mean(x * x, axis=-1, keepdims=True) + EPS) * w
        key = jax.random.key(seed)
        ks = jax.random.split(key, 10)
        s = 0.02
        return {'h': jax.random.normal(ks[0], (B, T, HID), jnp.float32), 'wq_comp': jax.random.normal(ks[1], (HID, QC), jnp.float32) * s, 'wq_up': jax.random.normal(ks[2], (QC, H * D), jnp.float32) * s, 'wk': jax.random.normal(ks[3], (HID, D), jnp.float32) * s, 'wv': jax.random.normal(ks[4], (HID, D), jnp.float32) * s, 'q_norm_w': jnp.ones((D,), jnp.float32), 'k_norm_w': jnp.ones((D,), jnp.float32), 'sink_logit': jnp.zeros((H,), jnp.float32), 'out_w1': jax.random.normal(ks[5], (G, H // G * D, INTER), jnp.float32) * s, 'out_w2': jax.random.normal(ks[6], (G * INTER, HID), jnp.float32) * s}
    _L1_attn_in = _L1_attn_setup()

    def _L1_ffn_setup():
        import jax, jax.numpy as jnp
        import numpy as np
        BLOCK_SIZE = 32
        HIDDEN_SIZE = 256
        MLP_DIM = 2048
        NVFP4_LUT = jnp.array([0.0, 0.5, 1.0, 1.5, 2.0, 3.0, 4.0, 6.0, 0.0, -0.5, -1.0, -1.5, -2.0, -3.0, -4.0, -6.0], dtype=jnp.float32)

        def dequant_nvfp4(W_packed, scales, block=BLOCK_SIZE):
            N = W_packed.shape[0]
            low = W_packed & 15
            high = W_packed >> 4 & 15
            idx = jnp.stack([low, high], axis=-1).reshape(N, -1)
            vals = NVFP4_LUT[idx]
            K = vals.shape[1]
            vals = vals.reshape(N, K // block, block) * scales[:, :, None]
            return vals.reshape(N, K)
        key = jax.random.key(seed)
        ks = jax.random.split(key, 7)
        x = jax.random.normal(ks[0], (4, 32, HIDDEN_SIZE), dtype=jnp.float32)
        gate_W_packed = jax.random.randint(ks[1], (MLP_DIM, HIDDEN_SIZE // 2), 0, 32, dtype=jnp.int32)
        gate_scales = jax.random.uniform(ks[2], (MLP_DIM, HIDDEN_SIZE // BLOCK_SIZE), dtype=jnp.float32) * 0.1 + 0.001
        up_W_packed = jax.random.randint(ks[3], (MLP_DIM, HIDDEN_SIZE // 2), 0, 32, dtype=jnp.int32)
        up_scales = jax.random.uniform(ks[4], (MLP_DIM, HIDDEN_SIZE // BLOCK_SIZE), dtype=jnp.float32) * 0.1 + 0.001
        down_W_packed = jax.random.randint(ks[5], (HIDDEN_SIZE, MLP_DIM // 2), 0, 32, dtype=jnp.int32)
        down_scales = jax.random.uniform(ks[6], (HIDDEN_SIZE, MLP_DIM // BLOCK_SIZE), dtype=jnp.float32) * 0.1 + 0.001
        return {'x': x, 'gate_W_packed': gate_W_packed, 'gate_scales': gate_scales, 'up_W_packed': up_W_packed, 'up_scales': up_scales, 'down_W_packed': down_W_packed, 'down_scales': down_scales}
    _L1_ffn_in = _L1_ffn_setup()
    _L1_c = _w((lambda *s: np.random.randn(*s).astype(np.float32) * 0.05)(1, 256))
    _L1_wmod = _w((lambda *s: np.random.randn(*s).astype(np.float32) * 0.05)(256, 6 * 256) * 256 ** (-0.5))
    _d = {'L0_attn_u': _L0_attn_in['u'], 'L0_attn_in_proj_w': _L0_attn_in['in_proj_w'], 'L0_attn_out_proj_w': _L0_attn_in['out_proj_w'], 'L0_attn_D': _L0_attn_in['D'], 'L0_attn_dt_bias': _L0_attn_in['dt_bias'], 'L0_attn_A_log': _L0_attn_in['A_log'], 'L0_attn_bnorm_w': _L0_attn_in['bnorm_w'], 'L0_attn_cnorm_w': _L0_attn_in['cnorm_w'], 'L0_attn_ln_w': _L0_attn_in['ln_w'], 'L0_attn_ln_b': _L0_attn_in['ln_b'], 'L0_ffn_gate_w': _L0_ffn_in['gate_w'], 'L0_ffn_wg': _L0_ffn_in['wg'], 'L0_ffn_wu': _L0_ffn_in['wu'], 'L0_ffn_wd': _L0_ffn_in['wd'], 'L0_c': _L0_c, 'L0_wmod': _L0_wmod, 'L1_attn_wq_comp': _L1_attn_in['wq_comp'], 'L1_attn_wq_up': _L1_attn_in['wq_up'], 'L1_attn_wk': _L1_attn_in['wk'], 'L1_attn_wv': _L1_attn_in['wv'], 'L1_attn_q_norm_w': _L1_attn_in['q_norm_w'], 'L1_attn_k_norm_w': _L1_attn_in['k_norm_w'], 'L1_attn_sink_logit': _L1_attn_in['sink_logit'], 'L1_attn_out_w1': _L1_attn_in['out_w1'], 'L1_attn_out_w2': _L1_attn_in['out_w2'], 'L1_ffn_gate_W_packed': _L1_ffn_in['gate_W_packed'], 'L1_ffn_gate_scales': _L1_ffn_in['gate_scales'], 'L1_ffn_up_W_packed': _L1_ffn_in['up_W_packed'], 'L1_ffn_up_scales': _L1_ffn_in['up_scales'], 'L1_ffn_down_W_packed': _L1_ffn_in['down_W_packed'], 'L1_ffn_down_scales': _L1_ffn_in['down_scales'], 'L1_c': _L1_c, 'L1_wmod': _L1_wmod}
    _x0 = _d['L0_attn_u']
    _d['L0_attn_u'] = jax.random.normal(jax.random.fold_in(jax.random.key(seed), 1), (1, 1024, 256), dtype=_x0.dtype)
    del _x0
    return _d

def reference(L0_attn_u, L0_attn_in_proj_w, L0_attn_out_proj_w, L0_attn_D, L0_attn_dt_bias, L0_attn_A_log, L0_attn_bnorm_w, L0_attn_cnorm_w, L0_attn_ln_w, L0_attn_ln_b, L0_ffn_gate_w, L0_ffn_wg, L0_ffn_wu, L0_ffn_wd, L0_c, L0_wmod, L1_attn_wq_comp, L1_attn_wq_up, L1_attn_wk, L1_attn_wv, L1_attn_q_norm_w, L1_attn_k_norm_w, L1_attn_sink_logit, L1_attn_out_w1, L1_attn_out_w2, L1_ffn_gate_W_packed, L1_ffn_gate_scales, L1_ffn_up_W_packed, L1_ffn_up_scales, L1_ffn_down_W_packed, L1_ffn_down_scales, L1_c, L1_wmod):

    def _L0_attn_ref(u, in_proj_w, out_proj_w, D, dt_bias, A_log, bnorm_w, cnorm_w, ln_w, ln_b):
        import jax, jax.numpy as jnp
        import numpy as np
        DIM = 256
        D_STATE = 128
        EXPAND = 2
        HEADDIM = 64
        CHUNK = 64
        NGROUPS = 1
        D_INNER = EXPAND * DIM
        NHEADS = D_INNER // HEADDIM
        D_PROJ = D_INNER * 2 + NGROUPS * D_STATE * 2 + NHEADS
        BATCH, SEQ = (2, 512)
        EPS = 1e-05

        def segsum(x):
            T = x.shape[-1]
            xx = jnp.broadcast_to(x[..., :, None], x.shape + (T,))
            keep = jnp.tril(jnp.ones((T, T), dtype=bool), -1)
            xx = jnp.where(keep, xx, 0.0)
            s = jnp.cumsum(xx, axis=-2)
            tri = jnp.tril(jnp.ones((T, T), dtype=bool), 0)
            return jnp.where(tri, s, -jnp.inf)

        def rms_norm(x, w):
            return x * jax.lax.rsqrt(jnp.mean(x * x, axis=-1, keepdims=True) + EPS) * w

        def layer_norm(x, w, b):
            mu = jnp.mean(x, axis=-1, keepdims=True)
            var = jnp.mean((x - mu) ** 2, axis=-1, keepdims=True)
            return (x - mu) * jax.lax.rsqrt(var + EPS) * w + b

        def ssd_chunked(x, A, B, C, chunk):
            b, s, h, p = x.shape
            n = B.shape[-1]
            if B.shape[2] < h:
                r = h // B.shape[2]
                B = jnp.repeat(B, r, axis=2)
                C = jnp.repeat(C, r, axis=2)
            c = s // chunk
            x = x.reshape(b, c, chunk, h, p)
            A = A.reshape(b, c, chunk, h).transpose(0, 3, 1, 2)
            B = B.reshape(b, c, chunk, h, n)
            C = C.reshape(b, c, chunk, h, n)
            L = jnp.exp(segsum(A))
            Y_diag = jnp.einsum('bclhn,bcshn,bhcls,bcshp->bclhp', C, B, L, x)
            A_cumsum = jnp.cumsum(A, axis=-1)
            decay_states = jnp.exp(A_cumsum[..., -1:] - A_cumsum)
            states = jnp.einsum('bclhn,bhcl,bclhp->bchpn', B, decay_states, x)
            A_chunk = jnp.pad(A_cumsum[..., -1], ((0, 0), (0, 0), (1, 0)))
            decay_chunk = jnp.exp(segsum(A_chunk))
            new_states = jnp.einsum('bhzc,bchpn->bzhpn', decay_chunk[:, :, :c, 1:c + 1], states)
            Y_off = jnp.einsum('bclhn,bchpn,bhcl->bclhp', C, new_states, jnp.exp(A_cumsum))
            return (Y_diag + Y_off).reshape(b, s, h, p)

        def mamba3_forward(u, in_proj_w, out_proj_w, D, dt_bias, A_log, bnorm_w, cnorm_w, ln_w, ln_b):
            b, s, _ = u.shape
            u_n = layer_norm(u, ln_w, ln_b)
            proj = jnp.einsum('bsd,ed->bse', u_n, in_proj_w)
            z = proj[..., :D_INNER]
            x = proj[..., D_INNER:2 * D_INNER]
            B = proj[..., 2 * D_INNER:2 * D_INNER + NGROUPS * D_STATE].reshape(b, s, NGROUPS, D_STATE)
            C = proj[..., 2 * D_INNER + NGROUPS * D_STATE:2 * D_INNER + 2 * NGROUPS * D_STATE].reshape(b, s, NGROUPS, D_STATE)
            dt = proj[..., -NHEADS:]
            B = rms_norm(B, bnorm_w)
            C = rms_norm(C, cnorm_w)
            x = x.reshape(b, s, NHEADS, HEADDIM)
            z = z.reshape(b, s, NHEADS, HEADDIM)
            dt_proc = jax.nn.softplus(dt + dt_bias)
            A = -jnp.exp(A_log)
            dA = dt_proc * A
            y = ssd_chunked(x, dA, B, C, CHUNK)
            y = y + x * D[None, None, :, None]
            y = y.reshape(b, s, D_INNER)
            z_flat = z.reshape(b, s, D_INNER)
            y = y * jax.nn.silu(z_flat)
            return u + jnp.einsum('bse,de->bsd', y, out_proj_w)
        return mamba3_forward(u, in_proj_w, out_proj_w, D, dt_bias, A_log, bnorm_w, cnorm_w, ln_w, ln_b)

    def _L0_ffn_ref(hidden_states, gate_w, wg, wu, wd):
        import jax, jax.numpy as jnp
        import numpy as np
        E = 64
        K = 8
        H = 256
        I = 96
        CAP = 64

        def _moe(hidden_states, gate_w, wg, wu, wd):
            B, S, Hd = hidden_states.shape
            x = hidden_states.reshape(-1, Hd)
            T = x.shape[0]
            logits = x @ gate_w.T
            probs = jax.nn.softmax(logits.astype(jnp.float32), axis=-1)
            w, sel = jax.lax.top_k(probs, K)
            w = w / jnp.sum(w, axis=-1, keepdims=True)
            w = w.astype(x.dtype)
            eid = sel.reshape(-1)
            tok = jnp.repeat(jnp.arange(T), K)
            oh = jax.nn.one_hot(eid, E, dtype=jnp.int32)
            pos = jnp.sum(jnp.cumsum(oh, axis=0) * oh, axis=-1) - 1
            valid = pos < CAP
            slot = jnp.where(valid, pos, CAP)
            xin = jnp.zeros((E, CAP + 1, Hd), x.dtype).at[eid, slot].set(x[tok])
            inp = xin[:, :CAP]
            h = jax.nn.silu(jnp.einsum('ech,ehi->eci', inp, wg)) * jnp.einsum('ech,ehi->eci', inp, wu)
            out = jnp.einsum('eci,eih->ech', h, wd)
            out_pad = jnp.concatenate([out, jnp.zeros((E, 1, Hd), out.dtype)], axis=1)
            g = out_pad[eid, slot] * (w.reshape(-1) * valid.astype(w.dtype))[:, None]
            y = jnp.zeros((T, Hd), x.dtype).at[tok].add(g)
            return y.reshape(B, S, Hd)
        return _moe(hidden_states, gate_w, wg, wu, wd)

    def _L1_attn_ref(h, wq_comp, wq_up, wk, wv, q_norm_w, k_norm_w, sink_logit, out_w1, out_w2):
        import jax, jax.numpy as jnp
        import numpy as np
        B, T, HID = (2, 256, 256)
        H, D, QC = (16, 128, 64)
        RD, THETA = (64, 10000.0)
        WIN = 64
        G, INTER = (4, 256)
        EPS = 1e-06

        def _rope_cache(t):
            inv = 1.0 / THETA ** (jnp.arange(0, RD, 2, dtype=jnp.float32) / RD)
            ang = jnp.arange(t, dtype=jnp.float32)[:, None] * inv[None, :]
            return (jnp.cos(ang), jnp.sin(ang))

        def _apply_partial_rope(x, cos, sin):
            x_rot, x_pass = (x[..., :RD], x[..., RD:])
            x1, x2 = (x_rot[..., :RD // 2], x_rot[..., RD // 2:])
            r1 = x1 * cos - x2 * sin
            r2 = x1 * sin + x2 * cos
            return jnp.concatenate([r1, r2, x_pass], axis=-1)

        def _rmsnorm(x, w):
            return x * jax.lax.rsqrt(jnp.mean(x * x, axis=-1, keepdims=True) + EPS) * w
        b, t, _ = h.shape
        cos, sin = _rope_cache(t)
        q = h @ wq_comp @ wq_up
        q = q.reshape(b, t, H, D).transpose(0, 2, 1, 3)
        q = _rmsnorm(_apply_partial_rope(q, cos, sin), q_norm_w)
        k = _rmsnorm(_apply_partial_rope(h @ wk, cos, sin), k_norm_w)
        v = h @ wv
        i = jnp.arange(t)
        diff = i[:, None] - i[None, :]
        mask = (diff >= 0) & (diff < WIN)
        scale = 1.0 / jnp.sqrt(jnp.asarray(D, h.dtype))
        scores = jnp.einsum('bhtd,bsd->bhts', q, k) * scale
        scores = jnp.where(mask[None, None], scores, jnp.asarray(-1e+30, h.dtype))
        sink = jnp.broadcast_to(sink_logit[None, :, None, None], (b, H, t, 1))
        probs = jax.nn.softmax(jnp.concatenate([scores, sink], axis=-1), axis=-1)
        attn = jnp.einsum('bhts,bsd->bhtd', probs[..., :t], v)
        x = attn.transpose(0, 2, 1, 3).reshape(b, t, G, H // G * D)
        x = jnp.einsum('btgi,gio->btgo', x, out_w1).reshape(b, t, G * INTER)
        return x @ out_w2

    def _L1_ffn_ref(x, gate_W_packed, gate_scales, up_W_packed, up_scales, down_W_packed, down_scales):
        import jax, jax.numpy as jnp
        import numpy as np
        BLOCK_SIZE = 32
        HIDDEN_SIZE = 256
        MLP_DIM = 2048
        NVFP4_LUT = jnp.array([0.0, 0.5, 1.0, 1.5, 2.0, 3.0, 4.0, 6.0, 0.0, -0.5, -1.0, -1.5, -2.0, -3.0, -4.0, -6.0], dtype=jnp.float32)

        def dequant_nvfp4(W_packed, scales, block=BLOCK_SIZE):
            N = W_packed.shape[0]
            low = W_packed & 15
            high = W_packed >> 4 & 15
            idx = jnp.stack([low, high], axis=-1).reshape(N, -1)
            vals = NVFP4_LUT[idx]
            K = vals.shape[1]
            vals = vals.reshape(N, K // block, block) * scales[:, :, None]
            return vals.reshape(N, K)
        B, S, H = x.shape
        xt = x.reshape(B * S, H)
        Wg = dequant_nvfp4(gate_W_packed, gate_scales)
        Wu = dequant_nvfp4(up_W_packed, up_scales)
        Wd = dequant_nvfp4(down_W_packed, down_scales)
        gate = jnp.einsum('th,nh->tn', xt, Wg)
        up = jnp.einsum('th,nh->tn', xt, Wu)
        gelu = jnp.tanh(0.7978845608028654 * (gate + 0.044715 * gate ** 3)) * gate * 0.5 + gate * 0.5
        inter = gelu * up
        out = jnp.einsum('tn,hn->th', inter, Wd)
        return out.reshape(B, S, H)
    x = L0_attn_u
    mod = (_silu(L0_c) @ L0_wmod).reshape(L0_c.shape[0], 6, 1, -1)
    sa, ca, ga, sb, cb, gb = (mod[:, 0], mod[:, 1], mod[:, 2], mod[:, 3], mod[:, 4], mod[:, 5])
    ga = (2 * (ga >= 0) - 1) * jnp.maximum(jnp.abs(ga), 0.25)
    gb = (2 * (gb >= 0) - 1) * jnp.maximum(jnp.abs(gb), 0.25)
    h = _layernorm(x, axis=-1) * (1 + ca) + sa
    x = x + ga * _L0_attn_ref(h, L0_attn_in_proj_w, L0_attn_out_proj_w, L0_attn_D, L0_attn_dt_bias, L0_attn_A_log, L0_attn_bnorm_w, L0_attn_cnorm_w, L0_attn_ln_w, L0_attn_ln_b)
    h = _layernorm(x, axis=-1) * (1 + cb) + sb
    x = x + gb * _L0_ffn_ref(h, L0_ffn_gate_w, L0_ffn_wg, L0_ffn_wu, L0_ffn_wd)
    mod = (_silu(L1_c) @ L1_wmod).reshape(L1_c.shape[0], 6, 1, -1)
    sa, ca, ga, sb, cb, gb = (mod[:, 0], mod[:, 1], mod[:, 2], mod[:, 3], mod[:, 4], mod[:, 5])
    ga = (2 * (ga >= 0) - 1) * jnp.maximum(jnp.abs(ga), 0.25)
    gb = (2 * (gb >= 0) - 1) * jnp.maximum(jnp.abs(gb), 0.25)
    h = _layernorm(x, axis=-1) * (1 + ca) + sa
    x = x + ga * _L1_attn_ref(h, L1_attn_wq_comp, L1_attn_wq_up, L1_attn_wk, L1_attn_wv, L1_attn_q_norm_w, L1_attn_k_norm_w, L1_attn_sink_logit, L1_attn_out_w1, L1_attn_out_w2)
    h = _layernorm(x, axis=-1) * (1 + cb) + sb
    x = x + gb * _L1_ffn_ref(h, L1_ffn_gate_W_packed, L1_ffn_gate_scales, L1_ffn_up_W_packed, L1_ffn_up_scales, L1_ffn_down_W_packed, L1_ffn_down_scales)
    return x

_drawn_inputs = setup_inputs


def setup_inputs(seed=0):
    import zlib

    import numpy as np

    out = dict(_drawn_inputs(seed))
    spreads = {'L0_attn_D': (1.0, 0.6),
     'L0_attn_bnorm_w': (1.0, 0.2),
     'L0_attn_cnorm_w': (1.0, 0.2),
     'L0_attn_ln_w': (1.0, 0.2),
     'L0_attn_ln_b': (0.0, 0.1),
     'L1_attn_q_norm_w': (1.0, 0.6),
     'L1_attn_k_norm_w': (1.0, 0.6),
     'L1_attn_sink_logit': (0.0, 2.0)}
    factors = {'L0_attn_dt_bias': 4.988,
     'L0_ffn_gate_w': 8.0,
     'L0_ffn_wg': 8.0,
     'L0_ffn_wu': 8.0,
     'L0_ffn_wd': 8.0,
     'L1_attn_wq_comp': 8.0,
     'L1_attn_wq_up': 8.0,
     'L1_attn_wk': 8.0,
     'L1_attn_wv': 7.855,
     'L1_attn_out_w1': 7.813,
     'L1_attn_out_w2': 7.839}
    for name, (base, spread) in spreads.items():
        noise = np.random.default_rng([zlib.crc32(name.encode()), seed]).standard_normal(out[name].shape)
        drawn = base * np.exp(spread * noise) if base else spread * noise
        out[name] = jnp.asarray(drawn.astype(out[name].dtype))
    for name, factor in factors.items():
        out[name] = (out[name] * factor).astype(out[name].dtype)
    return out
```

```python
import numpy as np
import concourse.bass as bass
from concourse import mybir
from contextlib import ExitStack

ARENA = 53100


def adaln_two_layers(nc, x_in, w_in, w_out, gate_w, wgu, wd, wmod, ccol, cols, rows, sinks, rope, consts,
                     wqc, wqup, wkv, w1, w2, gpk, upk, dpk, gsc, usc, dsc, out):
    f32, bf16, i16, i32, u32, f16 = (mybir.dt.float32, mybir.dt.bfloat16, mybir.dt.int16, mybir.dt.int32,
                                     mybir.dt.uint32, mybir.dt.float16)
    ALU = mybir.AluOpType
    ACT = mybir.ActivationFunctionType
    AX = mybir.AxisListType.X

    P = 128
    T = x_in.shape[0] // P
    DM = x_in.shape[1]
    KC = DM // P
    DI, H, HD, N = 512, 8, 64, 128
    E, CAP, TOPK, FI = 64, 64, 8, 96
    NOWHERE = 8192.0
    SLOTS = E * CAP

    xin = nc.dram_tensor("expert_in", (SLOTS, DM), f32, kind="Internal").ap()
    yex = nc.dram_tensor("expert_out", (SLOTS, DM), f32, kind="Internal").ap()

    ctx = ExitStack()
    with ctx:
        def sem(name):
            return ctx.enter_context(nc.semaphore(name))

        arena = ctx.enter_context(nc.sbuf_tensor("arena", [P, ARENA], f32))
        bank = [ctx.enter_context(nc.psum_tensor(f"bank{i}", [P, 512], f32)) for i in range(8)]

        def at(offset, *dims, parts=P):
            n = int(np.prod(dims))
            assert offset + n <= ARENA, (offset, dims)
            v = arena[0:parts, offset:offset + n]
            if len(dims) == 2:
                v = v.rearrange("p (a b) -> p a b", b=dims[1])
            elif len(dims) == 3:
                v = v.rearrange("p (a b c) -> p a b c", b=dims[1], c=dims[2])
            return v

        def packed(v, n):
            return v[:, 0:n]

        def over(v, n):
            return v.unsqueeze(2).to_broadcast([v.shape[0], v.shape[1], n])

        def under(v, n):
            return v.unsqueeze(1).to_broadcast([v.shape[0], n, v.shape[1]])

        x = at(0, T, DM)
        h = at(2048, T, DM)
        mod = [at(4096, 6, DM), at(5632, 6, DM)]
        con = at(7168, 6, P)
        ident, tri, tri_strict, mask_ssd, mask_first, mask_win = (con[:, i, :] for i in range(6))
        ident_b = at(7936, 64).bitcast(bf16)
        strict_b = at(8000, 64).bitcast(bf16)
        ones_b = at(8064, 64).bitcast(bf16)
        mask_ssd_b = at(8128, 256).bitcast(bf16)
        mask_first_b = at(8384, 256).bitcast(bf16)
        mask_win_b = at(8640, 256).bitcast(bf16)
        ones = at(8896, P)
        small = 9024
        ccol_s, cols_s, rows_s, sinks_s = at(small, 4), at(small + 4, 8), at(small + 560, 88), at(small + 36, 8)
        eps5, eps6, one_c = at(small + 44, 1), at(small + 45, 1), at(small + 46, 1)
        silu_c, silu_t = at(small + 48, 4), at(small + 52, 4)
        stats = at(small + 64, T, 6)
        mv = [at(small + 112 + 16 * i, T, 2) for i in range(5)]
        rstd = [at(small + 192 + 8 * i, T) for i in range(5)]
        w8 = at(small + 240, T, TOPK)
        slot8 = at(small + 304, T, TOPK)
        gather8 = at(small + 368, T, TOPK).bitcast(u32)
        scatter8 = at(small + 432, T, TOPK).bitcast(u32)
        wbc = at(small + 496, 1)
        wqk = at(small + 497, 1)
        rope_s = at(10048, T, 64)

        A0 = 10560
        uT = at(A0, KC, T * P)
        zs = at(A0 + 2048, T, DI)
        xs = at(A0 + 6144, T, DI)
        bc = at(A0 + 10240, T, 2 * N + H)
        state = at(A0 + 12352, 2, DI)
        w_in_s = at(A0 + 13376, KC, w_in.shape[2])
        w_out_s = at(A0 + 15952, 4, DM)
        cT = at(A0 + 16976, T, P)
        bT = at(A0 + 18000, T, P)
        bn = at(A0 + 19024, T, P)
        gate_s = at(A0 + 20048, KC, E)
        un = at(A0 + 20176, T, DM)
        Lm = at(A0 + 22224, 2, H * P)
        xdec = at(A0 + 24272, 2, DI)
        xD = at(A0 + 25296, 2, DI)
        yT = at(A0 + 26320, 2, DI)
        ez = at(A0 + 27344, 2, DI)
        un_y, yo_s = at(A0 + 20176, 2, DI), at(A0 + 21200, DI)
        junk = at(A0 + 28368, 2, P)
        dt = [at(A0 + 28624 + 64 * i, T * H) for i in range(4)]
        wmod_s = [at(A0 + 2048, KC, 6 * DM), at(A0 + 5120, KC, 6 * DM)]
        scb = at(A0 + 22224, 4, P)
        A1 = A0 + 28880
        ss = at(A1, T, 2)
        rbc = at(A1 + 16, T * 2)
        dA = at(A1 + 32, T, H)
        ncs, ecs, dec, etot = (at(A1 + 96 + 64 * i, T, H) for i in range(4))
        nA = at(A1 + 352, H)
        zero = at(A1 + 360, 1024)
        gabs = at(A0 + 20176, 4, DM)

        ld_x, ld_con, ld_mod, ld_small, ld_win, ld_wout, ld_gate = map(
            sem, ["ld_x", "ld_con", "ld_mod", "ld_small", "ld_win", "ld_wout", "ld_gate"])
        zero_set, xin_zeroed = sem("zero_set"), sem("xin_zeroed")
        dve_chain, act_chain, pool_chain = sem("dve_chain"), sem("act_chain"), sem("pool_chain")
        consts_ready, pool_consts = sem("consts_ready"), sem("pool_consts")
        exp_c, silu_ready, mod_mm, mod_copied, = map(sem, ["exp_c", "silu_ready", "mod_mm", "mod_copied"])
        var_ready, rstd_ready = sem("var_ready"), sem("rstd_ready")
        un_ready, uT_mm, uT_ready = sem("un_ready"), sem("uT_mm"), sem("uT_ready")
        proj_z, proj_x, proj_bc = sem("proj_z"), sem("proj_x"), sem("proj_bc")
        z_ready, xs_ready, bc_ready = map(sem, ["z_ready", "xs_ready", "bc_ready"])
        dt_abs, dt_log, dA_ready, cs_mm, cs_used, decs_in, decs_ready = map(
            sem, ["dt_abs", "dt_log", "dA_ready", "cs_mm", "cs_used", "decs_in", "decs_ready"])
        rbc_ready, bcn_ready, bcT_mm, bcT_ready = map(sem, ["rbc_ready", "bcn_ready", "bcT_mm", "bcT_ready"])
        csrow_mm, G_mm, L_ready, M_ready = map(sem, ["csrow_mm", "G_mm", "L_ready", "M_ready"])
        xdec_ready, Yd_mm, Yo_mm, st_mm, state_ready, y_ready = map(
            sem, ["xdec_ready", "Yd_mm", "Yo_mm", "st_mm", "state_ready", "y_ready"])
        yT_mm, yT_ready, o_mm, x1_ready = map(sem, ["yT_mm", "yT_ready", "o_mm", "x1_ready"])

        NS = 13
        PAIR = 4 * KC * FI + 2 * DM
        X0 = A1 + 1392
        slot_at = [X0 + PAIR * i if i < 4 else A0 + PAIR * (i - 4) for i in range(NS)]
        wgu_s = [at(o, 2, 2 * KC * FI) for o in slot_at]
        wd_s = [at(o + 4 * KC * FI, 2, DM, parts=FI) for o in slot_at]
        XB = X0 + 4 * PAIR
        xg = [at(XB + 512 * i, 2, DM) for i in range(2)]
        xgT = [at(XB + 1024 + 512 * i, 4, P) for i in range(2)]
        sg = [at(XB + 2048 + 256 * i, 4 * CAP, parts=FI) for i in range(2)]
        hidT = [at(XB + 2560 + 256 * i, 4 * CAP, parts=FI) for i in range(2)]
        ob = [at(XB + 3072 + 1024 * i, 4, DM, parts=CAP) for i in range(2)]
        NG = E // 4
        R0 = A0 + 23808
        h2T = [at(A0 + 28368 + 256 * i, KC, P) for i in range(2)]
        prob, rest, wfull, slotv, wvalid, eqk, mask, valid = (at(R0 + 512 * i, T, E) for i in range(8))
        mask_b, run_b = (at(A0 + 27904 + 256 * i, 256).bitcast(bf16).rearrange("p (a b) -> p a b", b=E) for i in range(2))
        top8 = at(A1, T, TOPK)
        rmax, rsum = at(A1 + 64, T), at(A1 + 72, T)

        h2_ready, h2T_mm, h2T_ready, logits_mm, lmax_ready, exp_ready = map(
            sem, ["h2_ready", "h2T_mm", "h2T_ready", "logits_mm", "lmax_ready", "exp_ready"])
        mask_ready, pos_mm, slots_ready, scattered = map(sem, ["mask_ready", "pos_mm", "slots_ready", "scattered"])
        w_loaded = [sem(f"w_loaded{i}") for i in range(NS)]
        xg_loaded = [sem(f"xg_loaded{i}") for i in range(2)]
        xgT_mm, xgT_ready, gu_mm, sg_ready, hid_ready, down_mm, ob_left, ob_right = map(
            sem, ["xgT_mm", "xgT_ready", "gu_mm", "sg_ready", "hid_ready", "down_mm", "ob_left", "ob_right"])
        ob_stored = [sem(f"ob_stored{i}") for i in range(2)]
        w8_ready, x2_ready = sem("w8_ready"), sem("x2_ready")
        gathered = [sem(f"gathered{i}") for i in range(2)]
        gath = [at(A0 + 2048 * i, TOPK, DM) for i in range(2)]
        tmp2 = at(A0 + 11008, DM)
        B0 = A0 + 11520
        MLP = 2048
        NT = MLP // P
        wg_s, wu_s = at(B0, 2, MLP), at(B0 + 4096, 2, MLP)
        wdn_s = at(B0 + 8192, NT, DM)
        QC = 512
        D0 = A0 + 23808
        pk = [at(D0 + 512 * i, QC) for i in range(2)]
        sc = [at(D0 + 1024 + 512 * i, QC) for i in range(2)]
        nib = [[at(D0 + 2048 + 256 * (3 * b + i), QC // 2) for i in range(3)] for b in range(2)]
        NQ = 3 * MLP // QC
        DEC_LOADS = [sum((48 if m >= 8 else 32) for m in range(n % 2, n + 1, 2)) for n in range(NQ)]
        NH, QD, WIN = 16, 64, 64
        PR = NH // 2
        w1_s, w2_s = at(A0 + 4096, NH, DM), at(A0 + 8192, 8, DM)
        wqc_s, wkv_s = at(A0 + 10240, KC, QD), at(A0 + 10368, KC, 2 * P)
        qk = at(D0, NH + 1, P)
        kT = at(D0 + 2176, WIN + T * P)
        Vw = [at(D0 + 3264 + 128 * i, P) for i in range(4)]
        PT = at(D0 + 3776, PR, P)
        oT1 = at(A1, 8, P)
        wqup_s = at(X0, NH * P, parts=QD)
        hT = at(X0 + 2048, KC, WIN + T * P)
        tmp = at(X0 + 4224, NH + 1, P)
        qT = at(X0 + 6400, 2, NH, WIN)
        Pb = at(X0 + 8448, PR, P)
        aT = at(X0 + 9472, NH, P)
        qcT = at(A1 + 1024, P, parts=QD)
        sm = small + 660
        ssq, rq = at(sm, NH + 1), at(sm + 20, NH + 1)
        st1, mv1, rs1 = at(sm + 40, 6), at(sm + 48, 2), at(sm + 50, 1)
        mx, es, den = at(sm + 56, PR), at(sm + 64, PR), at(sm + 72, PR)

        pk_loaded = [sem(f"pk_loaded{i}") for i in range(2)]
        dec_done = sem("dec_done")
        ld_w1, ld_w2, ld_wq, ld_wqup = map(sem, ["ld_w1", "ld_w2", "ld_wq", "ld_wqup"])
        pads = sem("pads")
        mom_ready, mom_rstd, ha_ready, haT_mm, haT_ready, qcT_mm, qcT_ready, kv_mm, kv_ready = map(
            sem, ["mom_ready", "mom_rstd", "ha_ready", "haT_mm", "haT_ready", "qcT_mm", "qcT_ready", "kv_mm", "kv_ready"])
        q_mm, sq_ready, ssq_ready, rq_ready, qn_ready, rope_dve, rope_pool = map(
            sem, ["q_mm", "sq_ready", "ssq_ready", "rq_ready", "qn_ready", "rope_dve", "rope_pool"])
        qT_mm, qT_ready, s_mm, mx_ready, p_ready, pn_ready, PT_mm, PT_ready, av_mm, av_ready = map(
            sem, ["qT_mm", "qT_ready", "s_mm", "mx_ready", "p_ready", "pn_ready", "PT_mm", "PT_ready", "av_mm", "av_ready"])
        o1_mm, o1_ready, o2_mm, x3_ready = map(sem, ["o1_mm", "o1_ready", "o2_mm", "x3_ready"])
        gl = [at(D0 + 512 * i, 512) for i in range(3)]
        it = [at(D0 + 1536 + 512 * i, 512) for i in range(3)]
        h4_ready, h4T_mm, h4T_ready, mgu_mm, gl_ready, it_ready, dn_mm, fin_ready, out_stored, mdn_mm = map(
            sem, ["h4_ready", "h4T_mm", "h4T_ready", "mgu_mm", "gl_ready", "it_ready", "dn_mm", "fin_ready", "out_stored", "mdn_mm"])
        block = ctx.enter_context(nc.Block())

        @block.sync
        def _(sp):
            sp.dma_start(ccol_s, ccol).then_inc(ld_small, 16)
            sp.dma_start(x, x_in.rearrange("(t p) c -> p t c", p=P)).then_inc(ld_x, 16)
            sp.dma_start(at(A0 + 2048, 2, KC * 6 * DM), wmod.rearrange("l p j n -> p l (j n)")).then_inc(ld_mod, 16)
            sp.dma_start(cols_s, cols).then_inc(ld_small, 16)
            sp.dma_start(rows_s, rows.to_broadcast([P, rows.shape[1]])).then_inc(ld_small, 16)
            for i in range(2):
                sp.dma_start(sinks_s[64 * i:64 * i + 64, :], sinks[i:i + 1, :].to_broadcast([64, 8])).then_inc(ld_small, 16)
            sp.dma_start(con, consts).then_inc(ld_con, 16)
            sp.dma_start(w_in_s, w_in).then_inc(ld_win, 16)
            sp.dma_start(w_out_s, w_out).then_inc(ld_wout, 16)
            sp.dma_start(gate_s, gate_w).then_inc(ld_gate, 16)
            sp.dma_start(rope_s, rope).then_inc(ld_small, 16)
            sp.wait_ge(zero_set, 1)
            sp.dma_start(xin.rearrange("(p r a) c -> p r (a c)", p=P, r=8), under(zero, 8)).then_inc(xin_zeroed, 16)
            def load_pair(q, sp=sp):
                i = q % NS
                if q == 4:
                    sp.wait_ge(yT_mm, T)
                    sp.wait_ge(bc_ready, T)
                if q >= NS:
                    sp.wait_ge(down_mm, (q - NS) // 2 + 1)
                sp.dma_start(wgu_s[i].rearrange("p a b -> p (a b)"), wgu[q]).then_inc(w_loaded[i], 16)
                sp.dma_start(wd_s[i].rearrange("p a b -> p (a b)"), wd[q]).then_inc(w_loaded[i], 16)

            def load_codes(n):
                which, c, i = n // 4, n % 4, n % 2
                if n == 0:
                    sp.wait_ge(w8_ready, 1)
                if n >= 2:
                    sp.wait_ge(dec_done, n - 1)
                if which < 2:
                    src, scales = ((gpk, gsc), (upk, usc))[which]
                    sp.dma_start(pk[i].bitcast(i32), src[:, c * QC:(c + 1) * QC]).then_inc(pk_loaded[i], 16)
                    sp.dma_start(sc[i], scales[:, c * QC:(c + 1) * QC].unsqueeze(1).to_broadcast([8, 16, QC])).then_inc(pk_loaded[i], 16)
                else:
                    sp.dma_start(pk[i].bitcast(i32).rearrange("p (a b) -> p a b", b=DM), dpk[:, 2 * c:2 * c + 2, :]).then_inc(pk_loaded[i], 16)
                    for a in range(2):
                        sp.dma_start(sc[i][:, a * DM:(a + 1) * DM],
                                     dsc[8 * (2 * c + a):8 * (2 * c + a) + 8, :].unsqueeze(1).to_broadcast([8, 16, DM])).then_inc(pk_loaded[i], 16)

            for q in range(NS):
                load_pair(q)
            sp.wait_ge(scattered, 16 * T * TOPK)
            for g in range(NG + 2):
                if g < NG:
                    if g >= 2:
                        sp.wait_ge(xgT_mm, g - 1)
                    sp.dma_start(xg[g % 2], xin[4 * CAP * g:4 * CAP * (g + 1), :].rearrange("(q p) c -> p q c", p=P))                        .then_inc(xg_loaded[g % 2], 16)
                if g >= 2:
                    sp.wait_ge(ob_left, g - 1)
                    sp.wait_ge(ob_right, g - 1)
                    sp.dma_start(yex[4 * CAP * (g - 2):4 * CAP * (g - 1), :].rearrange("(e s) c -> s e c", s=CAP), ob[g % 2])                        .then_inc(ob_stored[g % 2], 16)
                    if g - 2 < NQ:
                        load_codes(g - 2)
                    for q in (2 * g + NS - 4, 2 * g + NS - 3):
                        if NS <= q < E // 2:
                            load_pair(q)
            for i in range(2):
                sp.wait_ge(ob_stored[i], 16 * NG // 2)
            sp.wait_ge(down_mm, NG)
            sp.dma_start(wqup_s, wqup).then_inc(ld_wqup, 16)
            sp.dma_start(wqc_s, wqc).then_inc(ld_wq, 16)
            sp.dma_start(wkv_s, wkv).then_inc(ld_wq, 16)
            sp.dma_start(w1_s, w1).then_inc(ld_w1, 16)
            sp.dma_start(w2_s, w2).then_inc(ld_w2, 16)
            for t in range(T):
                sp.wait_ge(fin_ready, t + 1)
                sp.dma_start(out[t * P:(t + 1) * P, :], x[:, t, :]).then_inc(out_stored, 16)
            sp.wait_ge(out_stored, 16 * T)

        @block.gpsimd
        def _(pool):
            pool.memset(zero, 0.0).then_inc(zero_set, 1)
            for v, value in ((ones, 1.0), (eps5, 1e-5), (eps6, 1e-6), (one_c, 1.0)):
                pool.memset(v, value).then_inc(pool_consts, 1)
            pool.memset(ones_b, 1.0).then_inc(pool_consts, 1)
            pool.wait_ge(ld_con, 16)
            pool.tensor_copy(ident_b, ident).then_inc(pool_consts, 1)
            pool.tensor_copy(strict_b, tri_strict).then_inc(pool_consts, 1)
            for b, m in ((mask_ssd_b, mask_ssd), (mask_first_b, mask_first), (mask_win_b, mask_win)):
                pool.tensor_copy(b.rearrange("p (r c) -> p r c", c=P), under(m, 4)).then_inc(pool_consts, 1)
            pool.wait_ge(decs_ready, 3)
            for t in range(T):
                pool.wait_ge(xs_ready, t + 1)
                xt = xs[:, t, :].rearrange("p (a b) -> p a b", b=HD)
                if t >= 2:
                    pool.wait_ge(st_mm, t - 1)
                    pool.wait_ge(y_ready, t - 1)
                pool.tensor_tensor(xdec[:, t % 2, :].rearrange("p (a b) -> p a b", b=HD), xt,
                                   over(dec[:, t, :], HD), ALU.mult).then_inc(xdec_ready, 1)
                pool.tensor_tensor(xD[:, t % 2, :].rearrange("p (a b) -> p a b", b=HD), xt,
                                   over(rows_s[:, 0:H], HD), ALU.mult).then_inc(xdec_ready, 1)

            pool.wait_ge(xin_zeroed, 16)
            pool.wait_ge(slots_ready, 1)
            for t in range(T):
                pool.wait_ge(h2_ready, t + 1)
                for k in range(TOPK):
                    pool.indirect_dma_start(xin, bass.IndirectOffsetOnAxis(scatter8[:, t, k:k + 1], 0), h[:, t, :], None,
                                            bounds_check=SLOTS - 1, oob_is_err=False).then_inc(scattered, 16)
            for i in range(2):
                pool.wait_ge(ob_stored[i], 16 * NG // 2)
            pool.wait_ge(down_mm, NG)
            def gather(t):
                if t >= 2:
                    pool.wait_ge(x2_ready, t - 1)
                for k in range(TOPK):
                    pool.indirect_dma_start(gath[t % 2][:, k, :], None, yex, bass.IndirectOffsetOnAxis(gather8[:, t, k:k + 1], 0),
                                            bounds_check=SLOTS - 1, oob_is_err=False).then_inc(gathered[t % 2], 16)

            pool.memset(kT[:, 0:WIN], 0.0).then_inc(pads, 1)
            pool.memset(hT[:, :, 0:WIN], 0.0).then_inc(pads, 1)
            gather(0)
            gather(1)
            for t in range(T):
                pool.wait_ge(qn_ready, 5 * (t + 1))
                cos, sin = under(rope_s[:, t, 0:32], NH + 1), under(rope_s[:, t, 32:64], NH + 1)
                pool.tensor_tensor(tmp[:, :, 64:96], qk[:, :, 0:32], sin, ALU.mult).then_inc(rope_pool, 1)
                pool.tensor_tensor(tmp[:, :, 96:128], qk[:, :, 32:64], cos, ALU.mult).then_inc(rope_pool, 1)
                pool.wait_ge(rope_pool, 3 * t + 2)
                pool.wait_ge(rope_dve, 2 * t + 1)
                pool.tensor_tensor(qk[:, :, 32:64], tmp[:, :, 64:96], tmp[:, :, 96:128], ALU.add).then_inc(rope_pool, 1)
                if t + 2 < T:
                    gather(t + 2)
        @block.scalar
        def _(act):
            chained = [0]

            def link(ins):
                chained[0] += 1
                ins.then_inc(act_chain, 1)
                act.wait_ge(act_chain, chained[0])

            def rsqrt(o, i, scale, eps, done):
                link(act.activation(o, i, ACT.Ln, bias=eps, scale=scale))
                act.activation(o, o, ACT.Exp, scale=-0.5).then_inc(done, 1)

            act.preload_act_table_set("natural_log_exp_and_others")
            act.wait_ge(ld_small, 96)
            act.activation(silu_t, ccol_s, ACT.Exp, scale=-1.0).then_inc(exp_c, 1)
            for n in range(6):
                act.wait_ge(mod_mm, n + 1)
                act.activation(at(4096 + 512 * n, 512), bank[n][:, :], ACT.Copy).then_inc(mod_copied, 1)
            act.wait_ge(pool_consts, 10)
            for i in range(2):
                act.wait_ge(var_ready, i + 1)
                rsqrt(rstd[i], mv[i][:, :, 1], 1.0, eps5, rstd_ready)
            for t in range(T):
                act.wait_ge(uT_mm, t + 1)
                for j in range(KC):
                    act.activation(uT[:, j, t * P:(t + 1) * P], bank[6 + t % 2][:, j * P:(j + 1) * P], ACT.Identity,
                                   scale=cols_s[:, j:j + 1], bias=cols_s[:, 2 + j:3 + j]).then_inc(uT_ready, 1)
            act.preload_act_table_set("silu_and_others")
            for t in range(T):
                b = 3 * (t % 2)
                act.wait_ge(proj_z, t + 1)
                act.activation(zs[:, t, :], bank[b][:, :], ACT.Silu).then_inc(z_ready, 1)
                act.wait_ge(proj_x, t + 1)
                act.activation(xs[:, t, :], bank[b + 1][:, :], ACT.Copy).then_inc(xs_ready, 1)
                act.wait_ge(proj_bc, t + 1)
                if t >= 1:
                    act.wait_ge(bc_ready, t)
                act.activation(bc[:, t, :], bank[b + 2][:, 0:2 * N + H], ACT.Copy)
                for j in range(2):
                    ins = act.activation(junk[:, j, :], bank[b + 2][:, j * N:(j + 1) * N], ACT.Square,
                                         accum_out=ss[:, t, j:j + 1])
                ins.then_inc(bc_ready, 1)
            act.wait_ge(bc_ready, T)
            act.preload_act_table_set("natural_log_exp_and_others")
            rsqrt(rbc, ss.rearrange("p a b -> p (a b)"), 1.0 / N, eps5, rbc_ready)
            act.activation(nA, rows_s[:, 16:24], ACT.Exp).then_inc(dt_log, 1)
            act.wait_ge(dt_abs, 1)
            link(act.activation(dt[2], dt[1], ACT.Exp))
            act.activation(dt[2], dt[2], ACT.Ln, bias=1.0).then_inc(dt_log, 1)
            act.wait_ge(decs_in, 1)
            act.activation(ecs.rearrange("p a b -> p (a b)"), bank[6][:, 0:T * H], ACT.Exp).then_inc(decs_ready, 1)
            act.activation(etot.rearrange("p a b -> p (a b)"), bank[6][:, T * H:2 * T * H], ACT.Exp).then_inc(decs_ready, 1)
            act.activation(dec, dec, ACT.Exp).then_inc(decs_ready, 1)
            for t in range(T):
                act.wait_ge(bcT_mm, t + 1)
                act.activation(bT[:, t, :], bank[6 + t % 2][:, 0:P], ACT.Copy).then_inc(bcT_ready, 1)
                act.activation(cT[:, t, :], bank[6 + t % 2][:, P:2 * P], ACT.Copy, scale=wbc).then_inc(bcT_ready, 1)
            for t in range(T):
                b = 6 * (t % 2)
                act.wait_ge(csrow_mm, t + 1)
                if t >= 2:
                    act.wait_ge(Yd_mm, t - 1)
                for i in range(H):
                    ins = act.activation(Lm[:, t % 2, i * P:(i + 1) * P], bank[b + i // 4][:, (i % 4) * P:(i % 4 + 1) * P],
                                         ACT.Exp, bias=ncs[:, t, i:i + 1])
                ins.then_inc(L_ready, 1)
            for t in range(T):
                act.wait_ge(yT_mm, t + 1)
                if t >= 2:
                    act.wait_ge(o_mm, t - 1)
                act.activation(yT[:, t % 2, :], bank[6 + t % 2][:, :], ACT.Copy).then_inc(yT_ready, 1)

            act.wait_ge(var_ready, 3)
            rsqrt(rstd[2], mv[2][:, :, 1], 1.0, eps5, rstd_ready)
            for t in range(T):
                act.wait_ge(h2T_mm, t + 1)
                if t >= 2:
                    act.wait_ge(logits_mm, t - 1)
                act.activation(h2T[t % 2].rearrange("p a b -> p (a b)"), bank[2 + t % 2][:, 0:DM], ACT.Copy).then_inc(h2T_ready, 1)
            act.wait_ge(lmax_ready, 1)
            act.activation(prob, prob, ACT.Exp).then_inc(exp_ready, 1)
            act.wait_ge(exp_ready, 1)
            act.preload_act_table_set("silu_and_others")
            def copy_rows(g):
                act.wait_ge(xgT_mm, g + 1)
                if g >= 2:
                    act.wait_ge(gu_mm, g - 1)
                act.activation(xgT[g % 2].rearrange("p a b -> p (a b)"), bank[g % 2][:, :], ACT.Copy).then_inc(xgT_ready, 1)

            copy_rows(0)
            for g in range(NG + 1):
                if g + 1 < NG:
                    copy_rows(g + 1)
                if g < NG:
                    act.wait_ge(gu_mm, g + 1)
                    if g >= 2:
                        act.wait_ge(hid_ready, g - 1)
                    act.activation(sg[g % 2], bank[2 + g % 2][0:FI, 0:4 * CAP], ACT.Silu).then_inc(sg_ready, 1)
                if g >= 1:
                    i = (g - 1) % 2
                    act.wait_ge(down_mm, g)
                    if g >= 3:
                        act.wait_ge(ob_stored[i], 16 * ((g - 1) // 2))
                    act.activation(ob[i][:, 0:2, :].rearrange("p a b -> p (a b)"), bank[4 + 2 * i][0:CAP, :],
                                   ACT.Copy).then_inc(ob_left, 1)
            act.wait_ge(down_mm, NG)
            act.preload_act_table_set("natural_log_exp_and_others")

            def act_front(t):
                act.wait_ge(mom_ready, t + 1)
                rsqrt(rs1, mv1[:, 1:2], 1.0, eps5, mom_rstd)
                act.wait_ge(haT_mm, t + 1)
                act.activation(hT[:, :, WIN + t * P:WIN + (t + 1) * P], bank[4][:, 0:DM].rearrange("p (a b) -> p a b", b=P),
                               ACT.Copy).then_inc(haT_ready, 1)
                act.wait_ge(qcT_mm, t + 1)
                act.activation(qcT, bank[5][0:QD, 0:P], ACT.Copy).then_inc(qcT_ready, 1)
                act.wait_ge(kv_mm, t + 1)
                if t >= 2:
                    act.wait_ge(av_mm, 2 * t - 2)
                act.activation(Vw[(2 * t + 1) % 4], bank[6][:, P:2 * P], ACT.Copy)
                act.activation(Vw[(2 * t) % 4], bank[6][:, 2 * P:3 * P], ACT.Copy)
                if t >= 1:
                    act.wait_ge(rope_dve, 2 * t)
                    act.wait_ge(rope_pool, 3 * t)
                act.activation(tmp[:, NH, :], bank[6][:, 0:P], ACT.Square).then_inc(sq_ready, 1)
                for i in range(4):
                    act.wait_ge(q_mm, 4 * t + i + 1)
                    act.activation(tmp[:, 4 * i:4 * i + 4, :].rearrange("p a b -> p (a b)"), bank[(7, 4, 5, 3)[i]][:, :], ACT.Square).then_inc(sq_ready, 1)
                act.wait_ge(ssq_ready, t + 1)
                rsqrt(rq, ssq, 1.0 / P, eps6, rq_ready)
                for i in range(4):
                    act.wait_ge(qT_mm, 5 * t + i + 1)
                    if t >= 1:
                        act.wait_ge(s_mm, 2 * t)
                    act.activation(qT[:, :, 4 * i:4 * i + 4, :].rearrange("p s a b -> p a s b"),
                                   bank[4 + i][:, :].rearrange("p (a s b) -> p a s b", a=4, s=2), ACT.Copy).then_inc(qT_ready, 1)
                act.wait_ge(qT_mm, 5 * t + 5)
                act.activation(kT[:, WIN + t * P:WIN + (t + 1) * P], bank[3][:, 0:P], ACT.Copy, scale=wqk).then_inc(qT_ready, 1)

            def act_block(b):
                act.wait_ge(mx_ready, b + 1)
                if b >= 1:
                    act.wait_ge(PT_mm, b)
                for i in range(PR):
                    act.activation(Pb[:, i, :], bank[i // 4][:, (i % 4) * P:(i % 4 + 1) * P], ACT.Exp,
                                   bias=mx[:, i:i + 1], accum_out=den[:, i:i + 1])
                act.activation(es, es, ACT.Exp).then_inc(p_ready, 1)
                act.wait_ge(PT_mm, b + 1)
                if b >= 1:
                    act.wait_ge(av_mm, b)
                for i in range(2):
                    act.activation(PT[:, 4 * i:4 * i + 4, :].rearrange("p a b -> p (a b)"), bank[2 * i][:, :], ACT.Copy).then_inc(PT_ready, 1)
                act.wait_ge(av_mm, b + 1)
                if b % 2 == 0 and b >= 2:
                    act.wait_ge(o1_mm, b // 2)
                for i in range(2):
                    act.activation(aT[:, 8 * i:8 * i + 8, 64 * (b % 2):64 * (b % 2) + 64],
                                   bank[1 + 2 * i][:, :].rearrange("p (a b) -> p a b", b=64), ACT.Copy).then_inc(av_ready, 1)

            for t in range(T):
                act_front(t)
                for b in (2 * t, 2 * t + 1):
                    act_block(b)
                act.wait_ge(o1_mm, t + 1)
                if t >= 1:
                    act.wait_ge(o2_mm, t)
                for i in range(2):
                    act.activation(oT1[:, 4 * i:4 * i + 4, :].rearrange("p a b -> p (a b)"), bank[4 + i][:, :], ACT.Copy).then_inc(o1_ready, 1)
            for t in range(T):
                act.wait_ge(mom_ready, T + t + 1)
                rsqrt(rs1, mv1[:, 1:2], 1.0, eps5, mom_rstd)
            act.wait_ge(mom_rstd, 2 * T)
            act.preload_act_table_set("gelu_apprx_tanh_and_others")
            for t in range(T):
                act.wait_ge(h4T_mm, t + 1)
                act.activation(hT[:, :, WIN + t * P:WIN + (t + 1) * P], bank[t % 2][:, 0:DM].rearrange("p (a b) -> p a b", b=P),
                               ACT.Copy).then_inc(h4T_ready, 1)
            for n in range(2 * NT):
                act.wait_ge(mgu_mm, n + 1)
                if n >= 3:
                    act.wait_ge(it_ready, n - 2)
                act.activation(gl[n % 3], bank[2 * (n % 3)][:, :], ACT.Gelu_apprx_tanh).then_inc(gl_ready, 1)
        @block.vector
        def _(dve):
            chained = [0]

            def link(ins):
                chained[0] += 1
                ins.then_inc(dve_chain, 1)
                dve.wait_ge(dve_chain, chained[0])

            def moments(src, t, dst):
                link(dve.bn_stats(stats[:, t, :], src))
                return dve.bn_aggr(dst[:, t, :], stats[:, t, :])

            def normed(dst, src, t, m, r):
                return dve.tensor_scalar(dst, src, m[:, t, 0:1], r[:, t:t + 1], ALU.subtract, ALU.mult)

            dve.wait_ge(ld_x, 16)
            for t in range(T):
                ins = moments(x[:, t, :], t, mv[0])
            ins.then_inc(var_ready, 1)
            dve.wait_ge(exp_c, 1)
            link(dve.tensor_scalar(silu_t, silu_t, 1.0, None, ALU.add))
            link(dve.reciprocal(silu_t, silu_t))
            link(dve.tensor_tensor(silu_c, silu_t, ccol_s, ALU.mult))
            dve.tensor_copy(scb, over(silu_c, P)).then_inc(silu_ready, 1)
            link(dve.tensor_tensor(wbc, cols_s[:, 4:5], cols_s[:, 5:6], ALU.mult))
            link(dve.tensor_tensor(wqk, cols_s[:, 6:7], cols_s[:, 7:8], ALU.mult))
            link(dve.tensor_scalar(wqk, wqk, 1.0 / float(np.sqrt(128.0)), None, ALU.mult))
            dve.wait_ge(mod_copied, 6)
            for i in range(2):
                for j in (1, 4):
                    dve.tensor_scalar(mod[i][:, j, :], mod[i][:, j, :], 1.0, None, ALU.add)
                    g, a = mod[i][:, j + 1, :], gabs[:, 2 * i + j // 4, :]
                    link(dve.scalar_tensor_tensor(a, g, -1.0, g, ALU.mult, ALU.max))
                    link(dve.tensor_scalar(a, a, 0.25, None, ALU.max))
                    link(dve.tensor_scalar(mod[i][:, j + 1, :], mod[i][:, j + 1, :], 0.0, 2.0, ALU.is_ge, ALU.mult))
                    link(dve.scalar_tensor_tensor(mod[i][:, j + 1, :], mod[i][:, j + 1, :], -1.0, gabs[:, 2 * i + j // 4, :],
                                                  ALU.add, ALU.mult))
            dve.wait_ge(rstd_ready, 1)
            for t in range(T):
                link(normed(h[:, t, :], x[:, t, :], t, mv[0], rstd[0]))
                link(dve.tensor_tensor(h[:, t, :], h[:, t, :], mod[0][:, 1, :], ALU.mult))
                link(dve.tensor_tensor(h[:, t, :], h[:, t, :], mod[0][:, 0, :], ALU.add))
                ins = moments(h[:, t, :], t, mv[1])
            ins.then_inc(var_ready, 1)
            dve.wait_ge(rstd_ready, 2)
            for t in range(T):
                normed(un[:, t, :], h[:, t, :], t, mv[1], rstd[1]).then_inc(un_ready, 1)
            dve.wait_ge(bc_ready, T)
            dtv = [d.rearrange("p (a b) -> p a b", b=H) for d in dt]
            link(dve.tensor_tensor(dtv[0], bc[:, :, 2 * N:], under(rows_s[:, 8:16], T), ALU.add))
            dve.scalar_tensor_tensor(dt[1], dt[0], -1.0, dt[0], ALU.mult, ALU.min).then_inc(dt_abs, 1)
            link(dve.tensor_scalar(dt[0], dt[0], 0.0, None, ALU.max))
            dve.wait_ge(dt_log, 2)
            link(dve.tensor_tensor(dt[3], dt[0], dt[2], ALU.add))
            dve.scalar_tensor_tensor(dA, dtv[3], -1.0, under(nA, T), ALU.mult, ALU.mult).then_inc(dA_ready, 1)
            dve.wait_ge(rbc_ready, 1)
            for t in range(T):
                dve.tensor_scalar(bn[:, t, :], bc[:, t, 0:N], rbc[:, 2 * t:2 * t + 1], None, ALU.mult).then_inc(bcn_ready, 1)
                dve.tensor_scalar(bc[:, t, N:2 * N], bc[:, t, N:2 * N], rbc[:, 2 * t + 1:2 * t + 2], None,
                                  ALU.mult).then_inc(bcn_ready, 1)
            dve.wait_ge(cs_mm, 1)
            cs, tot = bank[6][:, 0:T * H], bank[6][:, T * H:2 * T * H]
            flat = lambda v: v.rearrange("p a b -> p (a b)")
            link(dve.tensor_scalar(flat(ncs), cs, -1.0, None, ALU.mult))
            dve.tensor_tensor(flat(dec), flat(ncs), tot, ALU.add).then_inc(decs_in, 1)
            dve.wait_ge(decs_ready, 3)
            for t in range(T):
                hd = lambda v: v.rearrange("p (a b) -> p a b", b=HD)
                M = Lm[:, t % 2, :].rearrange("p (a b) -> p a b", b=P)
                dve.wait_ge(L_ready, t + 1)
                dve.wait_ge(G_mm, t + 1)
                dve.tensor_tensor(M, M, under(bank[2][:, 0:P], H), ALU.mult).then_inc(M_ready, 1)
                if t < T - 1:
                    dve.wait_ge(st_mm, t + 1)
                    new = state[:, (t + 1) % 2, :]
                    if t == 0:
                        dve.tensor_copy(new, bank[5][:, :]).then_inc(state_ready, 1)
                    else:
                        link(dve.tensor_tensor(hd(new), hd(state[:, t % 2, :]), over(etot[:, t, :], HD), ALU.mult))
                        dve.tensor_tensor(new, new, bank[5][:, :], ALU.add).then_inc(state_ready, 1)
                y = un_y[:, t % 2, :]
                dve.wait_ge(Yd_mm, t + 1)
                dve.wait_ge(xdec_ready, 2 * t + 2)
                link(dve.tensor_tensor(y, xD[:, t % 2, :], bank[3][:, :], ALU.add))
                if t >= 1:
                    dve.wait_ge(Yo_mm, t)
                    link(dve.tensor_tensor(hd(yo_s), hd(bank[4][:, :]), over(ecs[:, t, :], HD), ALU.mult))
                    link(dve.tensor_tensor(y, y, yo_s, ALU.add))
                dve.tensor_tensor(zs[:, t, :], zs[:, t, :], y, ALU.mult).then_inc(y_ready, 1)
            for t in range(T):
                hx = h[:, t, :]
                dve.wait_ge(o_mm, t + 1)
                link(dve.tensor_tensor(hx, hx, bank[t % 2][:, 0:DM], ALU.add))
                link(dve.tensor_tensor(hx, hx, mod[0][:, 2, :], ALU.mult))
                dve.tensor_tensor(x[:, t, :], x[:, t, :], hx, ALU.add).then_inc(x1_ready, 1)

            for t in range(T):
                ins = moments(x[:, t, :], t, mv[2])
            ins.then_inc(var_ready, 1)
            dve.wait_ge(rstd_ready, 3)
            dve.wait_ge(x1_ready, T)
            for t in range(T):
                link(normed(h[:, t, :], x[:, t, :], t, mv[2], rstd[2]))
                link(dve.tensor_tensor(h[:, t, :], h[:, t, :], mod[0][:, 4, :], ALU.mult))
                dve.tensor_tensor(h[:, t, :], h[:, t, :], mod[0][:, 3, :], ALU.add).then_inc(h2_ready, 1)
            dve.wait_ge(logits_mm, T)
            logit = bank[4][:, :].rearrange("p (a b) -> p a b", b=E)
            link(dve.tensor_reduce(rmax, logit, AX, ALU.max))
            dve.tensor_tensor(prob, logit, over(rmax, E), ALU.subtract).then_inc(lmax_ready, 1)
            dve.wait_ge(exp_ready, 1)
            link(dve.tensor_reduce(rsum, prob, AX, ALU.add))
            link(dve.reciprocal(rsum, rsum))
            link(dve.tensor_tensor(prob, prob, over(rsum, E), ALU.mult))
            for t in range(T):
                ins = dve.max(top8[:, t, :], prob[:, t, :])
            link(ins)
            for t in range(T):
                ins = dve.match_replace(rest[:, t, :], top8[:, t, :], prob[:, t, :], -1.0)
            link(ins)
            link(dve.tensor_scalar(mask, rest, 0.0, None, ALU.is_lt))
            dve.tensor_copy(mask_b, mask)
            link(dve.memset(run_b[:, 0, :], 0.0))
            for t in range(1, T):
                ins = dve.tensor_tensor(run_b[:, t, :], run_b[:, t - 1, :], mask_b[:, t - 1, :], ALU.add)
                if t < T - 1:
                    link(ins)
            ins.then_inc(mask_ready, 1)
            link(dve.tensor_tensor(wfull, prob, mask, ALU.mult))
            link(dve.tensor_reduce(rsum, wfull, AX, ALU.add))
            link(dve.reciprocal(rsum, rsum))
            link(dve.tensor_tensor(wfull, wfull, over(rsum, E), ALU.mult))
            dve.wait_ge(pos_mm, 1)
            place = bank[5][:, :].rearrange("p (a b) -> p a b", b=E)
            dve.scalar_tensor_tensor(valid, place, float(CAP), mask, ALU.is_lt, ALU.mult)
            link(dve.tensor_tensor(slotv, under(rows_s[:, 24:88], T), place, ALU.subtract))
            link(dve.tensor_tensor(slotv, slotv, valid, ALU.mult))
            for t in range(T):
                ins = dve.max(slot8[:, t, :], slotv[:, t, :])
            link(ins)
            dve.tensor_scalar(scatter8, slot8, -1.0, NOWHERE, ALU.mult, ALU.add).then_inc(slots_ready, 1)
            link(dve.tensor_scalar(eqk[:, :, 0:TOPK], slot8, -1.0, NOWHERE, ALU.mult, ALU.add))
            dve.tensor_scalar(gather8, eqk[:, :, 0:TOPK], float(SLOTS - 1), None, ALU.min)
            link(dve.tensor_tensor(wvalid, wfull, valid, ALU.mult))
            for k in range(TOPK):
                link(dve.tensor_tensor(eqk, slotv, over(slot8[:, :, k], E), ALU.is_equal))
                link(dve.tensor_tensor(eqk, eqk, wvalid, ALU.mult))
                ins = dve.tensor_reduce(w8[:, :, k], eqk, AX, ALU.add)
                if k < TOPK - 1:
                    link(ins)
            ins.then_inc(w8_ready, 1)
            def decode(n):
                which, c, b = n // 4, n % 4, n % 2
                dve.wait_ge(pk_loaded[b], DEC_LOADS[n])
                codes = pk[b].bitcast(i16).rearrange("p (n two) -> p n two", two=2)[:, :, 0]
                v, f, s = (nib[b][i].bitcast(i16) for i in range(3))
                vf, ff = nib[b][0].bitcast(bf16), nib[b][1].bitcast(bf16)
                for par in range(2):
                    if par == 0:
                        link(dve.tensor_scalar(v, codes, 0x7, 6, ALU.bitwise_and, ALU.logical_shift_left))
                        dve.tensor_scalar(s, codes, 0x8, 12, ALU.bitwise_and, ALU.logical_shift_left)
                    else:
                        link(dve.tensor_scalar(v, codes, 0x70, 2, ALU.bitwise_and, ALU.logical_shift_left))
                        dve.tensor_scalar(s, codes, 0x80, 8, ALU.bitwise_and, ALU.logical_shift_left)
                    link(dve.tensor_scalar(v, v, 0x3E00, None, ALU.bitwise_or))
                    link(dve.tensor_scalar(ff, vf, -0.25, 0.0, ALU.add, ALU.min))
                    link(dve.tensor_tensor(ff, ff, vf, ALU.add))
                    link(dve.tensor_tensor(f, f, s, ALU.bitwise_or))
                    if which < 2:
                        dst = (wg_s, wu_s)[which][:, par, c * QC:(c + 1) * QC]
                        last = dve.scalar_tensor_tensor(dst, ff, 4.0, sc[b], ALU.mult, ALU.mult)
                    else:
                        dst = wdn_s[:, 4 * c + par:4 * c + par + 3:2, :]
                        last = dve.scalar_tensor_tensor(dst, ff.rearrange("p (a b) -> p a b", b=DM), 4.0,
                                                        sc[b].rearrange("p (a b) -> p a b", b=DM), ALU.mult, ALU.mult)
                    if par == 0:
                        link(last)
                last.then_inc(dec_done, 1)

            for g in range(NG + 1):
                if g < NG:
                    dve.wait_ge(sg_ready, g + 1)
                    if g >= 2:
                        dve.wait_ge(down_mm, g - 1)
                    dve.tensor_tensor(hidT[g % 2], sg[g % 2], bank[2 + g % 2][0:FI, 4 * CAP:8 * CAP], ALU.mult).then_inc(hid_ready, 1)
                if g >= 1:
                    i = (g - 1) % 2
                    dve.wait_ge(down_mm, g)
                    if g >= 3:
                        dve.wait_ge(ob_stored[i], 16 * ((g - 1) // 2))
                    dve.tensor_copy(ob[i][:, 2:4, :].rearrange("p a b -> p (a b)"), bank[5 + 2 * i][0:CAP, :]).then_inc(ob_right, 1)
                if 3 <= g < 3 + NQ:
                    decode(g - 3)

            def combine(t):
                dve.wait_ge(gathered[t % 2], 16 * TOPK * (t // 2 + 1))
                g = gath[t % 2]
                link(dve.tensor_scalar(g[:, 0, :], g[:, 0, :], w8[:, t, 0:1], None, ALU.mult))
                for k in range(1, TOPK):
                    link(dve.scalar_tensor_tensor(g[:, 0, :], g[:, k, :], w8[:, t, k:k + 1], g[:, 0, :], ALU.mult, ALU.add))
                link(dve.tensor_tensor(g[:, 1, :], g[:, 0, :], mod[0][:, 5, :], ALU.mult))
                dve.tensor_tensor(x[:, t, :], x[:, t, :], g[:, 1, :], ALU.add).then_inc(x2_ready, 1)
                dve.wait_ge(x2_ready, t + 1)

            def row_norm(t, m):
                link(dve.bn_stats(st1, x[:, t, :]))
                dve.bn_aggr(mv1, st1).then_inc(mom_ready, 1)
                dve.wait_ge(mom_rstd, t + 1 + (T if m else 0))
                link(dve.tensor_scalar(h[:, t, :], x[:, t, :], mv1[:, 0:1], rs1, ALU.subtract, ALU.mult))
                link(dve.tensor_tensor(h[:, t, :], h[:, t, :], mod[1][:, m + 1, :], ALU.mult))
                return dve.tensor_tensor(h[:, t, :], h[:, t, :], mod[1][:, m, :], ALU.add)

            def dve_front(t):
                combine(t)
                row_norm(t, 0).then_inc(ha_ready, 1)
                dve.wait_ge(sq_ready, 5 * (t + 1))
                dve.tensor_reduce(ssq, tmp, AX, ALU.add).then_inc(ssq_ready, 1)
                dve.wait_ge(rq_ready, t + 1)
                if t >= 1:
                    dve.wait_ge(qT_mm, 5 * t)
                dve.tensor_scalar(qk[:, NH, :], bank[6][:, 0:P], rq[:, NH:NH + 1], None, ALU.mult).then_inc(qn_ready, 1)
                for i in range(4):
                    dve.tensor_tensor(qk[:, 4 * i:4 * i + 4, :], bank[(7, 4, 5, 3)[i]][:, :].rearrange("p (a b) -> p a b", b=P),
                                      over(rq[:, 4 * i:4 * i + 4], P), ALU.mult).then_inc(qn_ready, 1)
                dve.wait_ge(qn_ready, 5 * (t + 1))
                cos, sin = under(rope_s[:, t, 0:32], NH + 1), under(rope_s[:, t, 32:64], NH + 1)
                dve.tensor_tensor(tmp[:, :, 0:32], qk[:, :, 0:32], cos, ALU.mult)
                dve.tensor_tensor(tmp[:, :, 32:64], qk[:, :, 32:64], sin, ALU.mult).then_inc(rope_dve, 1)
                dve.wait_ge(rope_dve, 2 * t + 1)
                dve.wait_ge(rope_pool, 3 * t + 2)
                dve.tensor_tensor(qk[:, :, 0:32], tmp[:, :, 0:32], tmp[:, :, 32:64], ALU.subtract).then_inc(rope_dve, 1)

            def dve_block(b):
                dve.wait_ge(s_mm, b + 1)
                if b >= 1:
                    dve.wait_ge(pn_ready, b)
                for i in range(2):
                    ins = dve.tensor_reduce(mx[:, 4 * i:4 * i + 4], bank[i][:, :].rearrange("p (a b) -> p a b", b=P), AX, ALU.max)
                link(ins)
                link(dve.tensor_tensor(mx, mx, sinks_s, ALU.max))
                link(dve.tensor_scalar(mx, mx, -1.0, None, ALU.mult))
                dve.tensor_tensor(es, sinks_s, mx, ALU.add).then_inc(mx_ready, 1)
                dve.wait_ge(p_ready, b + 1)
                link(dve.tensor_tensor(den, den, es, ALU.add))
                link(dve.reciprocal(den, den))
                dve.tensor_tensor(Pb, Pb, over(den, P), ALU.mult).then_inc(pn_ready, 1)

            for t in range(T):
                dve_front(t)
                for b in (2 * t, 2 * t + 1):
                    dve_block(b)
                dve.wait_ge(o2_mm, t + 1)
                link(dve.tensor_tensor(tmp2, bank[6][:, 0:DM], mod[1][:, 2, :], ALU.mult))
                dve.tensor_tensor(x[:, t, :], x[:, t, :], tmp2, ALU.add).then_inc(x3_ready, 1)
                dve.wait_ge(x3_ready, t + 1)
            for t in range(T):
                row_norm(t, 3).then_inc(h4_ready, 1)
            for n in range(2 * NT):
                dve.wait_ge(gl_ready, n + 1)
                if n >= 3:
                    dve.wait_ge(dn_mm, n - 2)
                dve.tensor_tensor(it[n % 3], gl[n % 3], bank[2 * (n % 3) + 1][:, :], ALU.mult).then_inc(it_ready, 1)
                if n % NT == NT - 1:
                    half = n // NT
                    dve.wait_ge(dn_mm, n + 1)
                    for i in range(4):
                        t = 4 * half + i
                        if t >= 1:
                            dve.wait_ge(fin_ready, t)
                        link(dve.tensor_tensor(tmp2, bank[6 + i // 2][:, (i % 2) * DM:(i % 2 + 1) * DM], mod[1][:, 5, :], ALU.mult))
                        dve.tensor_tensor(x[:, t, :], x[:, t, :], tmp2, ALU.add).then_inc(fin_ready, 1)
        @block.tensor
        def _(pe):
            def mm(o, lhsT, rhs, start=True, stop=True, **kw):
                return pe.matmul(o, lhsT, rhs, start=start, stop=stop, **kw)

            pe.wait_ge(silu_ready, 1)
            pe.wait_ge(ld_mod, 16)
            for i in range(2):
                for n in range(3):
                    for j in range(KC):
                        ins = mm(bank[3 * i + n][:, :], scb[:, 2 * i + j, :], wmod_s[i][:, j, n * 512:(n + 1) * 512],
                                 start=j == 0, stop=j == KC - 1)
                    ins.then_inc(mod_mm, 1)
            pe.wait_ge(ld_con, 16)
            for t in range(T):
                pe.wait_ge(un_ready, t + 1)
                if t >= 2:
                    pe.wait_ge(uT_ready, 2 * (t - 1))
                for j in range(KC):
                    ins = pe.transpose(bank[6 + t % 2][:, j * P:(j + 1) * P], un[:, t, j * P:(j + 1) * P], ident)
                ins.then_inc(uT_mm, 1)
            pe.wait_ge(ld_win, 16)
            pe.wait_ge(mod_copied, 6)
            for t in range(T):
                b = 3 * (t % 2)
                pe.wait_ge(uT_ready, 2 * (t + 1))
                for part, (lo, hi, done) in enumerate(((0, DI, proj_z), (DI, 2 * DI, proj_x), (2 * DI, 2 * DI + 2 * N + H, proj_bc))):
                    if t >= 2:
                        pe.wait_ge((z_ready, xs_ready, bc_ready)[part], t - 1)
                    for j in range(KC):
                        ins = mm(bank[b + part][:, 0:hi - lo], uT[:, j, t * P:(t + 1) * P], w_in_s[:, j, lo:hi],
                                 start=j == 0, stop=j == KC - 1)
                    ins.then_inc(done, 1)
            pe.wait_ge(dA_ready, 1)
            pe.wait_ge(pool_consts, 10)
            pe.wait_ge(uT_ready, 2 * T)
            dAf = dA.rearrange("p a b -> p (a b)")
            mm(bank[6][:, 0:T * H], tri, dAf)
            mm(bank[6][:, T * H:2 * T * H], ones, dAf).then_inc(cs_mm, 1)
            for t in range(T):
                pe.wait_ge(bcn_ready, 2 * t + 2)
                if t == 0:
                    pe.wait_ge(decs_ready, 3)
                if t >= 2:
                    pe.wait_ge(bcT_ready, 2 * (t - 1))
                pe.transpose(bank[6 + t % 2][:, 0:P], bn[:, t, :], ident)
                pe.transpose(bank[6 + t % 2][:, P:2 * P], bc[:, t, N:2 * N], ident).then_inc(bcT_mm, 1)
            pe.wait_ge(bcT_ready, 2 * T)
            pe.wait_ge(z_ready, T)
            pe.wait_ge(bc_ready, T)

            def chunk_front(t):
                b = 6 * (t % 2)
                if t >= 2:
                    pe.wait_ge(L_ready, t - 1)
                for i in range(H):
                    mm(bank[b + i // 4][:, (i % 4) * P:(i % 4 + 1) * P], dA[:, t, i:i + 1].to_broadcast([P, P]), tri,
                       start=i % 4 == 0, stop=False, skip_group_check=True)
                for i in range(2):
                    ins = mm(bank[b + i][:, :], ident_b, mask_ssd_b, start=False, stop=True, skip_group_check=True)
                ins.then_inc(csrow_mm, 1)
                if t >= 1:
                    pe.wait_ge(M_ready, t)
                mm(bank[2][:, 0:P], bT[:, t, :], cT[:, t, :]).then_inc(G_mm, 1)

            chunk_front(0)
            for t in range(T):
                if t < T - 1:
                    pe.wait_ge(xdec_ready, 2 * t + 1)
                    if t >= 1:
                        pe.wait_ge(state_ready, t)
                    mm(bank[5][:, :], bn[:, t, :], xdec[:, t % 2, :]).then_inc(st_mm, 1)
                if t >= 1:
                    pe.wait_ge(y_ready, t)
                    pe.wait_ge(state_ready, t)
                    mm(bank[4][:, :], cT[:, t, :], state[:, t % 2, :]).then_inc(Yo_mm, 1)
                pe.wait_ge(M_ready, t + 1)
                for i in range(H):
                    ins = mm(bank[3][:, i * HD:(i + 1) * HD], Lm[:, t % 2, i * P:(i + 1) * P], xs[:, t, i * HD:(i + 1) * HD])
                ins.then_inc(Yd_mm, 1)
                if t < T - 1:
                    chunk_front(t + 1)
            pe.wait_ge(ld_wout, 16)
            pe.wait_ge(L_ready, T)
            for t in range(T):
                pe.wait_ge(y_ready, t + 1)
                if t >= 2:
                    pe.wait_ge(yT_ready, t - 1)
                for j in range(4):
                    ins = pe.transpose(bank[6 + t % 2][:, j * P:(j + 1) * P], zs[:, t, j * P:(j + 1) * P], ident)
                ins.then_inc(yT_mm, 1)
                pe.wait_ge(yT_ready, t + 1)
                if t >= 2:
                    pe.wait_ge(x1_ready, t - 1)
                for j in range(4):
                    ins = mm(bank[t % 2][:, 0:DM], yT[:, t % 2, j * P:(j + 1) * P], w_out_s[:, j, :], start=j == 0, stop=j == 3)
                ins.then_inc(o_mm, 1)
            pe.wait_ge(ld_gate, 16)
            for t in range(T):
                pe.wait_ge(h2_ready, t + 1)
                if t >= 2:
                    pe.wait_ge(h2T_ready, t - 1)
                for j in range(KC):
                    ins = pe.transpose(bank[2 + t % 2][:, j * P:(j + 1) * P], h[:, t, j * P:(j + 1) * P], ident)
                ins.then_inc(h2T_mm, 1)
                pe.wait_ge(h2T_ready, t + 1)
                for j in range(KC):
                    ins = mm(bank[4][:, t * E:(t + 1) * E], h2T[t % 2][:, j, :], gate_s[:, j, :], start=j == 0, stop=j == KC - 1)
                ins.then_inc(logits_mm, 1)
            pe.wait_ge(mask_ready, 1)
            for t in range(T):
                mm(bank[5][:, t * E:(t + 1) * E], strict_b, mask_b[:, t, :], stop=False)
                ins = mm(bank[5][:, t * E:(t + 1) * E], ones_b, run_b[:, t, :], start=False)
            ins.then_inc(pos_mm, 1)

            def rows_T(g):
                pe.wait_ge(xg_loaded[g % 2], 16 * (g // 2 + 1))
                if g >= 2:
                    pe.wait_ge(xgT_ready, g - 1)
                for q in range(2):
                    for j in range(KC):
                        ins = pe.transpose(bank[g % 2][:, (2 * q + j) * P:(2 * q + j + 1) * P], xg[g % 2][:, q, j * P:(j + 1) * P], ident)
                ins.then_inc(xgT_mm, 1)

            def gate_up(g):
                pe.wait_ge(xgT_ready, g + 1)
                if g >= 2:
                    pe.wait_ge(hid_ready, g - 1)
                for e in range(4):
                    q = 2 * g + e // 2
                    if e % 2 == 0:
                        pe.wait_ge(w_loaded[q % NS], 32 * (q // NS + 1))
                    w = wgu_s[q % NS][:, e % 2, :].rearrange("p (a j f) -> p a j f", a=2, j=KC)
                    for a in range(2):
                        for j in range(KC):
                            ins = mm(bank[2 + g % 2][0:FI, (4 * a + e) * CAP:(4 * a + e + 1) * CAP], w[:, a, j, :],
                                     xgT[g % 2][:, 2 * (e // 2) + j, (e % 2) * CAP:(e % 2 + 1) * CAP], start=j == 0, stop=j == KC - 1)
                ins.then_inc(gu_mm, 1)

            def down(g):
                pe.wait_ge(hid_ready, g + 1)
                if g >= 2:
                    pe.wait_ge(ob_left, g - 1)
                    pe.wait_ge(ob_right, g - 1)
                for e in range(4):
                    q = 2 * g + e // 2
                    ins = mm(bank[4 + 2 * (g % 2) + e // 2][0:CAP, (e % 2) * DM:(e % 2 + 1) * DM],
                             hidT[g % 2][:, e * CAP:(e + 1) * CAP], wd_s[q % NS][:, e % 2, :])
                ins.then_inc(down_mm, 1)

            pe.wait_ge(slots_ready, 1)
            rows_T(0)
            for g in range(NG):
                if g + 1 < NG:
                    rows_T(g + 1)
                gate_up(g)
                if g >= 1:
                    down(g - 1)
            down(NG - 1)
            def pe_front(t):
                pe.wait_ge(ha_ready, t + 1)
                if t >= 1:
                    pe.wait_ge(qT_ready, 5 * t)
                    pe.wait_ge(o1_ready, 2 * t)
                    pe.wait_ge(x3_ready, t)
                for j in range(KC):
                    ins = pe.transpose(bank[4][:, j * P:(j + 1) * P], h[:, t, j * P:(j + 1) * P], ident)
                ins.then_inc(haT_mm, 1)
                pe.wait_ge(haT_ready, t + 1)
                now = slice(WIN + t * P, WIN + (t + 1) * P)
                for j in range(KC):
                    ins = mm(bank[5][0:QD, 0:P], wqc_s[:, j, :], hT[:, j, now], start=j == 0, stop=j == KC - 1)
                ins.then_inc(qcT_mm, 1)
                for j in range(KC):
                    mm(bank[6][:, 0:2 * P], hT[:, j, now], wkv_s[:, j, :], start=j == 0, stop=j == KC - 1)
                for j in range(KC):
                    ins = mm(bank[6][:, 2 * P:3 * P], hT[:, j, t * P:(t + 1) * P], wkv_s[:, j, P:2 * P], start=j == 0, stop=j == KC - 1)
                ins.then_inc(kv_mm, 1)
                pe.wait_ge(qcT_ready, t + 1)
                for i in range(4):
                    if i == 3 and t >= 1:
                        pe.wait_ge(av_ready, 4 * t)
                    mm(bank[(7, 4, 5, 3)[i]][:, :], qcT, wqup_s[:, i * 512:(i + 1) * 512]).then_inc(q_mm, 1)
                pe.wait_ge(rope_dve, 2 * t + 2)
                pe.wait_ge(rope_pool, 3 * t + 3)
                for i in range(4):
                    for j in range(4):
                        ins = pe.transpose(bank[4 + i][:, j * P:(j + 1) * P], qk[:, 4 * i + j, :], ident)
                    ins.then_inc(qT_mm, 1)
                pe.transpose(bank[3][:, 0:P], qk[:, NH, :], ident).then_inc(qT_mm, 1)

            def pe_block(b):
                t, hb = b // 2, b % 2
                if b >= 1:
                    pe.wait_ge(PT_ready, 2 * b)
                    pe.wait_ge(av_ready, 2 * b)
                keys = kT[:, 64 * b:64 * b + P]
                for i in range(2):
                    mm(bank[i][:, :], ident_b, mask_first_b if b == 0 else mask_win_b, start=True, stop=False, skip_group_check=True)
                    for j in range(4):
                        p = 4 * i + j
                        ins = mm(bank[i][:, j * P:(j + 1) * P], qT[:, hb, 2 * p:2 * p + 2, :].rearrange("p a b -> p (a b)"), keys,
                                 start=False, stop=True, skip_group_check=True)
                ins.then_inc(s_mm, 1)
                pe.wait_ge(pn_ready, b + 1)
                for i in range(PR):
                    ins = pe.transpose(bank[2 * (i // 4)][:, (i % 4) * P:(i % 4 + 1) * P], Pb[:, i, :], ident)
                ins.then_inc(PT_mm, 1)
                pe.wait_ge(PT_ready, 2 * b + 2)
                for i in range(2):
                    ins = mm(bank[1 + 2 * i][:, :], Vw[b % 4], PT[:, 4 * i:4 * i + 4, :])
                ins.then_inc(av_mm, 1)

            pe.wait_ge(ld_wq, 32)
            pe.wait_ge(ld_wqup, 16)
            pe.wait_ge(pads, 2)
            pe.wait_ge(ob_left, NG)
            pe.wait_ge(ob_right, NG)
            for t in range(T):
                pe_front(t)
                pe.wait_ge(qT_ready, 5 * (t + 1))
                for b in (2 * t, 2 * t + 1):
                    pe_block(b)
                pe.wait_ge(ld_w1, 16)
                pe.wait_ge(av_ready, 4 * (t + 1))
                for go in range(8):
                    g = go // 2
                    for j in range(4):
                        ins = mm(bank[4 + go // 4][:, (go % 4) * P:(go % 4 + 1) * P], w1_s[:, 4 * g + j, (go % 2) * P:(go % 2 + 1) * P],
                                 aT[:, 4 * g + j, :], start=j == 0, stop=j == 3)
                ins.then_inc(o1_mm, 1)
                pe.wait_ge(ld_w2, 16)
                pe.wait_ge(o1_ready, 2 * (t + 1))
                for go in range(8):
                    ins = mm(bank[6][:, 0:DM], oT1[:, go, :], w2_s[:, go, :], start=go == 0, stop=go == 7)
                ins.then_inc(o2_mm, 1)
            for t in range(T):
                pe.wait_ge(h4_ready, t + 1)
                if t >= 2:
                    pe.wait_ge(h4T_ready, t - 1)
                if t == 0:
                    pe.wait_ge(x3_ready, T)
                pair = h[:, t, :].rearrange("p (k two) -> p two k", two=2)
                for j in range(2):
                    ins = pe.transpose(bank[t % 2][:, j * P:(j + 1) * P], pair[:, j, :], ident)
                ins.then_inc(h4T_mm, 1)
            pe.wait_ge(dec_done, NQ)
            pe.wait_ge(h4T_ready, T)

            def mlp_down(n):
                half, i = n // NT, n % NT
                pe.wait_ge(it_ready, n + 1)
                if i == 0 and half == 1:
                    pe.wait_ge(fin_ready, 4)
                for j in range(4):
                    ins = mm(bank[6 + j // 2][:, (j % 2) * DM:(j % 2 + 1) * DM], it[n % 3][:, j * P:(j + 1) * P], wdn_s[:, i, :],
                             start=i == 0 and j % 2 == 0, stop=i == NT - 1, skip_group_check=True)
                ins.then_inc(dn_mm, 1)

            for n in range(2 * NT):
                half, i = n // NT, n % NT
                if n >= 3:
                    pe.wait_ge(it_ready, n - 2)
                toks = slice(WIN + half * 512, WIN + half * 512 + 512)
                for a, w in enumerate((wg_s, wu_s)):
                    for j in range(2):
                        ins = mm(bank[2 * (n % 3) + a][:, :], w[:, j, i * P:(i + 1) * P], hT[:, j, toks], start=j == 0, stop=j == 1)
                ins.then_inc(mgu_mm, 1)
                if n >= 1:
                    mlp_down(n - 1)
            mlp_down(2 * NT - 1)


def _layout(i):
    import numpy as np
    i = {k: np.asarray(v) for k, v in i.items()}
    P = 128
    fm = lambda w: np.ascontiguousarray(w.reshape(-1, P, w.shape[-1]).transpose(1, 0, 2))
    col = lambda v: v.reshape(-1, P).T
    f32 = np.float32
    r = np.arange(P)
    k, m = r[:, None], r[None, :]
    masks = [k == m, k <= m, k < m]
    big = f32(-1e30)
    q = k % 64
    window = (m > q) & (m <= q + 64)
    consts = np.stack([a.astype(f32) for a in masks] + [np.where(k > m, big, f32(0)),
                      np.where(window & (m >= 64), f32(0), big), np.where(window, f32(0), big)], 1)
    inv = f32(1.0) / (f32(10000.0) ** (np.arange(0, 64, 2, dtype=f32) / f32(64)))
    ang = np.arange(1024, dtype=f32)[:, None] * inv[None, :]
    rope = np.concatenate([np.cos(ang), np.sin(ang)], 1).astype(f32).reshape(8, P, 64).transpose(1, 0, 2)
    wg = i["L0_ffn_wg"].reshape(64, 2, P, 96)
    wu = i["L0_ffn_wu"].reshape(64, 2, P, 96)
    wgu = np.stack([wg, wu], 1).transpose(0, 3, 1, 2, 4).reshape(32, 2, P, 384).transpose(0, 2, 1, 3)
    wd = i["L0_ffn_wd"].reshape(32, 2, 96, 256).transpose(0, 2, 1, 3)
    perm = lambda w: w.reshape(8, P, 2, w.shape[-1]).transpose(0, 2, 1, 3).reshape(2048, w.shape[-1]).T
    down = i["L1_ffn_down_W_packed"]
    arrays = {
        "x": i["L0_attn_u"].reshape(1024, 256),
        "w_in": fm(i["L0_attn_in_proj_w"].T), "w_out": fm(i["L0_attn_out_proj_w"].T), "gate_w": fm(i["L0_ffn_gate_w"].T),
        "wgu": wgu.reshape(32, P, 768), "wd": wd.reshape(32, 96, 512),
        "wmod": np.stack([fm(i["L0_wmod"]), fm(i["L1_wmod"])]),
        "ccol": np.concatenate([col(i["L0_c"].reshape(-1)), col(i["L1_c"].reshape(-1))], 1),
        "cols": np.concatenate([col(i["L0_attn_ln_w"]), col(i["L0_attn_ln_b"]), col(i["L0_attn_bnorm_w"]), col(i["L0_attn_cnorm_w"]),
                                col(i["L1_attn_q_norm_w"]), col(i["L1_attn_k_norm_w"])], 1),
        "rows": np.concatenate([i["L0_attn_D"], i["L0_attn_dt_bias"], i["L0_attn_A_log"],
                                8192 - 64 * np.arange(64, dtype=f32)])[None],
        "sinks": i["L1_attn_sink_logit"].reshape(8, 2).T,
        "rope": rope, "consts": consts,
        "wqc": fm(i["L1_attn_wq_comp"]), "wqup": i["L1_attn_wq_up"],
        "wkv": np.concatenate([fm(i["L1_attn_wk"]), fm(i["L1_attn_wv"])], 2),
        "w1": i["L1_attn_out_w1"].reshape(4, 4, P, 256).transpose(2, 0, 1, 3).reshape(P, 16, 256),
        "w2": fm(i["L1_attn_out_w2"]),
        "gpk": perm(i["L1_ffn_gate_W_packed"]), "upk": perm(i["L1_ffn_up_W_packed"]),
        "dpk": down.T.reshape(8, P, 256).transpose(1, 0, 2),
        "gsc": perm(i["L1_ffn_gate_scales"]), "usc": perm(i["L1_ffn_up_scales"]), "dsc": i["L1_ffn_down_scales"].T,
    }
    return {n: np.ascontiguousarray(a) for n, a in arrays.items()}


def kernel(**inputs):
    import concourse.bacc as _bacc
    from concourse import mybir as _mybir
    from concourse.bass_utils import run_bass_kernel_spmd as _run

    nc = _bacc.Bacc("TRN2", target_bir_lowering=False, num_devices=1)
    arrays = {f"in_{n}": a for n, a in _layout(inputs).items()}
    args = [nc.dram_tensor(n, a.shape, _mybir.dt.from_np(a.dtype), kind="ExternalInput").ap() for n, a in arrays.items()]
    args.append(nc.dram_tensor("out_0", (1024, 256), _mybir.dt.float32, kind="ExternalOutput").ap())
    adaln_two_layers(nc, *args)
    r = _run(nc, [arrays], core_ids=[0])
    return r.results[0]["out_0"].reshape(1, 1024, 256)
```

```python
import numpy as np
import concourse.bass as bass
from concourse import mybir
from contextlib import ExitStack

ARENA = 53100


def adaln_two_layers(nc, x_in, w_in, w_out, gate_w, wgu, wd, wmod, ccol, cols, rows, sinks, rope, consts,
                     wqc, wqup, wkv, w1, w2, gpk, upk, dpk, gsc, usc, dsc, out):
    f32, bf16, i16, i32, u32, f16 = (mybir.dt.float32, mybir.dt.bfloat16, mybir.dt.int16, mybir.dt.int32,
                                     mybir.dt.uint32, mybir.dt.float16)
    ALU = mybir.AluOpType
    ACT = mybir.ActivationFunctionType
    AX = mybir.AxisListType.X

    P = 128
    T = x_in.shape[0] // P
    DM = x_in.shape[1]
    KC = DM // P
    DI, H, HD, N = 512, 8, 64, 128
    E, CAP, TOPK, FI = 64, 64, 8, 96
    NOWHERE = 8192.0
    SLOTS = E * CAP

    xin = nc.dram_tensor("expert_in", (SLOTS, DM), f32, kind="Internal").ap()
    yex = nc.dram_tensor("expert_out", (SLOTS, DM), f32, kind="Internal").ap()

    ctx = ExitStack()
    with ctx:
        def sem(name):
            return ctx.enter_context(nc.semaphore(name))

        arena = ctx.enter_context(nc.sbuf_tensor("arena", [P, ARENA], f32))
        bank = [ctx.enter_context(nc.psum_tensor(f"bank{i}", [P, 512], f32)) for i in range(8)]

        def at(offset, *dims, parts=P):
            n = int(np.prod(dims))
            assert offset + n <= ARENA, (offset, dims)
            v = arena[0:parts, offset:offset + n]
            if len(dims) == 2:
                v = v.rearrange("p (a b) -> p a b", b=dims[1])
            elif len(dims) == 3:
                v = v.rearrange("p (a b c) -> p a b c", b=dims[1], c=dims[2])
            return v

        def packed(v, n):
            return v[:, 0:n]

        def over(v, n):
            return v.unsqueeze(2).to_broadcast([v.shape[0], v.shape[1], n])

        def under(v, n):
            return v.unsqueeze(1).to_broadcast([v.shape[0], n, v.shape[1]])

        x = at(0, T, DM)
        h = at(2048, T, DM)
        mod = [at(4096, 6, DM), at(5632, 6, DM)]
        con = at(7168, 6, P)
        ident, tri, tri_strict, mask_ssd, mask_first, mask_win = (con[:, i, :] for i in range(6))
        ident_b = at(7936, 64).bitcast(bf16)
        strict_b = at(8000, 64).bitcast(bf16)
        ones_b = at(8064, 64).bitcast(bf16)
        mask_ssd_b = at(8128, 256).bitcast(bf16)
        mask_first_b = at(8384, 256).bitcast(bf16)
        mask_win_b = at(8640, 256).bitcast(bf16)
        ones = at(8896, P)
        small = 9024
        ccol_s, cols_s, rows_s, sinks_s = at(small, 4), at(small + 4, 8), at(small + 560, 88), at(small + 36, 8)
        eps5, eps6, one_c = at(small + 44, 1), at(small + 45, 1), at(small + 46, 1)
        silu_c, silu_t = at(small + 48, 4), at(small + 52, 4)
        stats = at(small + 64, T, 6)
        mv = [at(small + 112 + 16 * i, T, 2) for i in range(5)]
        rstd = [at(small + 192 + 8 * i, T) for i in range(5)]
        w8 = at(small + 240, T, TOPK)
        slot8 = at(small + 304, T, TOPK)
        gather8 = at(small + 368, T, TOPK).bitcast(u32)
        scatter8 = at(small + 432, T, TOPK).bitcast(u32)
        wbc = at(small + 496, 1)
        wqk = at(small + 497, 1)
        rope_s = at(10048, T, 64)

        A0 = 10560
        uT = at(A0, KC, T * P)
        zs = at(A0 + 2048, T, DI)
        xs = at(A0 + 6144, T, DI)
        bc = at(A0 + 10240, T, 2 * N + H)
        state = at(A0 + 12352, 2, DI)
        w_in_s = at(A0 + 13376, KC, w_in.shape[2])
        w_out_s = at(A0 + 15952, 4, DM)
        cT = at(A0 + 16976, T, P)
        bT = at(A0 + 18000, T, P)
        bn = at(A0 + 19024, T, P)
        gate_s = at(A0 + 20048, KC, E)
        un = at(A0 + 20176, T, DM)
        Lm = at(A0 + 22224, 2, H * P)
        yT = at(A0 + 26320, 2, DI)
        un_y, yo_s = at(A0 + 20176, 2, DI), at(A0 + 21200, DI)
        junk = at(A0 + 28368, 2, P)
        dt = [at(A0 + 28624 + 64 * i, T * H) for i in range(4)]
        wmod_s = at(A0 + 22224, 2, KC, 6 * DM)
        scb = at(A0 + 12352, 4, P)
        A1 = A0 + 28880
        ss = at(A1, T, 2)
        rbc = at(A1 + 16, T * 2)
        dA = at(A1 + 32, T, H)
        ncs, ecs, dec, etot = (at(A1 + 96 + 64 * i, T, H) for i in range(4))
        nA = at(A1 + 352, H)
        zero = at(A1 + 360, 1024)
        gabs = at(A0 + 16976, 4, DM)
        X0 = A1 + 1392
        XB = X0 + 5120
        xD = [at(XB + 512 * t, DI) for t in range(T)]
        xdec = [at(XB + 4096 + 512 * t if t < 5 else A0 + 24272 + 512 * (t - 5), DI) for t in range(T - 1)]

        ld_x, ld_con, ld_mod, ld_mod_rest, ld_small, ld_c, ld_win, ld_wout, ld_gate = map(
            sem, ["ld_x", "ld_con", "ld_mod", "ld_mod_rest", "ld_small", "ld_c", "ld_win", "ld_wout", "ld_gate"])
        zero_set, xin_zeroed = sem("zero_set"), sem("xin_zeroed")
        dve_chain, act_chain, pool_chain = sem("dve_chain"), sem("act_chain"), sem("pool_chain")
        consts_ready, pool_consts = sem("consts_ready"), sem("pool_consts")
        exp_c, silu_ready, mod_mm, mod_copied, = map(sem, ["exp_c", "silu_ready", "mod_mm", "mod_copied"])
        mod_rest_ready = sem("mod_rest_ready")
        var0_ready, rstd0_ready, var1_ready, rstd1_ready, var2_ready, rstd2_ready = map(
            sem, ["var0_ready", "rstd0_ready", "var1_ready", "rstd1_ready", "var2_ready", "rstd2_ready"])
        un_ready, uT_mm, uT_ready = sem("un_ready"), sem("uT_mm"), sem("uT_ready")
        proj_z, proj_x, proj_bc = sem("proj_z"), sem("proj_x"), sem("proj_bc")
        z_ready, xs_ready, bc_ready = map(sem, ["z_ready", "xs_ready", "bc_ready"])
        dt_abs, dt_log, dA_ready, cs_mm, cs_used, decs_in, decs_ready = map(
            sem, ["dt_abs", "dt_log", "dA_ready", "cs_mm", "cs_used", "decs_in", "decs_ready"])
        rbc_ready, bcn_ready, bcT_mm, bcT_ready = map(sem, ["rbc_ready", "bcn_ready", "bcT_mm", "bcT_ready"])
        csrow_mm, G_mm, L_ready, M_ready = map(sem, ["csrow_mm", "G_mm", "L_ready", "M_ready"])
        xD_ready, xh_ready, xdec_ready, Yd_mm, Yo_mm, yo_ready, st_mm, state_ready, y_ready = map(
            sem, ["xD_ready", "xh_ready", "xdec_ready", "Yd_mm", "Yo_mm", "yo_ready", "st_mm", "state_ready", "y_ready"])
        yT_mm, yT_ready, o_mm, x1_ready = map(sem, ["yT_mm", "yT_ready", "o_mm", "x1_ready"])

        NS = 13
        PAIR = 4 * KC * FI + 2 * DM
        slot_at = [X0 + PAIR * i if i < 4 else A0 + PAIR * (i - 4) for i in range(NS)]
        wgu_s = [at(o, 2, 2 * KC * FI) for o in slot_at]
        wd_s = [at(o + 4 * KC * FI, 2, DM, parts=FI) for o in slot_at]
        NX = 4
        xg = [at(XB + 5120 + 512 * i, 2, DM) for i in range(2)] + [at(XB + 512 * i, 2, DM) for i in range(2)]
        xgT = [at(XB + 1024 + 512 * i, 4, P) for i in range(2)]
        sg = [at(XB + 2048 + 256 * i, 4 * CAP, parts=FI) for i in range(2)]
        hidT = [at(XB + 2560 + 256 * i, 4 * CAP, parts=FI) for i in range(2)]
        ob = [at(XB + 3072 + 1024 * i, 4, DM, parts=CAP) for i in range(2)]
        NG = E // 4
        h2T = [at(A0 + 28368 + 256 * i, KC, P) for i in range(2)]
        R0 = A0 + 13376
        prob, slotv, wvalid, eqk = (at(R0 + 512 * i, T, E) for i in range(4))
        rest, mask, wfull, valid = (at(R0 + 2048 + 128 * i, 2, E) for i in range(4))
        mask_b, run_b = (at(A0 + 27904 + 256 * i, 256).bitcast(bf16).rearrange("p (a b) -> p a b", b=E) for i in range(2))
        top8 = at(A0 + 27344, T, TOPK)
        rmax, rsum = at(A0 + 27408, T), at(A0 + 27416, T)

        h2_ready, h2T_mm, h2T_ready, logits_mm, lmax_ready, exp_ready = map(
            sem, ["h2_ready", "h2T_mm", "h2T_ready", "logits_mm", "lmax_ready", "exp_ready"])
        mask_ready, pos_mm, slots_ready, scattered = map(sem, ["mask_ready", "pos_mm", "slots_ready", "scattered"])
        w_loaded = [sem(f"w_loaded{i}") for i in range(NS)]
        xg_loaded = [sem(f"xg_loaded{i}") for i in range(NX)]
        xgT_mm, xgT_ready, gu_mm, sg_ready, hid_ready, down_mm, ob_ready = map(
            sem, ["xgT_mm", "xgT_ready", "gu_mm", "sg_ready", "hid_ready", "down_mm", "ob_ready"])
        ob_stored = [sem(f"ob_stored{i}") for i in range(2)]
        w8_ready, x2_ready = sem("w8_ready"), sem("x2_ready")
        gathered = [sem(f"gathered{i}") for i in range(2)]
        gath = [at(A0 + 2048 * i, TOPK, DM) for i in range(2)]
        tmp2 = at(A0 + 11008, DM)
        B0 = A0 + 11520
        MLP = 2048
        NT = MLP // P
        wg_s, wu_s = at(B0, 2, MLP), at(B0 + 4096, 2, MLP)
        wdn_s = at(B0 + 8192, NT, DM)
        QC = 512
        D0 = A0 + 23808
        pk = [at(D0 + 512 * i, QC) for i in range(2)]
        sc = [at(D0 + 1024 + 512 * i, QC) for i in range(2)]
        nib = [[at(D0 + 2048 + 256 * (3 * b + i), QC // 2) for i in range(3)] for b in range(2)]
        NQ = 3 * MLP // QC
        NEARLY, PACE = 3, 1.3
        DEC_LOADS = [sum((48 if m >= 8 else 32) for m in range(n % 2, n + 1, 2)) for n in range(NQ)]
        NH, QD, WIN = 16, 64, 64
        PR = NH // 2
        w1_s, w2_s = at(A0 + 4096, NH, DM), at(A0 + 8192, 8, DM)
        wqc_s, wkv_s = at(A0 + 10240, KC, QD), at(A0 + 10368, KC, 2 * P)
        qk = at(D0, NH + 1, P)
        kT = at(D0 + 2176, WIN + T * P)
        Vw = [at(D0 + 3264 + 128 * i, P) for i in range(4)]
        PT = at(D0 + 3776, PR, P)
        oT1 = at(A1, 8, P)
        wqup_s = at(X0, NH * P, parts=QD)
        hT = at(X0 + 2048, KC, WIN + T * P)
        tmp = at(X0 + 4224, NH + 1, P)
        qT = at(X0 + 6400, 2, NH, WIN)
        Pb = [at(X0 + 8448, PR, P), at(2048 + 4 * DM, PR, P)]
        aT = at(X0 + 9472, NH, P)
        qcT = at(A1 + 1024, P, parts=QD)
        sm = small + 660
        ssq, rq = at(sm, NH + 1), at(sm + 20, NH + 1)
        st1, mv1, rs1 = at(sm + 40, 6), at(sm + 48, 2), at(sm + 50, 1)
        st4, mv4, rs4 = at(sm + 104, 6), at(sm + 112, 2), at(sm + 114, 1)
        mx, es, den = ([at(sm + 56 + 8 * i + 24 * b, PR) for b in range(2)] for i in range(3))

        pk_loaded = [sem(f"pk_loaded{i}") for i in range(2)]
        dec_done = sem("dec_done")
        ld_w1, ld_w2, ld_wq, ld_wqup = map(sem, ["ld_w1", "ld_w2", "ld_wq", "ld_wqup"])
        pads = sem("pads")
        mom_ready, mom_rstd, ha_ready, haT_mm, haT_ready, qcT_mm, qcT_ready, kv_mm, k_copied, v_ready = map(
            sem, ["mom_ready", "mom_rstd", "ha_ready", "haT_mm", "haT_ready", "qcT_mm", "qcT_ready", "kv_mm", "k_copied", "v_ready"])
        q_mm, q_copied, sq_ready, ssq_ready, rq_ready, qn_ready, rope_dve, rope_pool = map(
            sem, ["q_mm", "q_copied", "sq_ready", "ssq_ready", "rq_ready", "qn_ready", "rope_dve", "rope_pool"])
        qT_mm, qT_ready, s_mm, mx_ready, p_ready, pn_ready, PT_mm, PT_ready, av_mm, av_ready = map(
            sem, ["qT_mm", "qT_ready", "s_mm", "mx_ready", "p_ready", "pn_ready", "PT_mm", "PT_ready", "av_mm", "av_ready"])
        o1_mm, o1_ready, o2_mm, x3_ready, mom4_ready, mom4_rstd = map(
            sem, ["o1_mm", "o1_ready", "o2_mm", "x3_ready", "mom4_ready", "mom4_rstd"])
        gl = [at(D0 + 512 * i, 512) for i in range(3)]
        it = [at(D0 + 1536 + 512 * i, 512) for i in range(3)]
        h4_ready, h4T_mm, h4T_ready, mgu_mm, gl_ready, it_ready, dn_mm, fin_ready, out_stored, mdn_mm = map(
            sem, ["h4_ready", "h4T_mm", "h4T_ready", "mgu_mm", "gl_ready", "it_ready", "dn_mm", "fin_ready", "out_stored", "mdn_mm"])
        block = ctx.enter_context(nc.Block())

        @block.sync
        def _(sp):
            thirds = wmod.rearrange("l p j n -> p l j n")
            sp.dma_start(ccol_s, ccol).then_inc(ld_c, 16)
            sp.dma_start(x, x_in.rearrange("(t p) c -> p t c", p=P)).then_inc(ld_x, 16)
            sp.dma_start(wmod_s[:, 0, :, 0:2 * DM], thirds[:, 0, :, 0:2 * DM]).then_inc(ld_mod, 16)
            sp.dma_start(cols_s, cols).then_inc(ld_small, 16)
            sp.dma_start(con, consts).then_inc(ld_con, 16)
            sp.dma_start(w_in_s, w_in).then_inc(ld_win, 16)
            sp.dma_start(rows_s, rows.to_broadcast([P, rows.shape[1]])).then_inc(ld_small, 16)
            sp.dma_start(wmod_s[:, 0, :, 2 * DM:], thirds[:, 0, :, 2 * DM:]).then_inc(ld_mod_rest, 16)
            sp.dma_start(wmod_s[:, 1], thirds[:, 1]).then_inc(ld_mod_rest, 16)
            for i in range(2):
                sp.dma_start(sinks_s[64 * i:64 * i + 64, :], sinks[i:i + 1, :].to_broadcast([64, 8])).then_inc(ld_small, 16)
            sp.dma_start(w_out_s, w_out).then_inc(ld_wout, 16)
            sp.dma_start(gate_s, gate_w).then_inc(ld_gate, 16)
            sp.dma_start(rope_s, rope).then_inc(ld_small, 16)
            sp.wait_ge(zero_set, 1)
            sp.dma_start(xin.rearrange("(p r a) c -> p r (a c)", p=P, r=8), under(zero, 8)).then_inc(xin_zeroed, 16)
            def load_pair(q, sp=sp):
                i = q % NS
                if q >= NS:
                    sp.wait_ge(down_mm, (q - NS) // 2 + 1)
                sp.dma_start(wgu_s[i].rearrange("p a b -> p (a b)"), wgu[q]).then_inc(w_loaded[i], 16)
                sp.dma_start(wd_s[i].rearrange("p a b -> p (a b)"), wd[q]).then_inc(w_loaded[i], 16)

            def load_codes(n):
                which, c, i = n // 4, n % 4, n % 2
                if n >= 2:
                    sp.wait_ge(dec_done, n - 1)
                if which < 2:
                    src, scales = ((gpk, gsc), (upk, usc))[which]
                    sp.dma_start(pk[i].bitcast(i32), src[:, c * QC:(c + 1) * QC]).then_inc(pk_loaded[i], 16)
                    sp.dma_start(sc[i], scales[:, c * QC:(c + 1) * QC].unsqueeze(1).to_broadcast([8, 16, QC])).then_inc(pk_loaded[i], 16)
                else:
                    sp.dma_start(pk[i].bitcast(i32).rearrange("p (a b) -> p a b", b=DM), dpk[:, 2 * c:2 * c + 2, :]).then_inc(pk_loaded[i], 16)
                    for a in range(2):
                        sp.dma_start(sc[i][:, a * DM:(a + 1) * DM],
                                     dsc[8 * (2 * c + a):8 * (2 * c + a) + 8, :].unsqueeze(1).to_broadcast([8, 16, DM])).then_inc(pk_loaded[i], 16)

            for q in range(4):
                load_pair(q)
            sp.wait_ge(yT_mm, T)
            load_codes(0)
            load_codes(1)
            for q in range(4, NS):
                load_pair(q)
            for n in range(2, NEARLY):
                load_codes(n)

            def load_rows(g):
                if g >= NX:
                    sp.wait_ge(xgT_mm, g - NX + 1)
                sp.dma_start(xg[g % NX], xin[4 * CAP * g:4 * CAP * (g + 1), :].rearrange("(q p) c -> p q c", p=P))                    .then_inc(xg_loaded[g % NX], 16)

            sp.wait_ge(scattered, 16 * T * TOPK)
            for g in range(NX):
                load_rows(g)
            n = NEARLY
            for g in range(NG):
                while n < NQ and 2 * (n - 2) < 2 * NEARLY + g * PACE:
                    load_codes(n)
                    n += 1
                if g + NX < NG:
                    load_rows(g + NX)
                for q in (2 * g + NS - 1, 2 * g + NS):
                    if NS <= q < E // 2:
                        load_pair(q)
            sp.wait_ge(down_mm, NG)
            sp.dma_start(wqup_s, wqup).then_inc(ld_wqup, 16)
            sp.dma_start(wqc_s, wqc).then_inc(ld_wq, 16)
            sp.dma_start(wkv_s, wkv).then_inc(ld_wq, 16)
            sp.dma_start(w1_s, w1).then_inc(ld_w1, 16)
            sp.dma_start(w2_s, w2).then_inc(ld_w2, 16)
            for t in range(T):
                sp.wait_ge(fin_ready, t + 1)
                sp.dma_start(out[t * P:(t + 1) * P, :], x[:, t, :]).then_inc(out_stored, 16)
            sp.wait_ge(out_stored, 16 * T)

        @block.gpsimd
        def _(pool):
            pool.memset(zero, 0.0).then_inc(zero_set, 1)
            for v, value in ((ones, 1.0), (eps5, 1e-5), (eps6, 1e-6), (one_c, 1.0)):
                pool.memset(v, value).then_inc(pool_consts, 1)
            pool.memset(ones_b, 1.0).then_inc(pool_consts, 1)
            pool.wait_ge(ld_con, 16)
            pool.tensor_copy(ident_b, ident).then_inc(pool_consts, 1)
            pool.tensor_copy(strict_b, tri_strict).then_inc(pool_consts, 1)
            for b, m in ((mask_ssd_b, mask_ssd), (mask_first_b, mask_first), (mask_win_b, mask_win)):
                pool.tensor_copy(b.rearrange("p (r c) -> p r c", c=P), under(m, 4)).then_inc(pool_consts, 1)
            def by_head(v):
                return v.rearrange("p (a b) -> p a b", b=HD)

            pool.wait_ge(ld_small, 80)
            for t in range(T):
                pool.wait_ge(xs_ready, t + 1)
                pool.tensor_tensor(by_head(xD[t]), by_head(xs[:, t, :]), over(rows_s[:, 0:H], HD), ALU.mult).then_inc(xD_ready, 1)
            pool.wait_ge(decs_ready, 3)
            for t in range(T - 1):
                pool.tensor_tensor(by_head(xdec[t]), by_head(xs[:, t, :]), over(dec[:, t, :], HD), ALU.mult).then_inc(xdec_ready, 1)
            pool.wait_ge(mod_rest_ready, 1)
            pool.wait_ge(un_ready, T)
            for t in range(T):
                pool.tensor_tensor(h[:, t, :], h[:, t, :], mod[0][:, 2, :], ALU.mult).then_inc(pool_chain, 1)
                pool.wait_ge(pool_chain, t + 1)
                pool.tensor_tensor(x[:, t, :], x[:, t, :], h[:, t, :], ALU.add).then_inc(xh_ready, 1)

            pool.wait_ge(xin_zeroed, 16)
            for t in range(T):
                pool.wait_ge(slots_ready, t // 2 + 1)
                for k in range(TOPK):
                    pool.indirect_dma_start(xin, bass.IndirectOffsetOnAxis(scatter8[:, t, k:k + 1], 0), h[:, t, :], None,
                                            bounds_check=SLOTS - 1, oob_is_err=False).then_inc(scattered, 16)
            for g in range(NG):
                pool.wait_ge(ob_ready, 2 * (g + 1))
                pool.dma_start(yex[4 * CAP * g:4 * CAP * (g + 1), :].rearrange("(e s) c -> s e c", s=CAP), ob[g % 2])                    .then_inc(ob_stored[g % 2], 16)
            for i in range(2):
                pool.wait_ge(ob_stored[i], 16 * NG // 2)
            pool.wait_ge(down_mm, NG)
            def gather(t):
                if t >= 2:
                    pool.wait_ge(x2_ready, t - 1)
                for k in range(TOPK):
                    pool.indirect_dma_start(gath[t % 2][:, k, :], None, yex, bass.IndirectOffsetOnAxis(gather8[:, t, k:k + 1], 0),
                                            bounds_check=SLOTS - 1, oob_is_err=False).then_inc(gathered[t % 2], 16)

            pool.memset(kT[:, 0:WIN], 0.0).then_inc(pads, 1)
            pool.memset(hT[:, :, 0:WIN], 0.0).then_inc(pads, 1)
            for t in range(4):
                gather(t)
            for t in range(T):
                pool.wait_ge(qn_ready, t + 1)
                cos, sin = under(rope_s[:, t, 0:32], NH + 1), under(rope_s[:, t, 32:64], NH + 1)
                pool.tensor_tensor(tmp[:, :, 64:96], qk[:, :, 0:32], sin, ALU.mult).then_inc(rope_pool, 1)
                pool.tensor_tensor(tmp[:, :, 96:128], qk[:, :, 32:64], cos, ALU.mult).then_inc(rope_pool, 1)
                pool.wait_ge(rope_pool, 3 * t + 2)
                pool.wait_ge(rope_dve, 2 * t + 1)
                pool.tensor_tensor(qk[:, :, 32:64], tmp[:, :, 64:96], tmp[:, :, 96:128], ALU.add).then_inc(rope_pool, 1)
                if t + 3 < T and t >= 1:
                    gather(t + 3)
        @block.scalar
        def _(act):
            chained = [0]

            def link(ins):
                chained[0] += 1
                ins.then_inc(act_chain, 1)
                act.wait_ge(act_chain, chained[0])

            def rsqrt(o, i, scale, eps, done):
                link(act.activation(o, i, ACT.Ln, bias=eps, scale=scale))
                act.activation(o, o, ACT.Exp, scale=-0.5).then_inc(done, 1)

            act.preload_act_table_set("natural_log_exp_and_others")
            act.wait_ge(ld_c, 16)
            act.activation(silu_t, ccol_s, ACT.Exp, scale=-1.0).then_inc(exp_c, 1)
            act.wait_ge(pool_consts, 10)
            act.wait_ge(var0_ready, 1)
            rsqrt(rstd[0], mv[0][:, :, 1], 1.0, eps5, rstd0_ready)

            def copy_mod(n):
                act.wait_ge(mod_mm, n + 1)
                act.activation(at(4096 + 512 * n, 512), bank[4 + n % 2][:, :], ACT.Copy).then_inc(mod_copied, 1)

            copy_mod(0)
            act.wait_ge(ld_small, 80)
            for s in range(T + 2):
                if s < T:
                    act.wait_ge(var1_ready, s + 1)
                    rsqrt(rstd[1][:, s:s + 1], mv[1][:, s, 1:2], 1.0, eps5, rstd1_ready)
                if 1 <= s <= T:
                    t = s - 1
                    act.wait_ge(uT_mm, t + 1)
                    for j in range(KC):
                        act.activation(uT[:, j, t * P:(t + 1) * P], bank[6 + t % 2][:, j * P:(j + 1) * P], ACT.Identity,
                                       scale=cols_s[:, j:j + 1], bias=cols_s[:, 2 + j:3 + j]).then_inc(uT_ready, 1)
                if s >= 2:
                    t = s - 2
                    act.wait_ge(proj_bc, t + 1)
                    if t >= 1:
                        act.wait_ge(bc_ready, t)
                    act.activation(bc[:, t, :], bank[t % 2][:, 0:2 * N + H], ACT.Copy)
                    for j in range(2):
                        ins = act.activation(junk[:, j, :], bank[t % 2][:, j * N:(j + 1) * N], ACT.Square,
                                             accum_out=ss[:, t, j:j + 1])
                    ins.then_inc(bc_ready, 1)
                    act.wait_ge(proj_x, t + 1)
                    act.activation(xs[:, t, :], bank[2 + t % 2][:, :], ACT.Copy).then_inc(xs_ready, 1)
                if 4 <= s < 9:
                    copy_mod(s - 3)
            act.wait_ge(bc_ready, T)
            act.activation(nA, rows_s[:, 16:24], ACT.Exp).then_inc(dt_log, 1)
            act.wait_ge(dt_abs, 1)
            link(act.activation(dt[2], dt[1], ACT.Exp))
            act.activation(dt[2], dt[2], ACT.Ln, bias=1.0).then_inc(dt_log, 1)
            rsqrt(rbc, ss.rearrange("p a b -> p (a b)"), 1.0 / N, eps5, rbc_ready)
            act.wait_ge(decs_in, 1)
            act.activation(ecs.rearrange("p a b -> p (a b)"), bank[4][:, 0:T * H], ACT.Exp).then_inc(decs_ready, 1)
            act.activation(etot.rearrange("p a b -> p (a b)"), bank[4][:, T * H:2 * T * H], ACT.Exp).then_inc(decs_ready, 1)
            act.activation(dec, dec, ACT.Exp).then_inc(decs_ready, 1)

            def decay_matrices(t):
                act.wait_ge(csrow_mm, t + 1)
                if t >= 2:
                    act.wait_ge(Yd_mm, t - 1)
                for i in range(H):
                    ins = act.activation(Lm[:, t % 2, i * P:(i + 1) * P], bank[i // 4][:, (i % 4) * P:(i % 4 + 1) * P],
                                         ACT.Exp, bias=ncs[:, t, i:i + 1])
                ins.then_inc(L_ready, 1)

            decay_matrices(0)
            act.wait_ge(L_ready, 1)
            act.preload_act_table_set("silu_and_others")
            for t in range(T):
                act.wait_ge(proj_z, t + 1)
                act.activation(zs[:, t, :], bank[(6, 7, 5, 3)[t % 4]][:, :], ACT.Silu).then_inc(z_ready, 1)
            act.wait_ge(z_ready, T)
            act.preload_act_table_set("natural_log_exp_and_others")
            act.wait_ge(decs_ready, 3)
            for s in range(T + 3):
                if s + 1 < T:
                    decay_matrices(s + 1)
                if 1 <= s < T:
                    act.wait_ge(Yo_mm, s)
                    if s >= 2:
                        act.wait_ge(y_ready, s)
                    for i in range(H):
                        ins = act.activation(yo_s[:, i * HD:(i + 1) * HD], bank[4][:, i * HD:(i + 1) * HD], ACT.Copy, scale=ecs[:, s, i:i + 1])
                    ins.then_inc(yo_ready, 1)
                if 0 <= s - 3:
                    act.wait_ge(lmax_ready, s - 2)
                    act.activation(prob[:, s - 3, :], prob[:, s - 3, :], ACT.Exp).then_inc(exp_ready, 1)
                if 0 <= s - 1 < T:
                    t = s - 1
                    act.wait_ge(yT_mm, t + 1)
                    if t >= 1:
                        act.wait_ge(o_mm, t)
                    act.activation(yT[:, t % 2, :], bank[6][:, :], ACT.Copy).then_inc(yT_ready, 1)
                if 0 <= s - 2 < T:
                    t = s - 2
                    act.wait_ge(h2T_mm, t + 1)
                    if t >= 2:
                        act.wait_ge(logits_mm, t - 1)
                    act.activation(h2T[t % 2].rearrange("p a b -> p (a b)"), bank[6][:, 0:DM], ACT.Copy).then_inc(h2T_ready, 1)
                if 0 <= s - 1 < T:
                    act.wait_ge(var2_ready, s)
                    rsqrt(rstd[2][:, s - 1:s], mv[2][:, s - 1, 1:2], 1.0, eps5, rstd2_ready)

            act.wait_ge(exp_ready, T)
            act.preload_act_table_set("silu_and_others")
            def copy_rows(g):
                act.wait_ge(xgT_mm, g + 1)
                if g >= 2:
                    act.wait_ge(gu_mm, g - 1)
                act.activation(xgT[g % 2].rearrange("p a b -> p (a b)"), bank[g % 2][:, :], ACT.Copy).then_inc(xgT_ready, 1)

            copy_rows(0)
            for g in range(NG + 1):
                if g + 1 < NG:
                    copy_rows(g + 1)
                if g < NG:
                    act.wait_ge(gu_mm, g + 1)
                    if g >= 2:
                        act.wait_ge(hid_ready, g - 1)
                    act.activation(sg[g % 2], bank[2 + g % 2][0:FI, 0:4 * CAP], ACT.Silu).then_inc(sg_ready, 1)
                if g >= 1:
                    i = (g - 1) % 2
                    act.wait_ge(down_mm, g)
                    if g >= 3:
                        act.wait_ge(ob_stored[i], 16 * ((g - 1) // 2))
                    for a in range(2):
                        act.activation(ob[i][:, 2 * a:2 * a + 2, :].rearrange("p a b -> p (a b)"), bank[4 + 2 * i + a][0:CAP, :],
                                       ACT.Copy).then_inc(ob_ready, 1)
            act.wait_ge(down_mm, NG)
            act.preload_act_table_set("natural_log_exp_and_others")

            def exp_block(b):
                act.wait_ge(mx_ready, b + 1)
                if b >= 2:
                    act.wait_ge(PT_mm, b - 1)
                for i in range(PR):
                    act.activation(Pb[b % 2][:, i, :], bank[2 * (b % 2) + i // 4][:, (i % 4) * P:(i % 4 + 1) * P], ACT.Exp,
                                   bias=mx[b % 2][:, i:i + 1], accum_out=den[b % 2][:, i:i + 1])
                act.activation(es[b % 2], es[b % 2], ACT.Exp).then_inc(p_ready, 1)

            def copy_probs_T(b):
                act.wait_ge(PT_mm, b + 1)
                if b >= 1:
                    act.wait_ge(av_mm, b)
                for i in range(2):
                    src = bank[(6, 7, 2, 3)[2 * (b % 2) + i]]
                    act.activation(PT[:, 4 * i:4 * i + 4, :].rearrange("p a b -> p (a b)"), src[:, :], ACT.Copy).then_inc(PT_ready, 1)

            def copy_attended(b):
                act.wait_ge(av_mm, b + 1)
                if b % 2 == 0 and b >= 2:
                    act.wait_ge(o1_mm, b // 2)
                for i in range(2):
                    src = bank[(4, 5, 2, 3)[2 * (b % 2) + i]]
                    act.activation(aT[:, 8 * i:8 * i + 8, 64 * (b % 2):64 * (b % 2) + 64],
                                   src[:, :].rearrange("p (a b) -> p a b", b=64), ACT.Copy).then_inc(av_ready, 1)

            for s in range(-1, T + 1):
                nxt, last, done = s + 1, s - 1, s - 2
                if nxt < T:
                    if s == -1:
                        act.wait_ge(mom_ready, 1)
                        rsqrt(rs1, mv1[:, 1:2], 1.0, eps5, mom_rstd)
                    act.wait_ge(haT_mm, nxt + 1)
                    act.activation(hT[:, :, WIN + nxt * P:WIN + (nxt + 1) * P], bank[6][:, 0:DM].rearrange("p (a b) -> p a b", b=P),
                                   ACT.Copy).then_inc(haT_ready, 1)
                if 0 <= s < T:
                    exp_block(2 * s)
                if nxt < T:
                    act.wait_ge(qcT_mm, nxt + 1)
                    act.activation(qcT, bank[7][0:QD, 0:P], ACT.Copy).then_inc(qcT_ready, 1)
                    for i in range(4):
                        act.wait_ge(q_mm, 4 * nxt + i + 1)
                        if nxt >= 1 and i == 0:
                            act.wait_ge(qT_mm, 5 * nxt)
                        act.activation(qk[:, 4 * i:4 * i + 4, :].rearrange("p a b -> p (a b)"), bank[6 + i % 2][:, :],
                                       ACT.Copy).then_inc(q_copied, 1)
                        if i == 1 and done >= 0:
                            act.wait_ge(mom4_ready, done + 1)
                            rsqrt(rs4, mv4[:, 1:2], 1.0, eps5, mom4_rstd)
                    act.wait_ge(kv_mm, nxt + 1)
                    act.activation(qk[:, NH, :], bank[5][:, 0:P], ACT.Copy).then_inc(k_copied, 1)
                    if nxt >= 2:
                        act.wait_ge(av_mm, 2 * s)
                    act.activation(Vw[(2 * nxt + 1) % 4], bank[5][:, P:2 * P], ACT.Copy)
                    act.activation(Vw[(2 * nxt) % 4], bank[5][:, 2 * P:3 * P], ACT.Copy).then_inc(v_ready, 1)
                    act.wait_ge(k_copied, nxt + 1)
                    if nxt >= 1:
                        act.wait_ge(rope_dve, 2 * nxt)
                        act.wait_ge(rope_pool, 3 * nxt)
                    act.activation(tmp, qk, ACT.Square).then_inc(sq_ready, 1)
                elif done >= 0:
                    act.wait_ge(mom4_ready, done + 1)
                    rsqrt(rs4, mv4[:, 1:2], 1.0, eps5, mom4_rstd)
                if 0 <= s < T:
                    exp_block(2 * s + 1)
                if nxt < T:
                    act.wait_ge(ssq_ready, nxt + 1)
                    rsqrt(rq, ssq, 1.0 / P, eps6, rq_ready)
                if done >= 0:
                    act.wait_ge(h4T_mm, done + 1)
                    act.activation(hT[:, :, WIN + done * P:WIN + (done + 1) * P], bank[4][:, 0:DM].rearrange("p (a b) -> p a b", b=P),
                                   ACT.Copy).then_inc(h4T_ready, 1)
                if last >= 0:
                    act.wait_ge(o1_mm, last + 1)
                    if last >= 1:
                        act.wait_ge(o2_mm, last)
                    for i in range(2):
                        act.activation(oT1[:, 4 * i:4 * i + 4, :].rearrange("p a b -> p (a b)"), bank[i][:, :], ACT.Copy).then_inc(o1_ready, 1)
                if s + 2 < T:
                    act.wait_ge(mom_ready, s + 3)
                    rsqrt(rs1, mv1[:, 1:2], 1.0, eps5, mom_rstd)
                if 0 <= s < T:
                    copy_probs_T(2 * s)
                    copy_attended(2 * s)
                    copy_probs_T(2 * s + 1)
                if nxt < T:
                    for i in range(4):
                        act.wait_ge(qT_mm, 5 * nxt + i + 1)
                        if nxt >= 1:
                            act.wait_ge(s_mm, 2 * nxt)
                        act.activation(qT[:, :, 4 * i:4 * i + 4, :].rearrange("p s a b -> p a s b"),
                                       bank[(0, 1, 6, 7)[i]][:, :].rearrange("p (a s b) -> p a s b", a=4, s=2), ACT.Copy).then_inc(qT_ready, 1)
                    act.wait_ge(qT_mm, 5 * nxt + 5)
                    act.activation(kT[:, WIN + nxt * P:WIN + (nxt + 1) * P], bank[4][:, 0:P], ACT.Copy, scale=wqk).then_inc(qT_ready, 1)
                if 0 <= s < T:
                    copy_attended(2 * s + 1)
            act.wait_ge(mom4_ready, T)
            rsqrt(rs4, mv4[:, 1:2], 1.0, eps5, mom4_rstd)
            act.wait_ge(mom4_rstd, T)
            act.preload_act_table_set("gelu_apprx_tanh_and_others")
            for n in range(2 * NT):
                act.wait_ge(mgu_mm, n + 1)
                if n >= 3:
                    act.wait_ge(it_ready, n - 2)
                act.activation(gl[n % 3], bank[2 * (n % 3)][:, :], ACT.Gelu_apprx_tanh).then_inc(gl_ready, 1)
                if n == 1:
                    act.wait_ge(h4T_mm, T)
                    act.activation(hT[:, :, WIN + (T - 1) * P:WIN + T * P], bank[4][:, 0:DM].rearrange("p (a b) -> p a b", b=P),
                                   ACT.Copy).then_inc(h4T_ready, 1)
        @block.vector
        def _(dve):
            chained = [0]

            def link(ins):
                chained[0] += 1
                ins.then_inc(dve_chain, 1)
                dve.wait_ge(dve_chain, chained[0])

            def moments(src, t, dst):
                link(dve.bn_stats(stats[:, t, :], src))
                return dve.bn_aggr(dst[:, t, :], stats[:, t, :])

            def normed(dst, src, t, m, r):
                return dve.tensor_scalar(dst, src, m[:, t, 0:1], r[:, t:t + 1], ALU.subtract, ALU.mult)

            dve.wait_ge(exp_c, 1)
            link(dve.tensor_scalar(silu_t, silu_t, 1.0, None, ALU.add))
            link(dve.reciprocal(silu_t, silu_t))
            link(dve.tensor_tensor(silu_c, silu_t, ccol_s, ALU.mult))
            dve.tensor_copy(scb, over(silu_c, P)).then_inc(silu_ready, 1)
            dve.wait_ge(ld_x, 16)
            for t in range(T):
                ins = moments(x[:, t, :], t, mv[0])
            ins.then_inc(var0_ready, 1)
            dve.wait_ge(mod_copied, 1)
            link(dve.tensor_scalar(mod[0][:, 1, :], mod[0][:, 1, :], 1.0, None, ALU.add))
            dve.wait_ge(rstd0_ready, 1)
            for t in range(T + 1):
                if t < T:
                    link(normed(h[:, t, :], x[:, t, :], t, mv[0], rstd[0]))
                    link(dve.tensor_tensor(h[:, t, :], h[:, t, :], mod[0][:, 1, :], ALU.mult))
                    link(dve.tensor_tensor(h[:, t, :], h[:, t, :], mod[0][:, 0, :], ALU.add))
                    moments(h[:, t, :], t, mv[1]).then_inc(var1_ready, 1)
                if t >= 1:
                    dve.wait_ge(rstd1_ready, t)
                    normed(un[:, t - 1, :], h[:, t - 1, :], t - 1, mv[1], rstd[1]).then_inc(un_ready, 1)
            dve.wait_ge(ld_small, 80)
            link(dve.tensor_tensor(wbc, cols_s[:, 4:5], cols_s[:, 5:6], ALU.mult))
            link(dve.tensor_tensor(wqk, cols_s[:, 6:7], cols_s[:, 7:8], ALU.mult))
            link(dve.tensor_scalar(wqk, wqk, 1.0 / float(np.sqrt(128.0)), None, ALU.mult))
            dve.wait_ge(mod_copied, 6)
            for i in range(2):
                for j in (1, 4):
                    if i or j == 4:
                        dve.tensor_scalar(mod[i][:, j, :], mod[i][:, j, :], 1.0, None, ALU.add)
                    g, a = mod[i][:, j + 1, :], gabs[:, 2 * i + j // 4, :]
                    link(dve.scalar_tensor_tensor(a, g, -1.0, g, ALU.mult, ALU.max))
                    link(dve.tensor_scalar(a, a, 0.25, None, ALU.max))
                    link(dve.tensor_scalar(g, g, 0.0, 2.0, ALU.is_ge, ALU.mult))
                    ins = dve.scalar_tensor_tensor(g, g, -1.0, a, ALU.add, ALU.mult)
                    if i == 0 or j == 1:
                        link(ins)
            ins.then_inc(mod_rest_ready, 1)
            dve.wait_ge(bc_ready, T)
            dtv = [d.rearrange("p (a b) -> p a b", b=H) for d in dt]
            link(dve.tensor_tensor(dtv[0], bc[:, :, 2 * N:], under(rows_s[:, 8:16], T), ALU.add))
            dve.scalar_tensor_tensor(dt[1], dt[0], -1.0, dt[0], ALU.mult, ALU.min).then_inc(dt_abs, 1)
            link(dve.tensor_scalar(dt[0], dt[0], 0.0, None, ALU.max))
            dve.wait_ge(dt_log, 2)
            link(dve.tensor_tensor(dt[3], dt[0], dt[2], ALU.add))
            dve.scalar_tensor_tensor(dA, dtv[3], -1.0, under(nA, T), ALU.mult, ALU.mult).then_inc(dA_ready, 1)
            dve.wait_ge(rbc_ready, 1)

            def bc_norms(t):
                dve.tensor_scalar(bn[:, t, :], bc[:, t, 0:N], rbc[:, 2 * t:2 * t + 1], None, ALU.mult).then_inc(bcn_ready, 1)
                dve.tensor_scalar(bc[:, t, N:2 * N], bc[:, t, N:2 * N], rbc[:, 2 * t + 1:2 * t + 2], None,
                                  ALU.mult).then_inc(bcn_ready, 1)

            bc_norms(0)
            bc_norms(1)
            dve.wait_ge(cs_mm, 1)
            cs, tot = bank[4][:, 0:T * H], bank[4][:, T * H:2 * T * H]
            flat = lambda v: v.rearrange("p a b -> p (a b)")
            link(dve.tensor_scalar(flat(ncs), cs, -1.0, None, ALU.mult))
            dve.tensor_tensor(flat(dec), flat(ncs), tot, ALU.add).then_inc(decs_in, 1)
            for t in range(2, T):
                bc_norms(t)
            for q in range(T // 2):
                dve.wait_ge(bcT_mm, q + 1)
                both = bank[2][:, :].rearrange("p (t a b) -> p a t b", a=2, b=P)
                dve.tensor_copy(bT[:, 2 * q:2 * q + 2, :], both[:, 0])
                dve.tensor_scalar(cT[:, 2 * q:2 * q + 2, :], both[:, 1], wbc, None, ALU.mult).then_inc(bcT_ready, 1)

            hd = lambda v: v.rearrange("p (a b) -> p a b", b=HD)

            def make_M(t):
                M = Lm[:, t % 2, :].rearrange("p (a b) -> p a b", b=P)
                dve.wait_ge(L_ready, t + 1)
                dve.wait_ge(G_mm, t + 1)
                dve.tensor_tensor(M, M, under(bank[2][:, 0:P], H), ALU.mult).then_inc(M_ready, 1)

            def choose(q):
                pair = slice(2 * q, 2 * q + 2)
                dve.wait_ge(exp_ready, 2 * q + 2)
                link(dve.tensor_reduce(rsum[:, pair], prob[:, pair, :], AX, ALU.add))
                link(dve.reciprocal(rsum[:, pair], rsum[:, pair]))
                link(dve.tensor_tensor(prob[:, pair, :], prob[:, pair, :], over(rsum[:, pair], E), ALU.mult))
                for t in (2 * q, 2 * q + 1):
                    ins = dve.max(top8[:, t, :], prob[:, t, :])
                link(ins)
                for t in (2 * q, 2 * q + 1):
                    ins = dve.match_replace(rest[:, t % 2, :], top8[:, t, :], prob[:, t, :], -1.0)
                link(ins)
                link(dve.tensor_scalar(mask, rest, 0.0, None, ALU.is_lt))
                link(dve.tensor_copy(mask_b[:, pair, :], mask))
                for t in (2 * q, 2 * q + 1):
                    if t == 0:
                        link(dve.memset(run_b[:, 0, :], 0.0))
                    else:
                        ins = dve.tensor_tensor(run_b[:, t, :], run_b[:, t - 1, :], mask_b[:, t - 1, :], ALU.add)
                        if t % 2 == 0:
                            link(ins)
                ins.then_inc(mask_ready, 1)
                link(dve.tensor_tensor(wfull, prob[:, pair, :], mask, ALU.mult))
                link(dve.tensor_reduce(rsum[:, pair], wfull, AX, ALU.add))
                link(dve.reciprocal(rsum[:, pair], rsum[:, pair]))
                link(dve.tensor_tensor(wfull, wfull, over(rsum[:, pair], E), ALU.mult))

            def place_rows(q):
                pair = slice(2 * q, 2 * q + 2)
                dve.wait_ge(pos_mm, q + 1)
                place = bank[2][:, 2 * P:3 * P].rearrange("p (a b) -> p a b", b=E)
                sv = slotv[:, pair, :]
                dve.scalar_tensor_tensor(valid, place, float(CAP), mask, ALU.is_lt, ALU.mult)
                link(dve.tensor_tensor(sv, under(rows_s[:, 24:88], 2), place, ALU.subtract))
                link(dve.tensor_tensor(sv, sv, valid, ALU.mult))
                dve.tensor_tensor(wvalid[:, pair, :], wfull, valid, ALU.mult)
                for t in (2 * q, 2 * q + 1):
                    ins = dve.max(slot8[:, t, :], slotv[:, t, :])
                link(ins)
                dve.tensor_scalar(scatter8[:, pair, :], slot8[:, pair, :], -1.0, NOWHERE, ALU.mult, ALU.add).then_inc(slots_ready, 1)

            make_M(0)
            dve.wait_ge(decs_ready, 3)
            for s in range(T + 4):
                if s < T - 1:
                    dve.wait_ge(st_mm, s + 1)
                    new = state[:, (s + 1) % 2, :]
                    if s == 0:
                        dve.tensor_copy(new, bank[5][:, :]).then_inc(state_ready, 1)
                    else:
                        link(dve.tensor_tensor(hd(new), hd(state[:, s % 2, :]), over(etot[:, s, :], HD), ALU.mult))
                        dve.tensor_tensor(new, new, bank[5][:, :], ALU.add).then_inc(state_ready, 1)
                if s >= 5 and s % 2 == 1:
                    place_rows((s - 5) // 2)
                if 0 <= s - 3 < T:
                    t = s - 3
                    logit = bank[2][:, P:P + E]
                    dve.wait_ge(logits_mm, t + 1)
                    link(dve.tensor_reduce(rmax[:, t:t + 1], logit, AX, ALU.max))
                    dve.tensor_scalar(prob[:, t, :], logit, rmax[:, t:t + 1], None, ALU.subtract).then_inc(lmax_ready, 1)
                if s < T:
                    y = un_y[:, s % 2, :]
                    dve.wait_ge(Yd_mm, s + 1)
                    dve.wait_ge(xD_ready, s + 1)
                    link(dve.tensor_tensor(y, xD[s], bank[3][:, :], ALU.add))
                    if s >= 1:
                        dve.wait_ge(yo_ready, s)
                        link(dve.tensor_tensor(y, y, yo_s, ALU.add))
                    dve.tensor_tensor(zs[:, s, :], zs[:, s, :], y, ALU.mult).then_inc(y_ready, 1)
                if 0 <= s - 1 < T:
                    t = s - 1
                    dve.wait_ge(o_mm, t + 1)
                    dve.wait_ge(xh_ready, t + 1)
                    link(dve.tensor_tensor(h[:, t, :], bank[7][:, 0:DM], mod[0][:, 2, :], ALU.mult))
                    dve.tensor_tensor(x[:, t, :], x[:, t, :], h[:, t, :], ALU.add).then_inc(x1_ready, 1)
                    dve.wait_ge(x1_ready, t + 1)
                    moments(x[:, t, :], t, mv[2]).then_inc(var2_ready, 1)
                if s + 1 < T:
                    make_M(s + 1)
                if s >= 4 and s % 2 == 0:
                    choose((s - 4) // 2)
                if 0 <= s - 1 < T:
                    t = s - 1
                    dve.wait_ge(rstd2_ready, t + 1)
                    link(normed(h[:, t, :], x[:, t, :], t, mv[2], rstd[2]))
                    link(dve.tensor_tensor(h[:, t, :], h[:, t, :], mod[0][:, 4, :], ALU.mult))
                    dve.tensor_tensor(h[:, t, :], h[:, t, :], mod[0][:, 3, :], ALU.add).then_inc(h2_ready, 1)

            link(dve.tensor_scalar(eqk[:, :, 0:TOPK], slot8, -1.0, NOWHERE, ALU.mult, ALU.add))
            link(dve.tensor_scalar(gather8, eqk[:, :, 0:TOPK], float(SLOTS - 1), None, ALU.min))
            for k in range(TOPK):
                link(dve.tensor_tensor(eqk, slotv, over(slot8[:, :, k], E), ALU.is_equal))
                link(dve.tensor_tensor(eqk, eqk, wvalid, ALU.mult))
                ins = dve.tensor_reduce(w8[:, :, k], eqk, AX, ALU.add)
                if k < TOPK - 1:
                    link(ins)
            ins.then_inc(w8_ready, 1)
            def decode(n, par):
                which, c, b = n // 4, n % 4, n % 2
                dve.wait_ge(pk_loaded[b], DEC_LOADS[n])
                codes = pk[b].bitcast(i16).rearrange("p (n two) -> p n two", two=2)[:, :, 0]
                v, f, s = (nib[b][i].bitcast(i16) for i in range(3))
                vf, ff = nib[b][0].bitcast(bf16), nib[b][1].bitcast(bf16)
                if par == 0:
                    link(dve.tensor_scalar(v, codes, 0x7, 6, ALU.bitwise_and, ALU.logical_shift_left))
                    dve.tensor_scalar(s, codes, 0x8, 12, ALU.bitwise_and, ALU.logical_shift_left)
                else:
                    link(dve.tensor_scalar(v, codes, 0x70, 2, ALU.bitwise_and, ALU.logical_shift_left))
                    dve.tensor_scalar(s, codes, 0x80, 8, ALU.bitwise_and, ALU.logical_shift_left)
                link(dve.tensor_scalar(v, v, 0x3E00, None, ALU.bitwise_or))
                link(dve.tensor_scalar(ff, vf, -0.25, 0.0, ALU.add, ALU.min))
                link(dve.tensor_tensor(ff, ff, vf, ALU.add))
                link(dve.tensor_tensor(f, f, s, ALU.bitwise_or))
                if which < 2:
                    dst = (wg_s, wu_s)[which][:, par, c * QC:(c + 1) * QC]
                    last = dve.scalar_tensor_tensor(dst, ff, 4.0, sc[b], ALU.mult, ALU.mult)
                else:
                    dst = wdn_s[:, 4 * c + par:4 * c + par + 3:2, :]
                    last = dve.scalar_tensor_tensor(dst, ff.rearrange("p (a b) -> p a b", b=DM), 4.0,
                                                    sc[b].rearrange("p (a b) -> p a b", b=DM), ALU.mult, ALU.mult)
                if par == 0:
                    link(last)
                else:
                    last.then_inc(dec_done, 1)

            for n in range(NEARLY):
                decode(n, 0)
                decode(n, 1)
            late = 2 * NEARLY
            for g in range(NG):
                dve.wait_ge(sg_ready, g + 1)
                if g >= 2:
                    dve.wait_ge(down_mm, g - 1)
                dve.tensor_tensor(hidT[g % 2], sg[g % 2], bank[2 + g % 2][0:FI, 4 * CAP:8 * CAP], ALU.mult).then_inc(hid_ready, 1)
                while late < 2 * NQ and late < 2 * NEARLY + (g + 1) * PACE:
                    decode(late // 2, late % 2)
                    late += 1

            def combine(t):
                dve.wait_ge(gathered[t % 2], 16 * TOPK * (t // 2 + 1))
                g = gath[t % 2]
                link(dve.tensor_scalar(g[:, 0, :], g[:, 0, :], w8[:, t, 0:1], None, ALU.mult))
                for k in range(1, TOPK):
                    link(dve.scalar_tensor_tensor(g[:, 0, :], g[:, k, :], w8[:, t, k:k + 1], g[:, 0, :], ALU.mult, ALU.add))
                link(dve.tensor_tensor(g[:, 1, :], g[:, 0, :], mod[0][:, 5, :], ALU.mult))
                dve.tensor_tensor(x[:, t, :], x[:, t, :], g[:, 1, :], ALU.add).then_inc(x2_ready, 1)
                dve.wait_ge(x2_ready, t + 1)

            def shift_scale(dst, t, m, mean_var, rs):
                link(dve.tensor_scalar(dst, x[:, t, :], mean_var[:, 0:1], rs, ALU.subtract, ALU.mult))
                link(dve.tensor_tensor(dst, dst, mod[1][:, m + 1, :], ALU.mult))
                return dve.tensor_tensor(dst, dst, mod[1][:, m, :], ALU.add)

            def combine_moments(t):
                combine(t)
                link(dve.bn_stats(st1, x[:, t, :]))
                dve.bn_aggr(mv1, st1).then_inc(mom_ready, 1)

            def norm_a(t):
                dve.wait_ge(mom_rstd, t + 1)
                if t >= 2:
                    dve.wait_ge(haT_mm, t - 1)
                shift_scale(h[:, t % 2, :], t, 0, mv1, rs1).then_inc(ha_ready, 1)

            def residual(t):
                dve.wait_ge(o2_mm, t + 1)
                link(dve.tensor_tensor(tmp2, bank[5][:, 0:DM], mod[1][:, 2, :], ALU.mult))
                link(dve.tensor_tensor(x[:, t, :], x[:, t, :], tmp2, ALU.add))
                link(dve.bn_stats(st4, x[:, t, :]))
                dve.bn_aggr(mv4, st4).then_inc(mom4_ready, 1)

            def norm_4(t):
                dve.wait_ge(mom4_rstd, t + 1)
                if t >= 2:
                    dve.wait_ge(h4T_mm, t - 1)
                shift_scale(h[:, 2 + t % 2, :], t, 3, mv4, rs4).then_inc(h4_ready, 1)

            def maxima(b):
                m, e = mx[b % 2], es[b % 2]
                dve.wait_ge(s_mm, b + 1)
                for i in range(2):
                    ins = dve.tensor_reduce(m[:, 4 * i:4 * i + 4], bank[2 * (b % 2) + i][:, :].rearrange("p (a b) -> p a b", b=P), AX, ALU.max)
                link(ins)
                link(dve.tensor_tensor(m, m, sinks_s, ALU.max))
                link(dve.tensor_scalar(m, m, -1.0, None, ALU.mult))
                dve.tensor_tensor(e, sinks_s, m, ALU.add).then_inc(mx_ready, 1)

            def over_sums(b):
                d = den[b % 2]
                dve.wait_ge(p_ready, b + 1)
                link(dve.tensor_tensor(d, d, es[b % 2], ALU.add))
                link(dve.reciprocal(d, d))
                dve.tensor_tensor(Pb[b % 2], Pb[b % 2], over(d, P), ALU.mult).then_inc(pn_ready, 1)

            for s in range(-1, T + 1):
                nxt, done = s + 1, s - 2
                if s == -1:
                    combine_moments(0)
                    norm_a(0)
                if 0 <= s < T:
                    maxima(2 * s)
                if done >= 0:
                    residual(done)
                if 0 <= s < T:
                    maxima(2 * s + 1)
                    over_sums(2 * s)
                if done >= 0:
                    norm_4(done)
                if s + 2 < T:
                    combine_moments(s + 2)
                if nxt < T:
                    dve.wait_ge(sq_ready, nxt + 1)
                    dve.tensor_reduce(ssq, tmp, AX, ALU.add).then_inc(ssq_ready, 1)
                if 0 <= s < T:
                    over_sums(2 * s + 1)
                if nxt < T:
                    dve.wait_ge(rq_ready, nxt + 1)
                    dve.tensor_tensor(qk, qk, over(rq, P), ALU.mult).then_inc(qn_ready, 1)
                    dve.wait_ge(qn_ready, nxt + 1)
                    cos, sin = under(rope_s[:, nxt, 0:32], NH + 1), under(rope_s[:, nxt, 32:64], NH + 1)
                    dve.tensor_tensor(tmp[:, :, 0:32], qk[:, :, 0:32], cos, ALU.mult)
                    dve.tensor_tensor(tmp[:, :, 32:64], qk[:, :, 32:64], sin, ALU.mult).then_inc(rope_dve, 1)
                    dve.wait_ge(rope_dve, 2 * nxt + 1)
                    dve.wait_ge(rope_pool, 3 * nxt + 2)
                    dve.tensor_tensor(qk[:, :, 0:32], tmp[:, :, 0:32], tmp[:, :, 32:64], ALU.subtract).then_inc(rope_dve, 1)
                if s + 2 < T:
                    norm_a(s + 2)
            residual(T - 1)
            norm_4(T - 1)
            for n in range(2 * NT):
                dve.wait_ge(gl_ready, n + 1)
                if n >= 3:
                    dve.wait_ge(dn_mm, n - 2)
                dve.tensor_tensor(it[n % 3], gl[n % 3], bank[2 * (n % 3) + 1][:, :], ALU.mult).then_inc(it_ready, 1)
                if n % NT == NT - 1:
                    half = n // NT
                    dve.wait_ge(dn_mm, n + 1)
                    for i in range(4):
                        t = 4 * half + i
                        if t >= 1:
                            dve.wait_ge(fin_ready, t)
                        link(dve.tensor_tensor(tmp2, bank[6 + i // 2][:, (i % 2) * DM:(i % 2 + 1) * DM], mod[1][:, 5, :], ALU.mult))
                        dve.tensor_tensor(x[:, t, :], x[:, t, :], tmp2, ALU.add).then_inc(fin_ready, 1)
        @block.tensor
        def _(pe):
            def mm(o, lhsT, rhs, start=True, stop=True, **kw):
                return pe.matmul(o, lhsT, rhs, start=start, stop=stop, **kw)

            def modulation(n):
                if n >= 2:
                    pe.wait_ge(mod_copied, n - 1)
                for j in range(KC):
                    ins = mm(bank[4 + n % 2][:, :], scb[:, 2 * (n // 3) + j, :], wmod_s[:, n // 3, j, (n % 3) * 512:(n % 3 + 1) * 512],
                             start=j == 0, stop=j == KC - 1)
                ins.then_inc(mod_mm, 1)

            def project(t, o, lo, hi, done):
                for j in range(KC):
                    ins = mm(o[:, 0:hi - lo], uT[:, j, t * P:(t + 1) * P], w_in_s[:, j, lo:hi], start=j == 0, stop=j == KC - 1)
                ins.then_inc(done, 1)

            pe.wait_ge(silu_ready, 1)
            pe.wait_ge(ld_mod, 16)
            modulation(0)
            pe.wait_ge(ld_con, 16)
            for s in range(T + 1):
                if s < T:
                    pe.wait_ge(un_ready, s + 1)
                    if s >= 2:
                        pe.wait_ge(uT_ready, 2 * (s - 1))
                    for j in range(KC):
                        ins = pe.transpose(bank[6 + s % 2][:, j * P:(j + 1) * P], un[:, s, j * P:(j + 1) * P], ident)
                    ins.then_inc(uT_mm, 1)
                if s >= 1:
                    t = s - 1
                    if t == 0:
                        pe.wait_ge(ld_win, 16)
                    pe.wait_ge(uT_ready, 2 * (t + 1))
                    if t >= 2:
                        pe.wait_ge(bc_ready, t - 1)
                        pe.wait_ge(xs_ready, t - 1)
                    project(t, bank[t % 2], 2 * DI, 2 * DI + 2 * N + H, proj_bc)
                    project(t, bank[2 + t % 2], DI, 2 * DI, proj_x)
                if 3 <= s < 8:
                    if s == 3:
                        pe.wait_ge(ld_mod_rest, 32)
                    modulation(s - 2)
            pe.wait_ge(uT_ready, 2 * T)
            pe.wait_ge(mod_copied, 6)
            for t in range(4):
                if t == 3:
                    pe.wait_ge(xs_ready, T)
                project(t, bank[(6, 7, 5, 3)[t]], 0, DI, proj_z)
            pe.wait_ge(dA_ready, 1)
            pe.wait_ge(pool_consts, 10)
            dAf = dA.rearrange("p a b -> p (a b)")
            mm(bank[4][:, 0:T * H], tri, dAf)
            mm(bank[4][:, T * H:2 * T * H], ones, dAf).then_inc(cs_mm, 1)

            def cs_rows(t):
                if t >= 1:
                    pe.wait_ge(L_ready, t)
                for i in range(H):
                    mm(bank[i // 4][:, (i % 4) * P:(i % 4 + 1) * P], dA[:, t, i:i + 1].to_broadcast([P, P]), tri,
                       start=i % 4 == 0, stop=False, skip_group_check=True)
                for i in range(2):
                    ins = mm(bank[i][:, :], ident_b, mask_ssd_b, start=False, stop=True, skip_group_check=True)
                ins.then_inc(csrow_mm, 1)

            cs_rows(0)
            for q in range(T // 2):
                pe.wait_ge(bcn_ready, 4 * q + 4)
                if q >= 1:
                    pe.wait_ge(bcT_ready, q)
                for i in range(2):
                    pe.transpose(bank[2][:, 2 * i * P:(2 * i + 1) * P], bn[:, 2 * q + i, :], ident)
                    ins = pe.transpose(bank[2][:, (2 * i + 1) * P:(2 * i + 2) * P], bc[:, 2 * q + i, N:2 * N], ident)
                ins.then_inc(bcT_mm, 1)
                t = 4 + q
                pe.wait_ge(z_ready, t - 3)
                project(t, bank[(6, 7, 5, 3)[q]], 0, DI, proj_z)
            pe.wait_ge(bcT_ready, T // 2)
            mm(bank[2][:, 0:P], bT[:, 0, :], cT[:, 0, :]).then_inc(G_mm, 1)
            pe.wait_ge(decs_ready, 3)
            for s in range(T + 3):
                if s + 1 < T:
                    cs_rows(s + 1)
                if s < T:
                    if s == 0:
                        pe.wait_ge(z_ready, T)
                    if s < T - 1:
                        pe.wait_ge(xdec_ready, s + 1)
                        if s >= 1:
                            pe.wait_ge(state_ready, s)
                        mm(bank[5][:, :], bn[:, s, :], xdec[s]).then_inc(st_mm, 1)
                    if s >= 1:
                        pe.wait_ge(state_ready, s)
                        if s >= 2:
                            pe.wait_ge(yo_ready, s - 1)
                        mm(bank[4][:, :], cT[:, s, :], state[:, s % 2, :]).then_inc(Yo_mm, 1)
                    pe.wait_ge(M_ready, s + 1)
                    if s >= 1:
                        pe.wait_ge(y_ready, s)
                    for i in range(H):
                        ins = mm(bank[3][:, i * HD:(i + 1) * HD], Lm[:, s % 2, i * P:(i + 1) * P], xs[:, s, i * HD:(i + 1) * HD])
                    ins.then_inc(Yd_mm, 1)
                if 0 <= s - 1 < T:
                    t = s - 1
                    pe.wait_ge(y_ready, t + 1)
                    if t >= 2:
                        pe.wait_ge(h2T_ready, t - 1)
                    for j in range(4):
                        ins = pe.transpose(bank[6][:, j * P:(j + 1) * P], zs[:, t, j * P:(j + 1) * P], ident)
                    ins.then_inc(yT_mm, 1)
                if s + 1 < T:
                    if s >= 3:
                        pe.wait_ge(lmax_ready, s - 2)
                    if s >= 5:
                        pe.wait_ge(slots_ready, (s - 3) // 2)
                    mm(bank[2][:, 0:P], bT[:, s + 1, :], cT[:, s + 1, :]).then_inc(G_mm, 1)
                if 0 <= s - 1 < T:
                    t = s - 1
                    if t == 0:
                        pe.wait_ge(ld_wout, 16)
                    pe.wait_ge(yT_ready, t + 1)
                    if t >= 1:
                        pe.wait_ge(x1_ready, t)
                    for j in range(4):
                        ins = mm(bank[7][:, 0:DM], yT[:, t % 2, j * P:(j + 1) * P], w_out_s[:, j, :], start=j == 0, stop=j == 3)
                    ins.then_inc(o_mm, 1)
                if 0 <= s - 2 < T:
                    t = s - 2
                    pe.wait_ge(h2_ready, t + 1)
                    for j in range(KC):
                        ins = pe.transpose(bank[6][:, j * P:(j + 1) * P], h[:, t, j * P:(j + 1) * P], ident)
                    ins.then_inc(h2T_mm, 1)
                    if t == 0:
                        pe.wait_ge(ld_gate, 16)
                    pe.wait_ge(h2T_ready, t + 1)
                    pe.wait_ge(M_ready, min(s + 2, T))
                    if s + 1 >= T:
                        pe.wait_ge(lmax_ready, s - 2)
                        pe.wait_ge(slots_ready, (s - 3) // 2)
                    for j in range(KC):
                        ins = mm(bank[2][:, P:P + E], h2T[t % 2][:, j, :], gate_s[:, j, :], start=j == 0, stop=j == KC - 1)
                    ins.then_inc(logits_mm, 1)
                if s >= 4 and s % 2 == 0:
                    q = (s - 4) // 2
                    pe.wait_ge(mask_ready, q + 1)
                    if s - 2 == T:
                        pe.wait_ge(lmax_ready, T)
                    for i in range(2):
                        o = bank[2][:, 2 * P + i * E:2 * P + (i + 1) * E]
                        mm(o, strict_b, mask_b[:, 2 * q + i, :], stop=False)
                        ins = mm(o, ones_b, run_b[:, 2 * q + i, :], start=False)
                    ins.then_inc(pos_mm, 1)
            def rows_T(g):
                pe.wait_ge(xg_loaded[g % NX], 16 * (g // NX + 1))
                if g >= 2:
                    pe.wait_ge(xgT_ready, g - 1)
                for q in range(2):
                    for j in range(KC):
                        ins = pe.transpose(bank[g % 2][:, (2 * q + j) * P:(2 * q + j + 1) * P], xg[g % NX][:, q, j * P:(j + 1) * P], ident)
                ins.then_inc(xgT_mm, 1)

            def gate_up(g):
                pe.wait_ge(xgT_ready, g + 1)
                if g >= 2:
                    pe.wait_ge(hid_ready, g - 1)
                for e in range(4):
                    q = 2 * g + e // 2
                    if e % 2 == 0:
                        pe.wait_ge(w_loaded[q % NS], 32 * (q // NS + 1))
                    w = wgu_s[q % NS][:, e % 2, :].rearrange("p (a j f) -> p a j f", a=2, j=KC)
                    for a in range(2):
                        for j in range(KC):
                            ins = mm(bank[2 + g % 2][0:FI, (4 * a + e) * CAP:(4 * a + e + 1) * CAP], w[:, a, j, :],
                                     xgT[g % 2][:, 2 * (e // 2) + j, (e % 2) * CAP:(e % 2 + 1) * CAP], start=j == 0, stop=j == KC - 1)
                ins.then_inc(gu_mm, 1)

            def down(g):
                pe.wait_ge(hid_ready, g + 1)
                if g >= 2:
                    pe.wait_ge(ob_ready, 2 * (g - 1))
                for e in range(4):
                    q = 2 * g + e // 2
                    ins = mm(bank[4 + 2 * (g % 2) + e // 2][0:CAP, (e % 2) * DM:(e % 2 + 1) * DM],
                             hidT[g % 2][:, e * CAP:(e + 1) * CAP], wd_s[q % NS][:, e % 2, :])
                ins.then_inc(down_mm, 1)

            pe.wait_ge(slots_ready, T // 2)
            rows_T(0)
            for g in range(NG):
                if g + 1 < NG:
                    rows_T(g + 1)
                gate_up(g)
                if g >= 1:
                    down(g - 1)
            down(NG - 1)
            def scores(b):
                keys = kT[:, 64 * b:64 * b + P]
                for i in range(2):
                    o = bank[2 * (b % 2) + i]
                    mm(o[:, :], ident_b, mask_first_b if b == 0 else mask_win_b, start=True, stop=False, skip_group_check=True)
                    for j in range(4):
                        p = 4 * i + j
                        ins = mm(o[:, j * P:(j + 1) * P], qT[:, b % 2, 2 * p:2 * p + 2, :].rearrange("p a b -> p (a b)"), keys,
                                 start=False, stop=True, skip_group_check=True)
                ins.then_inc(s_mm, 1)

            def probs_T(b):
                pe.wait_ge(pn_ready, b + 1)
                for i in range(PR):
                    o = bank[(6, 7, 2, 3)[2 * (b % 2) + i // 4]]
                    ins = pe.transpose(o[:, (i % 4) * P:(i % 4 + 1) * P], Pb[b % 2][:, i, :], ident)
                ins.then_inc(PT_mm, 1)

            def attend(b):
                pe.wait_ge(PT_ready, 2 * b + 2)
                for i in range(2):
                    ins = mm(bank[(4, 5, 2, 3)[2 * (b % 2) + i]][:, :], Vw[b % 4], PT[:, 4 * i:4 * i + 4, :])
                ins.then_inc(av_mm, 1)

            def mlp_rows_T(t):
                pe.wait_ge(h4_ready, t + 1)
                pair = h[:, 2 + t % 2, :].rearrange("p (k two) -> p two k", two=2)
                for j in range(2):
                    ins = pe.transpose(bank[4][:, j * P:(j + 1) * P], pair[:, j, :], ident)
                ins.then_inc(h4T_mm, 1)

            pe.wait_ge(ld_wq, 32)
            pe.wait_ge(ld_wqup, 16)
            pe.wait_ge(pads, 2)
            pe.wait_ge(ob_ready, 2 * NG)
            for s in range(-1, T + 1):
                nxt, last, done = s + 1, s - 1, s - 2
                if nxt < T:
                    pe.wait_ge(ha_ready, nxt + 1)
                    if nxt >= 1:
                        pe.wait_ge(qT_ready, 5 * nxt)
                    for j in range(KC):
                        ins = pe.transpose(bank[6][:, j * P:(j + 1) * P], h[:, nxt % 2, j * P:(j + 1) * P], ident)
                    ins.then_inc(haT_mm, 1)
                if 0 <= s < T:
                    if s >= 1:
                        pe.wait_ge(av_ready, 4 * s)
                    scores(2 * s + 1)
                if nxt < T:
                    now = slice(WIN + nxt * P, WIN + (nxt + 1) * P)
                    pe.wait_ge(haT_ready, nxt + 1)
                    for j in range(KC):
                        ins = mm(bank[7][0:QD, 0:P], wqc_s[:, j, :], hT[:, j, now], start=j == 0, stop=j == KC - 1)
                    ins.then_inc(qcT_mm, 1)
                    pe.wait_ge(qcT_ready, nxt + 1)
                    for i in range(4):
                        if i >= 2:
                            pe.wait_ge(q_copied, 4 * nxt + i - 1)
                        mm(bank[6 + i % 2][:, :], qcT, wqup_s[:, i * 512:(i + 1) * 512]).then_inc(q_mm, 1)
                    if done >= 0:
                        pe.wait_ge(mom4_ready, done + 1)
                    for j in range(KC):
                        mm(bank[5][:, 0:2 * P], hT[:, j, now], wkv_s[:, j, :], start=j == 0, stop=j == KC - 1)
                    for j in range(KC):
                        ins = mm(bank[5][:, 2 * P:3 * P], hT[:, j, nxt * P:(nxt + 1) * P], wkv_s[:, j, P:2 * P], start=j == 0, stop=j == KC - 1)
                    ins.then_inc(kv_mm, 1)
                if done >= 0:
                    mlp_rows_T(done)
                if last >= 0:
                    if last == 0:
                        pe.wait_ge(ld_w1, 16)
                    pe.wait_ge(av_ready, 4 * s)
                    if s < T:
                        pe.wait_ge(p_ready, 2 * s + 1)
                    for go in range(8):
                        g = go // 2
                        for j in range(4):
                            ins = mm(bank[go // 4][:, (go % 4) * P:(go % 4 + 1) * P], w1_s[:, 4 * g + j, (go % 2) * P:(go % 2 + 1) * P],
                                     aT[:, 4 * g + j, :], start=j == 0, stop=j == 3)
                    ins.then_inc(o1_mm, 1)
                if 0 <= s < T:
                    if nxt < T:
                        pe.wait_ge(q_copied, 4 * (nxt + 1))
                    probs_T(2 * s)
                    pe.wait_ge(v_ready, min(nxt + 1, T))
                    if done >= 0:
                        pe.wait_ge(h4T_ready, done + 1)
                        pe.wait_ge(mom4_ready, done + 1)
                    attend(2 * s)
                    probs_T(2 * s + 1)
                if nxt < T:
                    pe.wait_ge(rope_dve, 2 * nxt + 2)
                    pe.wait_ge(rope_pool, 3 * nxt + 3)
                    pe.wait_ge(q_copied, 4 * (nxt + 1))
                    if last >= 0:
                        pe.wait_ge(o1_ready, 2 * s)
                    if s >= 0:
                        pe.wait_ge(PT_ready, 4 * s + 2)
                    for i in range(4):
                        for j in range(4):
                            ins = pe.transpose(bank[(0, 1, 6, 7)[i]][:, j * P:(j + 1) * P], qk[:, 4 * i + j, :], ident)
                        ins.then_inc(qT_mm, 1)
                    if s >= 0:
                        pe.wait_ge(av_ready, 4 * s + 1)
                    pe.transpose(bank[4][:, 0:P], qk[:, NH, :], ident).then_inc(qT_mm, 1)
                if 0 <= s < T:
                    attend(2 * s + 1)
                if last >= 0:
                    if last == 0:
                        pe.wait_ge(ld_w2, 16)
                    pe.wait_ge(o1_ready, 2 * s)
                    if s < T:
                        pe.wait_ge(av_ready, 4 * s + 2)
                    if s == T:
                        pe.wait_ge(mom4_ready, done + 1)
                    for go in range(8):
                        ins = mm(bank[5][:, 0:DM], oT1[:, go, :], w2_s[:, go, :], start=go == 0, stop=go == 7)
                    ins.then_inc(o2_mm, 1)
                if nxt < T:
                    pe.wait_ge(qT_ready, 5 * (nxt + 1))
                    scores(2 * nxt)
            pe.wait_ge(dec_done, NQ)
            pe.wait_ge(h4T_ready, T - 1)

            def mlp_down(n):
                half, i = n // NT, n % NT
                pe.wait_ge(it_ready, n + 1)
                if i == 0 and half == 1:
                    pe.wait_ge(fin_ready, 4)
                for j in range(4):
                    ins = mm(bank[6 + j // 2][:, (j % 2) * DM:(j % 2 + 1) * DM], it[n % 3][:, j * P:(j + 1) * P], wdn_s[:, i, :],
                             start=i == 0 and j % 2 == 0, stop=i == NT - 1, skip_group_check=True)
                ins.then_inc(dn_mm, 1)

            for n in range(2 * NT):
                half, i = n // NT, n % NT
                if n == 2:
                    mlp_rows_T(T - 1)
                    pe.wait_ge(h4T_ready, T)
                    pe.wait_ge(mom4_ready, T)
                if n >= 3:
                    pe.wait_ge(it_ready, n - 2)
                toks = slice(WIN + half * 512, WIN + half * 512 + 512)
                for a, w in enumerate((wg_s, wu_s)):
                    for j in range(2):
                        ins = mm(bank[2 * (n % 3) + a][:, :], w[:, j, i * P:(i + 1) * P], hT[:, j, toks], start=j == 0, stop=j == 1)
                ins.then_inc(mgu_mm, 1)
                if n >= 1:
                    mlp_down(n - 1)
            mlp_down(2 * NT - 1)


def _layout(i):
    import numpy as np
    i = {k: np.asarray(v) for k, v in i.items()}
    P = 128
    fm = lambda w: np.ascontiguousarray(w.reshape(-1, P, w.shape[-1]).transpose(1, 0, 2))
    col = lambda v: v.reshape(-1, P).T
    f32 = np.float32
    r = np.arange(P)
    k, m = r[:, None], r[None, :]
    masks = [k == m, k <= m, k < m]
    big = f32(-1e30)
    q = k % 64
    window = (m > q) & (m <= q + 64)
    consts = np.stack([a.astype(f32) for a in masks] + [np.where(k > m, big, f32(0)),
                      np.where(window & (m >= 64), f32(0), big), np.where(window, f32(0), big)], 1)
    inv = f32(1.0) / (f32(10000.0) ** (np.arange(0, 64, 2, dtype=f32) / f32(64)))
    ang = np.arange(1024, dtype=f32)[:, None] * inv[None, :]
    rope = np.concatenate([np.cos(ang), np.sin(ang)], 1).astype(f32).reshape(8, P, 64).transpose(1, 0, 2)
    wg = i["L0_ffn_wg"].reshape(64, 2, P, 96)
    wu = i["L0_ffn_wu"].reshape(64, 2, P, 96)
    wgu = np.stack([wg, wu], 1).transpose(0, 3, 1, 2, 4).reshape(32, 2, P, 384).transpose(0, 2, 1, 3)
    wd = i["L0_ffn_wd"].reshape(32, 2, 96, 256).transpose(0, 2, 1, 3)
    perm = lambda w: w.reshape(8, P, 2, w.shape[-1]).transpose(0, 2, 1, 3).reshape(2048, w.shape[-1]).T
    down = i["L1_ffn_down_W_packed"]
    arrays = {
        "x": i["L0_attn_u"].reshape(1024, 256),
        "w_in": fm(i["L0_attn_in_proj_w"].T), "w_out": fm(i["L0_attn_out_proj_w"].T), "gate_w": fm(i["L0_ffn_gate_w"].T),
        "wgu": wgu.reshape(32, P, 768), "wd": wd.reshape(32, 96, 512),
        "wmod": np.stack([fm(i["L0_wmod"]), fm(i["L1_wmod"])]),
        "ccol": np.concatenate([col(i["L0_c"].reshape(-1)), col(i["L1_c"].reshape(-1))], 1),
        "cols": np.concatenate([col(i["L0_attn_ln_w"]), col(i["L0_attn_ln_b"]), col(i["L0_attn_bnorm_w"]), col(i["L0_attn_cnorm_w"]),
                                col(i["L1_attn_q_norm_w"]), col(i["L1_attn_k_norm_w"])], 1),
        "rows": np.concatenate([i["L0_attn_D"], i["L0_attn_dt_bias"], i["L0_attn_A_log"],
                                8192 - 64 * np.arange(64, dtype=f32)])[None],
        "sinks": i["L1_attn_sink_logit"].reshape(8, 2).T,
        "rope": rope, "consts": consts,
        "wqc": fm(i["L1_attn_wq_comp"]), "wqup": i["L1_attn_wq_up"],
        "wkv": np.concatenate([fm(i["L1_attn_wk"]), fm(i["L1_attn_wv"])], 2),
        "w1": i["L1_attn_out_w1"].reshape(4, 4, P, 256).transpose(2, 0, 1, 3).reshape(P, 16, 256),
        "w2": fm(i["L1_attn_out_w2"]),
        "gpk": perm(i["L1_ffn_gate_W_packed"]), "upk": perm(i["L1_ffn_up_W_packed"]),
        "dpk": down.T.reshape(8, P, 256).transpose(1, 0, 2),
        "gsc": perm(i["L1_ffn_gate_scales"]), "usc": perm(i["L1_ffn_up_scales"]), "dsc": i["L1_ffn_down_scales"].T,
    }
    return {n: np.ascontiguousarray(a) for n, a in arrays.items()}


def kernel(**inputs):
    import concourse.bacc as _bacc
    from concourse import mybir as _mybir
    from concourse.bass_utils import run_bass_kernel_spmd as _run

    nc = _bacc.Bacc("TRN2", target_bir_lowering=False, num_devices=1)
    arrays = {f"in_{n}": a for n, a in _layout(inputs).items()}
    args = [nc.dram_tensor(n, a.shape, _mybir.dt.from_np(a.dtype), kind="ExternalInput").ap() for n, a in arrays.items()]
    args.append(nc.dram_tensor("out_0", (1024, 256), _mybir.dt.float32, kind="ExternalOutput").ap())
    adaln_two_layers(nc, *args)
    r = _run(nc, [arrays], core_ids=[0])
    return r.results[0]["out_0"].reshape(1, 1024, 256)
```

```python
import numpy as np
import concourse.bass as bass
from concourse import mybir
from contextlib import ExitStack

ARENA = 53100


def adaln_two_layers(nc, x_in, w_in, w_out, gate_w, wgu, wd, wmod, ccol, cols, rows, sinks, rope, consts,
                     wqc, wqup, wkv, w1, w2, gpk, upk, dpk, gsc, usc, dsc, out):
    f32, bf16, i16, i32, u32, f16 = (mybir.dt.float32, mybir.dt.bfloat16, mybir.dt.int16, mybir.dt.int32,
                                     mybir.dt.uint32, mybir.dt.float16)
    ALU = mybir.AluOpType
    ACT = mybir.ActivationFunctionType
    AX = mybir.AxisListType.X

    P = 128
    T = x_in.shape[0] // P
    DM = x_in.shape[1]
    KC = DM // P
    DI, H, HD, N = 512, 8, 64, 128
    E, CAP, TOPK, FI = 64, 64, 8, 96
    NOWHERE = 8192.0
    SLOTS = E * CAP

    xin = nc.dram_tensor("expert_in", (SLOTS, DM), f32, kind="Internal").ap()
    yex = nc.dram_tensor("expert_out", (SLOTS, DM), f32, kind="Internal").ap()

    ctx = ExitStack()
    with ctx:
        def sem(name):
            return ctx.enter_context(nc.semaphore(name))

        with nc.sbuf_tensor("arena", [P, ARENA], f32) as arena:
            pass
        bank = [ctx.enter_context(nc.psum_tensor(f"bank{i}", [P, 512], f32)) for i in range(8)]

        def at(offset, *dims, parts=P):
            n = int(np.prod(dims))
            assert offset + n <= ARENA, (offset, dims)
            v = arena[0:parts, offset:offset + n]
            if len(dims) == 2:
                v = v.rearrange("p (a b) -> p a b", b=dims[1])
            elif len(dims) == 3:
                v = v.rearrange("p (a b c) -> p a b c", b=dims[1], c=dims[2])
            return v

        def over(v, n):
            return v.unsqueeze(2).to_broadcast([v.shape[0], v.shape[1], n])

        def under(v, n):
            return v.unsqueeze(1).to_broadcast([v.shape[0], n, v.shape[1]])


        x = at(0, T, DM)
        h = at(2048, T, DM)
        mod = [at(4096, 6, DM), at(5632, 6, DM)]
        con = at(7168, 6, P)
        ident, tri, tri_strict, mask_ssd, mask_first, mask_win = (con[:, i, :] for i in range(6))
        ident_b = at(7936, 64).bitcast(bf16)
        strict_b = at(8000, 64).bitcast(bf16)
        ones_b = at(8064, 64).bitcast(bf16)
        mask_ssd_b = at(8128, 256).bitcast(bf16)
        mask_first_b = at(8384, 256).bitcast(bf16)
        mask_win_b = at(8640, 256).bitcast(bf16)
        ones = at(8896, P)
        small = 9024
        ccol_s, cols_s, rows_s, sinks_s = at(small, 4), at(small + 4, 8), at(small + 560, 88), at(small + 36, 8)
        eps5, eps6, one_c = at(small + 44, 1), at(small + 45, 1), at(small + 46, 1)
        silu_c, silu_t = at(small + 48, 4), at(small + 52, 4)
        stats = at(small + 64, T, 6)
        mv = [at(small + 112 + 16 * i, T, 2) for i in range(5)]
        rstd = [at(small + 192 + 8 * i, T) for i in range(5)]
        w8 = at(small + 240, T, TOPK)
        slot8 = at(small + 304, T, TOPK)
        gather8 = at(small + 368, T, TOPK).bitcast(u32)
        scatter8 = at(small + 432, T, TOPK).bitcast(u32)
        wbc = at(small + 496, 1)
        wqk = at(small + 497, 1)
        rope_s = at(10048, T, 64)

        A0 = 10560
        uT = at(A0, KC, T * P)
        zs = at(A0 + 2048, T, DI)
        xs = at(A0 + 6144, T, DI)
        bc = at(A0 + 10240, T, 2 * N + H)
        state = at(A0 + 12352, 2, DI)
        w_in_s = at(A0 + 13376, KC, w_in.shape[2])
        w_out_s = at(A0 + 15952, 4, DM)
        cT = at(A0 + 16976, T, P)
        bT = at(A0 + 18000, T, P)
        bn = at(A0 + 19024, T, P)
        gate_s = at(A0 + 20048, KC, E)
        un = at(A0 + 20176, T, DM)
        Lm = at(A0 + 22224, 2, H * P)
        yT = at(A0 + 26320, 2, DI)
        un_y, yo_s = at(A0 + 20176, 2, DI), at(A0 + 21200, DI)
        junk = at(A0 + 28368, 2, P)
        dt = [at(A0 + 28624 + 64 * i, T * H) for i in range(4)]
        wmod_s = at(A0 + 22224, 2, KC, 6 * DM)
        scb = at(A0 + 12352, 4, P)
        A1 = A0 + 28880
        ss = at(A1, T, 2)
        rbc = at(A1 + 16, T * 2)
        dA = at(A1 + 32, T, H)
        ncs, ecs, dec, etot = (at(A1 + 96 + 64 * i, T, H) for i in range(4))
        nA = at(A1 + 352, H)
        zero = at(A1 + 360, 1024)
        gabs = at(A0 + 16976, 4, DM)
        X0 = A1 + 1392
        XB = X0 + 5120
        xD = [at(XB + 512 * t, DI) for t in range(T)]
        xdec = [at(XB + 4096 + 512 * t if t < 5 else A0 + 24272 + 512 * (t - 5), DI) for t in range(T - 1)]

        ld_x, ld_con, ld_mod, ld_mod_rest, ld_small, ld_c, ld_cols, ld_win, ld_wout, ld_gate = map(
            sem, ["ld_x", "ld_con", "ld_mod", "ld_mod_rest", "ld_small", "ld_c", "ld_cols", "ld_win", "ld_wout", "ld_gate"])
        zero_set, xin_zeroed = sem("zero_set"), sem("xin_zeroed")
        dve_chain, act_chain, pool_chain = sem("dve_chain"), sem("act_chain"), sem("pool_chain")
        pool_consts = sem("pool_consts")
        exp_c, silu_ready, mod_mm, mod_copied, = map(sem, ["exp_c", "silu_ready", "mod_mm", "mod_copied"])
        mod_rest_ready = sem("mod_rest_ready")
        var0_ready, rstd0_ready, var1_ready, rstd1_ready, var2_ready, rstd2_ready = map(
            sem, ["var0_ready", "rstd0_ready", "var1_ready", "rstd1_ready", "var2_ready", "rstd2_ready"])
        un_ready, uT_mm, uT_ready = sem("un_ready"), sem("uT_mm"), sem("uT_ready")
        proj_z, proj_x, proj_bc = sem("proj_z"), sem("proj_x"), sem("proj_bc")
        z_ready, xs_ready, bc_ready = map(sem, ["z_ready", "xs_ready", "bc_ready"])
        dt_abs, dt_log, dA_ready, cs_mm, decs_in, decs_ready = map(
            sem, ["dt_abs", "dt_log", "dA_ready", "cs_mm", "decs_in", "decs_ready"])
        rbc_ready, bcn_ready, bcT_mm, bcT_ready = map(sem, ["rbc_ready", "bcn_ready", "bcT_mm", "bcT_ready"])
        csrow_mm, G_mm, L_ready, M_ready = map(sem, ["csrow_mm", "G_mm", "L_ready", "M_ready"])
        xD_ready, xh_ready, xdec_ready, Yd_mm, Yo_mm, yo_ready, st_mm, state_ready, y_ready = map(
            sem, ["xD_ready", "xh_ready", "xdec_ready", "Yd_mm", "Yo_mm", "yo_ready", "st_mm", "state_ready", "y_ready"])
        yT_mm, yT_ready, o_mm, x1_ready = map(sem, ["yT_mm", "yT_ready", "o_mm", "x1_ready"])

        NS = 13
        PAIR = 4 * KC * FI + 2 * DM
        slot_at = [X0 + PAIR * i if i < 4 else A0 + PAIR * (i - 4) for i in range(NS)]
        wgu_s = [at(o, 2, 2 * KC * FI) for o in slot_at]
        wd_s = [at(o + 4 * KC * FI, 2, DM, parts=FI) for o in slot_at]
        NX = 4
        xg = [at(XB + 5120 + 512 * i, 2, DM) for i in range(2)] + [at(XB + 512 * i, 2, DM) for i in range(2)]
        xgT = [at(XB + 1024 + 512 * i, 4, P) for i in range(2)]
        sg = [at(XB + 2048 + 256 * i, 4 * CAP, parts=FI) for i in range(2)]
        hidT = [at(XB + 2560 + 256 * i, 4 * CAP, parts=FI) for i in range(2)]
        ob = [at(XB + 3072 + 1024 * i, 4, DM, parts=CAP) for i in range(2)]
        NG = E // 4
        h2T = [at(A0 + 28368 + 256 * i, KC, P) for i in range(2)]
        BATCHES = [(0, 1), (1, 3), (3, 4), (4, 5), (5, 6), (6, 7), (7, 8)]
        LAST = [hi - 1 for lo, hi in BATCHES]
        R0 = A0 + 13376
        prob, slotv, wvalid, eqk = (at(R0 + 512 * i, T, E) for i in range(4))
        rest, mask, wfull, valid = (at(R0 + 2048 + 128 * i, 2, E) for i in range(4))
        mask_b, run_b = (at(A0 + 27904 + 256 * i, 256).bitcast(bf16).rearrange("p (a b) -> p a b", b=E) for i in range(2))
        top8 = at(A0 + 27344, T, TOPK)
        rmax, rsum = at(A0 + 27408, T), at(A0 + 27416, T)

        h2_ready, h2T_mm, h2T_ready, logits_mm, lmax_ready, exp_ready = map(
            sem, ["h2_ready", "h2T_mm", "h2T_ready", "logits_mm", "lmax_ready", "exp_ready"])
        mask_ready, pos_mm, slots_ready, scattered = map(sem, ["mask_ready", "pos_mm", "slots_ready", "scattered"])
        w_loaded = [sem(f"w_loaded{i}") for i in range(NS)]
        xg_loaded = [sem(f"xg_loaded{i}") for i in range(NX)]
        xgT_mm, xgT_ready, gu_mm, sg_ready, hid_ready, down_mm, ob_ready = map(
            sem, ["xgT_mm", "xgT_ready", "gu_mm", "sg_ready", "hid_ready", "down_mm", "ob_ready"])
        ob_stored = [sem(f"ob_stored{i}") for i in range(2)]
        w8_ready, x2_ready = sem("w8_ready"), sem("x2_ready")
        gathered = [sem(f"gathered{i}") for i in range(2)]
        gath = [at(A0 + 2048 * i, TOPK, DM) for i in range(2)]
        tmp2 = at(A0 + 11008, DM)
        B0 = A0 + 11520
        MLP = 2048
        NT = MLP // P
        wg_s, wu_s = at(B0, 2, MLP), at(B0 + 4096, 2, MLP)
        wdn_s = at(B0 + 8192, NT, DM)
        QC = 512
        D0 = A0 + 23808
        pk = [at(D0 + 512 * i, QC) for i in range(2)]
        sc = [at(D0 + 1024 + 512 * i, QC) for i in range(2)]
        nib = [[at(D0 + 2048 + 256 * (3 * b + i), QC // 2) for i in range(3)] for b in range(2)]
        NQ = 3 * MLP // QC
        NEARLY, PACE = 2, 1.25
        DEC_LOADS = [sum((48 if m >= 8 else 32) for m in range(n % 2, n + 1, 2)) for n in range(NQ)]
        NH, QD, WIN = 16, 64, 64
        PR = NH // 2
        w12_s = at(A0 + 4096, NH, DM)
        w2_s = at(A0 + 8192, 8, DM)
        wqc_s, wkv_s = at(A0 + 10240, KC, QD), at(A0 + 10368, KC, 2 * P)
        qk = at(D0, NH + 1, P)
        kT = at(D0 + 2176, WIN + T * P)
        Vw = [at(D0 + 3264 + 128 * i, P) for i in range(4)]
        PT = at(D0 + 3776, PR, P)
        wqup_s = at(X0, NH * P, parts=QD)
        hT = at(X0 + 2048, KC, WIN + T * P)
        tmp = at(X0 + 4224, NH + 1, P)
        qT = at(X0 + 6400, 2, NH, WIN)
        Pb = [at(X0 + 8448, PR, P), at(2048 + 4 * DM, PR, P)]
        aT = [at(X0 + 9472, NH, P), at(A0 + 8192, NH, P)]
        qcT = at(A1 + 1024, P, parts=QD)
        sm = small + 660
        ssq, rq = at(sm, NH + 1), at(sm + 20, NH + 1)
        st1, mv1, rs1 = at(sm + 40, 6), at(sm + 48, 2), at(sm + 50, 1)
        st4, mv4, rs4 = at(sm + 104, 6), at(sm + 112, 2), at(sm + 114, 1)
        mx, es, den = ([at(sm + 56 + 8 * i + 24 * b, PR) for b in range(2)] for i in range(3))

        pk_loaded = [sem(f"pk_loaded{i}") for i in range(2)]
        dec_done = sem("dec_done")
        ld_w12, ld_wq, ld_wqup = map(sem, ["ld_w12", "ld_wq", "ld_wqup"])
        pads = sem("pads")
        mom_ready, mom_rstd, ha_ready, haT_mm, haT_ready, qcT_mm, qcT_ready, kv_mm, k_copied, v_ready = map(
            sem, ["mom_ready", "mom_rstd", "ha_ready", "haT_mm", "haT_ready", "qcT_mm", "qcT_ready", "kv_mm", "k_copied", "v_ready"])
        q_mm, q_copied, sq_ready, ssq_ready, rq_ready, qn_ready, rope_dve, rope_pool = map(
            sem, ["q_mm", "q_copied", "sq_ready", "ssq_ready", "rq_ready", "qn_ready", "rope_dve", "rope_pool"])
        qT_mm, qT_ready, s_mm, mx_ready, p_ready, pn_ready, PT_mm, PT_ready, av_mm, av_ready = map(
            sem, ["qT_mm", "qT_ready", "s_mm", "mx_ready", "p_ready", "pn_ready", "PT_mm", "PT_ready", "av_mm", "av_ready"])
        sq_pool, w12_mm, w12_ready, out_mm, mom4_ready, mom4_rstd = map(
            sem, ["sq_pool", "w12_mm", "w12_ready", "out_mm", "mom4_ready", "mom4_rstd"])
        gl = [at(D0 + 512 * i, 512) for i in range(3)]
        it = [at(D0 + 1536 + 512 * i, 512) for i in range(3)]
        f32r = mybir.dt.float32r

        X1 = X0 + 2048
        places = [(A0 + 2048 * i, "gu_hi") for i in range(4)] + [(A0 + 8192, None)] + [(B0 + 2048 * i, "low") for i in range(6)] + [
            (D0, None), (D0 + 1536, "it_low"), (D0 + 3072, "it_hi"), (D0 + 4608, None), (A1, "h4_hi"), (A1 + 1024, None),
            (X0, "dn_hi"), (X1, "h4_low"), (X1 + 1088, "h4_low"), (X0 + 4224, "dn_hi"), (X0 + 6272, None), (X0 + 8448, "h4_hi"),
            (X0 + 9472, None)]
        split = []
        gap = ctx.enter_context(nc.sbuf_tensor("gap", [P, A0], f32))
        for n, (start, name) in enumerate(places):
            end = places[n + 1][0] if n + 1 < len(places) else ARENA
            v = ctx.enter_context(nc.sbuf_tensor(f"{name or 'gap'}_{n}", [P, end - start], f32r if name else f32))
            if name:
                split.append((start, end, v))

        def rounded(v):
            last = v.offset + sum(step * (count - 1) for step, count in list(v.ap)[1:])
            start, end, tensor = next(a for a in split if a[0] <= v.offset and last < a[1])
            return bass.AP(tensor, v.offset - start, [[end - start, P]] + [list(d) for d in list(v.ap)[1:]])

        it_hi = [at(D0 + 3072 + 512 * i, 512) for i in range(3)]
        gu_hi = [at(A0 + 512 * i, 2, 2, P) for i in range(NT)]
        dn_hi = [at(X0 + 256 * i if i < 8 else X0 + 4224 + 256 * (i - 8), DM) for i in range(NT)]
        h4_hi = [at(A1, KC, 512), at(X0 + 8448, KC, 512)]
        h4_split, w_hi_ready, w_split = map(sem, ["h4_split", "w_hi_ready", "w_split"])
        h4_ready, h4T_mm, h4T_ready, mgu_mm, gl_ready, it_ready, dn_mm, fin_ready, out_stored = map(
            sem, ["h4_ready", "h4T_mm", "h4T_ready", "mgu_mm", "gl_ready", "it_ready", "dn_mm", "fin_ready", "out_stored"])
        block = ctx.enter_context(nc.Block())

        @block.sync
        def _(sp):
            thirds = wmod.rearrange("l p j n -> p l j n")
            sp.dma_start(ccol_s, ccol).then_inc(ld_c, 16)
            sp.dma_start(x, x_in.rearrange("(t p) c -> p t c", p=P)).then_inc(ld_x, 16)
            sp.dma_start(wmod_s[:, 0, :, 0:2 * DM], thirds[:, 0, :, 0:2 * DM]).then_inc(ld_mod, 16)
            sp.dma_start(cols_s, cols).then_inc(ld_cols, 16)
            sp.dma_start(con, consts).then_inc(ld_con, 16)
            sp.dma_start(w_in_s, w_in).then_inc(ld_win, 16)
            sp.dma_start(rows_s, rows.to_broadcast([P, rows.shape[1]])).then_inc(ld_small, 16)
            sp.dma_start(wmod_s[:, 0, :, 2 * DM:], thirds[:, 0, :, 2 * DM:]).then_inc(ld_mod_rest, 16)
            sp.dma_start(wmod_s[:, 1], thirds[:, 1]).then_inc(ld_mod_rest, 16)
            for i in range(2):
                sp.dma_start(sinks_s[64 * i:64 * i + 64, :], sinks[i:i + 1, :].to_broadcast([64, 8])).then_inc(ld_small, 16)
            sp.dma_start(w_out_s, w_out).then_inc(ld_wout, 16)
            sp.dma_start(gate_s, gate_w).then_inc(ld_gate, 16)
            sp.dma_start(rope_s, rope).then_inc(ld_small, 16)
            sp.wait_ge(zero_set, 1)
            sp.dma_start(xin.rearrange("(p r a) c -> p r (a c)", p=P, r=8), under(zero, 8)).then_inc(xin_zeroed, 16)
            def load_pair(q, sp=sp):
                i = q % NS
                if q >= NS:
                    sp.wait_ge(down_mm, (q - NS) // 2 + 1)
                sp.dma_start(wgu_s[i].rearrange("p a b -> p (a b)"), wgu[q]).then_inc(w_loaded[i], 16)
                sp.dma_start(wd_s[i].rearrange("p a b -> p (a b)"), wd[q]).then_inc(w_loaded[i], 16)

            def load_codes(n):
                which, c, i = n // 4, n % 4, n % 2
                if n >= 2:
                    sp.wait_ge(dec_done, n - 1)
                if which < 2:
                    src, scales = ((gpk, gsc), (upk, usc))[which]
                    sp.dma_start(pk[i].bitcast(i32), src[:, c * QC:(c + 1) * QC]).then_inc(pk_loaded[i], 16)
                    sp.dma_start(sc[i], scales[:, c * QC:(c + 1) * QC].unsqueeze(1).to_broadcast([8, 16, QC])).then_inc(pk_loaded[i], 16)
                else:
                    sp.dma_start(pk[i].bitcast(i32).rearrange("p (a b) -> p a b", b=DM), dpk[:, 2 * c:2 * c + 2, :]).then_inc(pk_loaded[i], 16)
                    for a in range(2):
                        sp.dma_start(sc[i][:, a * DM:(a + 1) * DM],
                                     dsc[8 * (2 * c + a):8 * (2 * c + a) + 8, :].unsqueeze(1).to_broadcast([8, 16, DM])).then_inc(pk_loaded[i], 16)

            for q in range(4):
                load_pair(q)
            sp.wait_ge(yT_mm, T)
            load_codes(0)
            load_codes(1)
            for q in range(4, NS):
                load_pair(q)
            for n in range(2, NEARLY):
                load_codes(n)

            def load_rows(g):
                if g >= NX:
                    sp.wait_ge(xgT_mm, g - NX + 1)
                sp.dma_start(xg[g % NX], xin[4 * CAP * g:4 * CAP * (g + 1), :].rearrange("(q p) c -> p q c", p=P))                    .then_inc(xg_loaded[g % NX], 16)

            sp.wait_ge(scattered, 16 * T * TOPK)
            for g in range(NX):
                load_rows(g)
            n = NEARLY
            for g in range(NG):
                while n < NQ and 2 * (n - 2) < 2 * NEARLY + g * PACE:
                    load_codes(n)
                    n += 1
                if g + NX < NG:
                    load_rows(g + NX)
                for q in (2 * g + NS - 1, 2 * g + NS):
                    if NS <= q < E // 2:
                        load_pair(q)
                if g == 13:
                    sp.wait_ge(down_mm, 13)
                    sp.dma_start(w12_s, w1).then_inc(ld_w12, 16)
                    sp.dma_start(w2_s, w2).then_inc(ld_w12, 16)
                    sp.dma_start(wqc_s, wqc).then_inc(ld_wq, 16)
                    sp.dma_start(wkv_s, wkv).then_inc(ld_wq, 16)
                    sp.wait_ge(down_mm, 14)
                    sp.dma_start(wqup_s, wqup).then_inc(ld_wqup, 16)
            for t in range(T):
                sp.wait_ge(fin_ready, t + 1)
                sp.dma_start(out[t * P:(t + 1) * P, :], x[:, t, :]).then_inc(out_stored, 16)
            sp.wait_ge(out_stored, 16 * T)

        @block.gpsimd
        def _(pool):
            pool.memset(zero, 0.0).then_inc(zero_set, 1)
            for v, value in ((ones, 1.0), (eps5, 1e-5), (eps6, 1e-6), (one_c, 1.0)):
                pool.memset(v, value).then_inc(pool_consts, 1)
            pool.memset(ones_b, 1.0).then_inc(pool_consts, 1)
            pool.wait_ge(ld_con, 16)
            pool.tensor_copy(ident_b, ident).then_inc(pool_consts, 1)
            pool.tensor_copy(strict_b, tri_strict).then_inc(pool_consts, 1)
            for b, m in ((mask_ssd_b, mask_ssd), (mask_first_b, mask_first), (mask_win_b, mask_win)):
                pool.tensor_copy(b.rearrange("p (r c) -> p r c", c=P), under(m, 4)).then_inc(pool_consts, 1)
            def by_head(v):
                return v.rearrange("p (a b) -> p a b", b=HD)

            pool.wait_ge(ld_small, 64)
            for t in range(T):
                pool.wait_ge(xs_ready, t + 1)
                pool.tensor_tensor(by_head(xD[t]), by_head(xs[:, t, :]), over(rows_s[:, 0:H], HD), ALU.mult).then_inc(xD_ready, 1)
            pool.wait_ge(decs_ready, 3)
            for t in range(T - 1):
                pool.tensor_tensor(by_head(xdec[t]), by_head(xs[:, t, :]), over(dec[:, t, :], HD), ALU.mult).then_inc(xdec_ready, 1)
            pool.wait_ge(mod_rest_ready, 1)
            pool.wait_ge(un_ready, T)
            for t in range(T):
                pool.tensor_tensor(h[:, t, :], h[:, t, :], mod[0][:, 2, :], ALU.mult).then_inc(pool_chain, 1)
                pool.wait_ge(pool_chain, t + 1)
                pool.tensor_tensor(x[:, t, :], x[:, t, :], h[:, t, :], ALU.add).then_inc(xh_ready, 1)

            pool.wait_ge(xin_zeroed, 16)
            for t in range(T):
                pool.wait_ge(slots_ready, 1 + sum(t > last for last in LAST))
                for k in range(TOPK):
                    pool.indirect_dma_start(xin, bass.IndirectOffsetOnAxis(scatter8[:, t, k:k + 1], 0), h[:, t, :], None,
                                            bounds_check=SLOTS - 1, oob_is_err=False).then_inc(scattered, 16)
            for g in range(NG):
                pool.wait_ge(ob_ready, 2 * (g + 1))
                pool.dma_start(yex[4 * CAP * g:4 * CAP * (g + 1), :].rearrange("(e s) c -> s e c", s=CAP), ob[g % 2])                    .then_inc(ob_stored[g % 2], 16)
            for i in range(2):
                pool.wait_ge(ob_stored[i], 16 * NG // 2)
            pool.wait_ge(down_mm, NG)
            def gather(t):
                if t >= 2:
                    pool.wait_ge(x2_ready, t - 1)
                for k in range(TOPK):
                    pool.indirect_dma_start(gath[t % 2][:, k, :], None, yex, bass.IndirectOffsetOnAxis(gather8[:, t, k:k + 1], 0),
                                            bounds_check=SLOTS - 1, oob_is_err=False).then_inc(gathered[t % 2], 16)

            pool.memset(kT[:, 0:WIN], 0.0).then_inc(pads, 1)
            pool.memset(hT[:, :, 0:WIN], 0.0).then_inc(pads, 1)
            for t in range(3):
                gather(t)
            for t in range(T):
                pool.wait_ge(q_copied, 4 * t + 2)
                if t >= 1:
                    pool.wait_ge(rope_dve, 2 * t)
                pool.tensor_tensor(tmp[:, 0:NH // 2, :], qk[:, 0:NH // 2, :], qk[:, 0:NH // 2, :], ALU.mult).then_inc(sq_pool, 1)
                pool.wait_ge(qn_ready, t + 1)
                pool.tensor_tensor(tmp[:, :, 64:96], qk[:, :, 0:32], under(rope_s[:, t, 32:64], NH + 1), ALU.mult).then_inc(rope_pool, 1)
                if t + 3 < T:
                    gather(t + 3)
            for i in range(NT):
                pool.wait_ge(w_hi_ready, i + 1)
                cols = slice(i * P, (i + 1) * P)
                for a, w in enumerate((wg_s, wu_s)):
                    for j in range(2):
                        pool.tensor_tensor(rounded(w[:, j, cols]), w[:, j, cols], rounded(gu_hi[i][:, a, j]), ALU.subtract)
                pool.tensor_tensor(rounded(wdn_s[:, i, :]), wdn_s[:, i, :], rounded(dn_hi[i]), ALU.subtract).then_inc(w_split, 1)
        @block.scalar
        def _(act):
            chained = [0]

            def link(ins):
                chained[0] += 1
                ins.then_inc(act_chain, 1)
                act.wait_ge(act_chain, chained[0])

            def rsqrt(o, i, scale, eps, done):
                link(act.activation(o, i, ACT.Ln, bias=eps, scale=scale))
                act.activation(o, o, ACT.Exp, scale=-0.5).then_inc(done, 1)

            act.preload_act_table_set("natural_log_exp_and_others")
            act.wait_ge(ld_c, 16)
            act.activation(silu_t, ccol_s, ACT.Exp, scale=-1.0).then_inc(exp_c, 1)

            def copy_mod(n):
                act.wait_ge(mod_mm, n + 1)
                act.activation(at(4096 + 512 * n, 512), bank[4 + n % 2][:, :], ACT.Copy).then_inc(mod_copied, 1)

            act.wait_ge(pool_consts, 4)
            act.wait_ge(var0_ready, 1)
            rsqrt(rstd[0], mv[0][:, :, 1], 1.0, eps5, rstd0_ready)
            copy_mod(0)
            act.wait_ge(ld_cols, 16)
            for s in range(T + 2):
                if s < T:
                    act.wait_ge(var1_ready, s + 1)
                    rsqrt(rstd[1][:, s:s + 1], mv[1][:, s, 1:2], 1.0, eps5, rstd1_ready)
                if 1 <= s <= T:
                    t = s - 1
                    act.wait_ge(uT_mm, t + 1)
                    for j in range(KC):
                        act.activation(uT[:, j, t * P:(t + 1) * P], bank[6 + t % 2][:, j * P:(j + 1) * P], ACT.Identity,
                                       scale=cols_s[:, j:j + 1], bias=cols_s[:, 2 + j:3 + j]).then_inc(uT_ready, 1)
                if s >= 2:
                    t = s - 2
                    act.wait_ge(proj_bc, t + 1)
                    if t >= 1:
                        act.wait_ge(bc_ready, t)
                    act.activation(bc[:, t, :], bank[t % 2][:, 0:2 * N + H], ACT.Copy)
                    for j in range(2):
                        ins = act.activation(junk[:, j, :], bank[t % 2][:, j * N:(j + 1) * N], ACT.Square,
                                             accum_out=ss[:, t, j:j + 1])
                    ins.then_inc(bc_ready, 1)
                    act.wait_ge(proj_x, t + 1)
                    act.activation(xs[:, t, :], bank[2 + t % 2][:, :], ACT.Copy).then_inc(xs_ready, 1)
                if 4 <= s < 9:
                    copy_mod(s - 3)
            act.wait_ge(bc_ready, T)
            act.wait_ge(ld_small, 64)
            act.activation(nA, rows_s[:, 16:24], ACT.Exp).then_inc(dt_log, 1)
            act.wait_ge(dt_abs, 1)
            link(act.activation(dt[2], dt[1], ACT.Exp))
            act.activation(dt[2], dt[2], ACT.Ln, bias=1.0).then_inc(dt_log, 1)
            rsqrt(rbc, ss.rearrange("p a b -> p (a b)"), 1.0 / N, eps5, rbc_ready)
            act.wait_ge(decs_in, 1)
            act.activation(ecs.rearrange("p a b -> p (a b)"), bank[4][:, 0:T * H], ACT.Exp).then_inc(decs_ready, 1)
            act.activation(etot.rearrange("p a b -> p (a b)"), bank[4][:, T * H:2 * T * H], ACT.Exp).then_inc(decs_ready, 1)
            act.activation(dec, dec, ACT.Exp).then_inc(decs_ready, 1)

            def decay_matrices(t):
                act.wait_ge(csrow_mm, t + 1)
                if t >= 2:
                    act.wait_ge(Yd_mm, t - 1)
                for i in range(H):
                    ins = act.activation(Lm[:, t % 2, i * P:(i + 1) * P], bank[i // 4][:, (i % 4) * P:(i % 4 + 1) * P],
                                         ACT.Exp, bias=ncs[:, t, i:i + 1])
                ins.then_inc(L_ready, 1)

            decay_matrices(0)
            act.wait_ge(L_ready, 1)
            act.preload_act_table_set("silu_and_others")
            for t in range(T):
                act.wait_ge(proj_z, t + 1)
                act.activation(zs[:, t, :], bank[(6, 7, 5, 3)[t % 4]][:, :], ACT.Silu).then_inc(z_ready, 1)
            act.wait_ge(z_ready, T)
            act.preload_act_table_set("natural_log_exp_and_others")
            act.wait_ge(decs_ready, 3)
            for s in range(T + 3):
                if s + 1 < T:
                    decay_matrices(s + 1)
                if 1 <= s < T:
                    act.wait_ge(Yo_mm, s)
                    if s >= 2:
                        act.wait_ge(y_ready, s)
                    for i in range(H):
                        ins = act.activation(yo_s[:, i * HD:(i + 1) * HD], bank[4][:, i * HD:(i + 1) * HD], ACT.Copy, scale=ecs[:, s, i:i + 1])
                    ins.then_inc(yo_ready, 1)
                if 0 <= s - 3:
                    act.wait_ge(lmax_ready, s - 2)
                    act.activation(prob[:, s - 3, :], prob[:, s - 3, :], ACT.Exp).then_inc(exp_ready, 1)
                if 0 <= s - 1 < T:
                    t = s - 1
                    act.wait_ge(yT_mm, t + 1)
                    if t >= 1:
                        act.wait_ge(o_mm, t)
                    act.activation(yT[:, t % 2, :], bank[6][:, :], ACT.Copy).then_inc(yT_ready, 1)
                if 0 <= s - 2 < T:
                    t = s - 2
                    act.wait_ge(h2T_mm, t + 1)
                    if t >= 2:
                        act.wait_ge(logits_mm, t - 1)
                    act.activation(h2T[t % 2].rearrange("p a b -> p (a b)"), bank[6][:, 0:DM], ACT.Copy).then_inc(h2T_ready, 1)
                if 0 <= s - 1 < T:
                    act.wait_ge(var2_ready, s)
                    rsqrt(rstd[2][:, s - 1:s], mv[2][:, s - 1, 1:2], 1.0, eps5, rstd2_ready)

            act.wait_ge(exp_ready, T)
            act.preload_act_table_set("silu_and_others")
            def copy_rows(g):
                act.wait_ge(xgT_mm, g + 1)
                if g >= 2:
                    act.wait_ge(gu_mm, g - 1)
                act.activation(xgT[g % 2].rearrange("p a b -> p (a b)"), bank[g % 2][:, :], ACT.Copy).then_inc(xgT_ready, 1)

            copy_rows(0)
            for g in range(NG + 1):
                if g + 1 < NG:
                    copy_rows(g + 1)
                if g < NG:
                    act.wait_ge(gu_mm, g + 1)
                    if g >= 2:
                        act.wait_ge(hid_ready, g - 1)
                    act.activation(sg[g % 2], bank[2 + g % 2][0:FI, 0:4 * CAP], ACT.Silu).then_inc(sg_ready, 1)
                if g >= 1:
                    i = (g - 1) % 2
                    act.wait_ge(down_mm, g)
                    if g >= 3:
                        act.wait_ge(ob_stored[i], 16 * ((g - 1) // 2))
                    for a in range(2):
                        act.activation(ob[i][:, 2 * a:2 * a + 2, :].rearrange("p a b -> p (a b)"), bank[4 + 2 * i + a][0:CAP, :],
                                       ACT.Copy).then_inc(ob_ready, 1)
            act.wait_ge(down_mm, NG)
            act.preload_act_table_set("natural_log_exp_and_others")

            for q in range(NH // 2):
                act.wait_ge(w12_mm, q + 1)
                act.activation(w12_s[:, 2 * q:2 * q + 2, :].rearrange("p a b -> p (a b)"), bank[q % 4][:, :], ACT.Copy).then_inc(w12_ready, 1)

            def exp_block(b, half):
                if half == 0:
                    act.wait_ge(mx_ready, b + 1)
                    if b >= 2:
                        act.wait_ge(PT_mm, b - 1)
                for i in range(4 * half, 4 * half + 4):
                    act.activation(Pb[b % 2][:, i, :], bank[2 * (b % 2) + i // 4][:, (i % 4) * P:(i % 4 + 1) * P], ACT.Exp,
                                   bias=mx[b % 2][:, i:i + 1], accum_out=den[b % 2][:, i:i + 1])
                if half == 1:
                    act.activation(es[b % 2], es[b % 2], ACT.Exp).then_inc(p_ready, 1)

            def rows_T(t):
                act.wait_ge(haT_mm, t + 1)
                act.activation(hT[:, :, WIN + t * P:WIN + (t + 1) * P], bank[6][:, 0:DM].rearrange("p (a b) -> p a b", b=P),
                               ACT.Copy).then_inc(haT_ready, 1)
                act.wait_ge(qcT_mm, t + 1)
                act.activation(qcT, bank[7][0:QD, 0:P], ACT.Copy).then_inc(qcT_ready, 1)

            def copy_probs_T(b):
                act.wait_ge(PT_mm, b + 1)
                if b >= 1:
                    act.wait_ge(av_mm, b)
                for i in range(2):
                    src = bank[6 + i]
                    act.activation(PT[:, 4 * i:4 * i + 4, :].rearrange("p a b -> p (a b)"), src[:, :], ACT.Copy).then_inc(PT_ready, 1)

            def copy_attended(b):
                act.wait_ge(av_mm, b + 1)
                if b % 2 == 0 and b >= 4:
                    act.wait_ge(out_mm, b // 2 - 1)
                for i in range(2):
                    src = bank[(1, 5, 2, 3)[2 * (b % 2) + i]]
                    act.activation(aT[b // 2 % 2][:, 8 * i:8 * i + 8, 64 * (b % 2):64 * (b % 2) + 64],
                                   src[:, :].rearrange("p (a b) -> p a b", b=64), ACT.Copy).then_inc(av_ready, 1)

            act.wait_ge(mom_ready, 1)
            rsqrt(rs1, mv1[:, 1:2], 1.0, eps5, mom_rstd)
            rows_T(0)
            for s in range(-1, T + 1):
                nxt, done = s + 1, s - 2
                if 0 <= s < T:
                    exp_block(2 * s, 0)
                    exp_block(2 * s, 1)
                if nxt < T:
                    for i in range(4):
                        act.wait_ge(q_mm, 4 * nxt + i + 1)
                        if nxt >= 1 and i == 0:
                            act.wait_ge(qT_mm, 5 * nxt)
                        act.activation(qk[:, 4 * i:4 * i + 4, :].rearrange("p a b -> p (a b)"), bank[6 + i % 2][:, :],
                                       ACT.Copy).then_inc(q_copied, 1)
                    act.wait_ge(kv_mm, nxt + 1)
                    act.activation(qk[:, NH, :], bank[5][:, 0:P], ACT.Copy).then_inc(k_copied, 1)
                    if nxt >= 2:
                        act.wait_ge(av_mm, 2 * s)
                    act.activation(Vw[(2 * nxt + 1) % 4], bank[5][:, P:2 * P], ACT.Copy)
                    act.activation(Vw[(2 * nxt) % 4], bank[5][:, 2 * P:3 * P], ACT.Copy).then_inc(v_ready, 1)
                    act.wait_ge(k_copied, nxt + 1)
                    if nxt >= 1:
                        act.wait_ge(rope_dve, 2 * nxt)
                    act.activation(tmp[:, NH // 2:, :], qk[:, NH // 2:, :], ACT.Square).then_inc(sq_ready, 1)
                if s == -1:
                    act.wait_ge(mom_ready, 2)
                    rsqrt(rs1, mv1[:, 1:2], 1.0, eps5, mom_rstd)
                if 0 <= s < T:
                    copy_probs_T(2 * s)
                    exp_block(2 * s + 1, 0)
                if nxt < T:
                    act.wait_ge(ssq_ready, nxt + 1)
                    rsqrt(rq, ssq, 1.0 / P, eps6, rq_ready)
                if 0 <= s < T:
                    exp_block(2 * s + 1, 1)
                if done >= 0:
                    act.wait_ge(h4T_mm, done + 1)
                    act.activation(hT[:, :, WIN + done * P:WIN + (done + 1) * P], bank[0][:, 0:DM].rearrange("p (a b) -> p a b", b=P),
                                   ACT.Copy).then_inc(h4T_ready, 1)
                if 0 <= s < T:
                    copy_attended(2 * s)
                    copy_probs_T(2 * s + 1)
                    copy_attended(2 * s + 1)
                if nxt < T:
                    for i in range(4):
                        act.wait_ge(qT_mm, 5 * nxt + i + 1)
                        if nxt >= 1:
                            act.wait_ge(s_mm, 2 * nxt)
                        act.activation(qT[:, :, 4 * i:4 * i + 4, :].rearrange("p s a b -> p a s b"),
                                       bank[(0, 1, 5, 6)[i]][:, :].rearrange("p (a s b) -> p a s b", a=4, s=2), ACT.Copy).then_inc(qT_ready, 1)
                    act.wait_ge(qT_mm, 5 * nxt + 5)
                    act.activation(kT[:, WIN + nxt * P:WIN + (nxt + 1) * P], bank[7][:, 0:P], ACT.Copy, scale=wqk).then_inc(qT_ready, 1)
                if s + 2 < T:
                    rows_T(s + 2)
                if s + 3 < T:
                    act.wait_ge(mom_ready, s + 4)
                    rsqrt(rs1, mv1[:, 1:2], 1.0, eps5, mom_rstd)
                if 1 <= s <= T:
                    act.wait_ge(mom4_ready, s)
                    rsqrt(rs4, mv4[:, 1:2], 1.0, eps5, mom4_rstd)
            act.wait_ge(mom4_rstd, T)
            act.preload_act_table_set("gelu_apprx_tanh_and_others")
            for n in range(2 * NT):
                act.wait_ge(mgu_mm, n + 1)
                if n >= 3:
                    act.wait_ge(it_ready, n - 2)
                act.activation(gl[n % 3], bank[2 * (n % 3)][:, :], ACT.Gelu_apprx_tanh).then_inc(gl_ready, 1)
                if n == 1:
                    act.wait_ge(h4T_mm, T)
                    act.activation(hT[:, :, WIN + (T - 1) * P:WIN + T * P], bank[4][:, 0:DM].rearrange("p (a b) -> p a b", b=P),
                                   ACT.Copy).then_inc(h4T_ready, 1)
        @block.vector
        def _(dve):
            chained = [0]

            def link(ins):
                chained[0] += 1
                ins.then_inc(dve_chain, 1)
                dve.wait_ge(dve_chain, chained[0])

            def moments(src, t, dst):
                link(dve.bn_stats(stats[:, t, :], src))
                return dve.bn_aggr(dst[:, t, :], stats[:, t, :])

            def normed(dst, src, t, m, r):
                return dve.tensor_scalar(dst, src, m[:, t, 0:1], r[:, t:t + 1], ALU.subtract, ALU.mult)

            dve.wait_ge(exp_c, 1)
            link(dve.tensor_scalar(silu_t, silu_t, 1.0, None, ALU.add))
            link(dve.reciprocal(silu_t, silu_t))
            link(dve.tensor_tensor(silu_c, silu_t, ccol_s, ALU.mult))
            dve.tensor_copy(scb, over(silu_c, P)).then_inc(silu_ready, 1)
            dve.wait_ge(ld_x, 16)
            for t in range(T):
                ins = moments(x[:, t, :], t, mv[0])
            ins.then_inc(var0_ready, 1)
            dve.wait_ge(mod_copied, 1)
            link(dve.tensor_scalar(mod[0][:, 1, :], mod[0][:, 1, :], 1.0, None, ALU.add))
            dve.wait_ge(rstd0_ready, 1)
            for t in range(T + 1):
                if t < T:
                    link(normed(h[:, t, :], x[:, t, :], t, mv[0], rstd[0]))
                    link(dve.tensor_tensor(h[:, t, :], h[:, t, :], mod[0][:, 1, :], ALU.mult))
                    link(dve.tensor_tensor(h[:, t, :], h[:, t, :], mod[0][:, 0, :], ALU.add))
                    moments(h[:, t, :], t, mv[1]).then_inc(var1_ready, 1)
                if t >= 1:
                    dve.wait_ge(rstd1_ready, t)
                    normed(un[:, t - 1, :], h[:, t - 1, :], t - 1, mv[1], rstd[1]).then_inc(un_ready, 1)
            dve.wait_ge(ld_small, 64)
            dve.wait_ge(ld_cols, 16)
            link(dve.tensor_tensor(wbc, cols_s[:, 4:5], cols_s[:, 5:6], ALU.mult))
            link(dve.tensor_tensor(wqk, cols_s[:, 6:7], cols_s[:, 7:8], ALU.mult))
            link(dve.tensor_scalar(wqk, wqk, 1.0 / float(np.sqrt(128.0)), None, ALU.mult))
            dve.wait_ge(mod_copied, 6)
            for i in range(2):
                for j in (1, 4):
                    if i or j == 4:
                        dve.tensor_scalar(mod[i][:, j, :], mod[i][:, j, :], 1.0, None, ALU.add)
                    g, a = mod[i][:, j + 1, :], gabs[:, 2 * i + j // 4, :]
                    link(dve.scalar_tensor_tensor(a, g, -1.0, g, ALU.mult, ALU.max))
                    link(dve.tensor_scalar(a, a, 0.25, None, ALU.max))
                    link(dve.tensor_scalar(g, g, 0.0, 2.0, ALU.is_ge, ALU.mult))
                    ins = dve.scalar_tensor_tensor(g, g, -1.0, a, ALU.add, ALU.mult)
                    if i == 0 or j == 1:
                        link(ins)
            ins.then_inc(mod_rest_ready, 1)
            dve.wait_ge(bc_ready, T)
            dtv = [d.rearrange("p (a b) -> p a b", b=H) for d in dt]
            link(dve.tensor_tensor(dtv[0], bc[:, :, 2 * N:], under(rows_s[:, 8:16], T), ALU.add))
            dve.scalar_tensor_tensor(dt[1], dt[0], -1.0, dt[0], ALU.mult, ALU.min).then_inc(dt_abs, 1)
            link(dve.tensor_scalar(dt[0], dt[0], 0.0, None, ALU.max))
            dve.wait_ge(dt_log, 2)
            link(dve.tensor_tensor(dt[3], dt[0], dt[2], ALU.add))
            dve.scalar_tensor_tensor(dA, dtv[3], -1.0, under(nA, T), ALU.mult, ALU.mult).then_inc(dA_ready, 1)
            dve.wait_ge(rbc_ready, 1)

            def bc_norms(t):
                dve.tensor_scalar(bn[:, t, :], bc[:, t, 0:N], rbc[:, 2 * t:2 * t + 1], None, ALU.mult).then_inc(bcn_ready, 1)
                dve.tensor_scalar(bc[:, t, N:2 * N], bc[:, t, N:2 * N], rbc[:, 2 * t + 1:2 * t + 2], None,
                                  ALU.mult).then_inc(bcn_ready, 1)

            bc_norms(0)
            bc_norms(1)
            dve.wait_ge(cs_mm, 1)
            cs, tot = bank[4][:, 0:T * H], bank[4][:, T * H:2 * T * H]
            flat = lambda v: v.rearrange("p a b -> p (a b)")
            link(dve.tensor_scalar(flat(ncs), cs, -1.0, None, ALU.mult))
            dve.tensor_tensor(flat(dec), flat(ncs), tot, ALU.add).then_inc(decs_in, 1)
            for t in range(2, T):
                bc_norms(t)
            for q in range(T // 2):
                dve.wait_ge(bcT_mm, q + 1)
                both = bank[2][:, :].rearrange("p (t a b) -> p a t b", a=2, b=P)
                dve.tensor_copy(bT[:, 2 * q:2 * q + 2, :], both[:, 0])
                dve.tensor_scalar(cT[:, 2 * q:2 * q + 2, :], both[:, 1], wbc, None, ALU.mult).then_inc(bcT_ready, 1)

            hd = lambda v: v.rearrange("p (a b) -> p a b", b=HD)

            def make_M(t):
                M = Lm[:, t % 2, :].rearrange("p (a b) -> p a b", b=P)
                dve.wait_ge(L_ready, t + 1)
                dve.wait_ge(G_mm, t + 1)
                dve.tensor_tensor(M, M, under(bank[2][:, 0:P], H), ALU.mult).then_inc(M_ready, 1)

            def state_after(s):
                dve.wait_ge(st_mm, s + 1)
                new = state[:, (s + 1) % 2, :]
                if s == 0:
                    dve.tensor_copy(new, bank[5][:, :]).then_inc(state_ready, 1)
                else:
                    link(dve.tensor_tensor(hd(new), hd(state[:, s % 2, :]), over(etot[:, s, :], HD), ALU.mult))
                    dve.tensor_tensor(new, new, bank[5][:, :], ALU.add).then_inc(state_ready, 1)

            def less_maximum(t):
                logit = bank[6][:, 2 * P:2 * P + E]
                dve.wait_ge(logits_mm, t + 1)
                link(dve.tensor_reduce(rmax[:, t:t + 1], logit, AX, ALU.max))
                dve.tensor_scalar(prob[:, t, :], logit, rmax[:, t:t + 1], None, ALU.subtract).then_inc(lmax_ready, 1)

            def choose(q):
                lo, hi = BATCHES[q]
                n, ts = hi - lo, slice(lo, hi)
                dve.wait_ge(exp_ready, hi)
                link(dve.tensor_reduce(rsum[:, ts], prob[:, ts, :], AX, ALU.add))
                link(dve.reciprocal(rsum[:, ts], rsum[:, ts]))
                link(dve.tensor_tensor(prob[:, ts, :], prob[:, ts, :], over(rsum[:, ts], E), ALU.mult))
                for t in range(lo, hi):
                    ins = dve.max(top8[:, t, :], prob[:, t, :])
                link(ins)
                for t in range(lo, hi):
                    ins = dve.match_replace(rest[:, t - lo, :], top8[:, t, :], prob[:, t, :], -1.0)
                link(ins)
                link(dve.tensor_scalar(mask[:, 0:n], rest[:, 0:n], 0.0, None, ALU.is_lt))
                link(dve.tensor_copy(mask_b[:, ts, :], mask[:, 0:n]))
                for t in range(lo, hi):
                    if t == 0:
                        ins = dve.memset(run_b[:, 0, :], 0.0)
                    else:
                        ins = dve.tensor_tensor(run_b[:, t, :], run_b[:, t - 1, :], mask_b[:, t - 1, :], ALU.add)
                    if t < hi - 1:
                        link(ins)
                ins.then_inc(mask_ready, 1)
                link(dve.tensor_tensor(wfull[:, 0:n], prob[:, ts, :], mask[:, 0:n], ALU.mult))
                link(dve.tensor_reduce(rsum[:, ts], wfull[:, 0:n], AX, ALU.add))
                link(dve.reciprocal(rsum[:, ts], rsum[:, ts]))
                link(dve.tensor_tensor(wfull[:, 0:n], wfull[:, 0:n], over(rsum[:, ts], E), ALU.mult))

            def place_rows(q):
                lo, hi = BATCHES[q]
                n, ts = hi - lo, slice(lo, hi)
                dve.wait_ge(pos_mm, q + 1)
                place = bank[2][:, P:P + n * E].rearrange("p (a b) -> p a b", b=E)
                sv = slotv[:, ts, :]
                dve.scalar_tensor_tensor(valid[:, 0:n], place, float(CAP), mask[:, 0:n], ALU.is_lt, ALU.mult)
                link(dve.tensor_tensor(sv, under(rows_s[:, 24:88], n), place, ALU.subtract))
                link(dve.tensor_tensor(sv, sv, valid[:, 0:n], ALU.mult))
                for t in range(lo, hi):
                    ins = dve.max(slot8[:, t, :], slotv[:, t, :])
                link(ins)
                dve.tensor_scalar(scatter8[:, ts, :], slot8[:, ts, :], -1.0, NOWHERE, ALU.mult, ALU.add).then_inc(slots_ready, 1)
                dve.tensor_tensor(wvalid[:, ts, :], wfull[:, 0:n], valid[:, 0:n], ALU.mult)

            make_M(0)
            dve.wait_ge(decs_ready, 3)
            for s in range(T + 4):
                if s < T - 1:
                    state_after(s)
                if 0 <= s - 3 < T:
                    less_maximum(s - 3)
                if s + 1 < T:
                    make_M(s + 1)
                if s < T:
                    dve.wait_ge(Yd_mm, s + 1)
                    if s >= 1:
                        dve.wait_ge(yo_ready, s)
                        y = un_y[:, s % 2, :]
                        link(dve.tensor_tensor(y, yo_s, bank[3][:, :], ALU.add))
                        dve.tensor_tensor(zs[:, s, :], zs[:, s, :], y, ALU.mult).then_inc(y_ready, 1)
                    else:
                        dve.tensor_tensor(zs[:, s, :], zs[:, s, :], bank[3][:, :], ALU.mult).then_inc(y_ready, 1)
                if 0 <= s - 1 < T:
                    t = s - 1
                    dve.wait_ge(o_mm, t + 1)
                    dve.wait_ge(xh_ready, t + 1)
                    link(dve.tensor_tensor(h[:, t, :], bank[7][:, 0:DM], mod[0][:, 2, :], ALU.mult))
                    dve.tensor_tensor(x[:, t, :], x[:, t, :], h[:, t, :], ALU.add).then_inc(x1_ready, 1)
                    dve.wait_ge(x1_ready, t + 1)
                    moments(x[:, t, :], t, mv[2]).then_inc(var2_ready, 1)
                if s - 4 in LAST:
                    place_rows(LAST.index(s - 4))
                if s - 3 in LAST:
                    choose(LAST.index(s - 3))
                if 0 <= s - 1 < T:
                    t = s - 1
                    dve.wait_ge(rstd2_ready, t + 1)
                    link(normed(h[:, t, :], x[:, t, :], t, mv[2], rstd[2]))
                    link(dve.tensor_tensor(h[:, t, :], h[:, t, :], mod[0][:, 4, :], ALU.mult))
                    dve.tensor_tensor(h[:, t, :], h[:, t, :], mod[0][:, 3, :], ALU.add).then_inc(h2_ready, 1)

            link(dve.tensor_scalar(eqk[:, :, 0:TOPK], slot8, -1.0, NOWHERE, ALU.mult, ALU.add))
            link(dve.tensor_scalar(gather8, eqk[:, :, 0:TOPK], float(SLOTS - 1), None, ALU.min))
            for k in range(TOPK):
                link(dve.tensor_tensor(eqk, slotv, over(slot8[:, :, k], E), ALU.is_equal))
                link(dve.tensor_tensor(eqk, eqk, wvalid, ALU.mult))
                ins = dve.tensor_reduce(w8[:, :, k], eqk, AX, ALU.add)
                if k < TOPK - 1:
                    link(ins)
            ins.then_inc(w8_ready, 1)
            def decode(n, par):
                which, c, b = n // 4, n % 4, n % 2
                dve.wait_ge(pk_loaded[b], DEC_LOADS[n])
                codes = pk[b].bitcast(i16).rearrange("p (n two) -> p n two", two=2)[:, :, 0]
                v, f, s = (nib[b][i].bitcast(i16) for i in range(3))
                vf, ff = nib[b][0].bitcast(bf16), nib[b][1].bitcast(bf16)
                if par == 0:
                    link(dve.tensor_scalar(v, codes, 0x7, 6, ALU.bitwise_and, ALU.logical_shift_left))
                    dve.tensor_scalar(s, codes, 0x8, 12, ALU.bitwise_and, ALU.logical_shift_left)
                else:
                    link(dve.tensor_scalar(v, codes, 0x70, 2, ALU.bitwise_and, ALU.logical_shift_left))
                    dve.tensor_scalar(s, codes, 0x80, 8, ALU.bitwise_and, ALU.logical_shift_left)
                link(dve.tensor_scalar(v, v, 0x3E00, None, ALU.bitwise_or))
                link(dve.tensor_scalar(ff, vf, -0.25, 0.0, ALU.add, ALU.min))
                link(dve.tensor_tensor(ff, ff, vf, ALU.add))
                link(dve.tensor_tensor(f, f, s, ALU.bitwise_or))
                if which < 2:
                    dst = (wg_s, wu_s)[which][:, par, c * QC:(c + 1) * QC]
                    last = dve.scalar_tensor_tensor(dst, ff, 4.0, sc[b], ALU.mult, ALU.mult)
                else:
                    dst = wdn_s[:, 4 * c + par:4 * c + par + 3:2, :]
                    last = dve.scalar_tensor_tensor(dst, ff.rearrange("p (a b) -> p a b", b=DM), 4.0,
                                                    sc[b].rearrange("p (a b) -> p a b", b=DM), ALU.mult, ALU.mult)
                if par == 0:
                    link(last)
                else:
                    last.then_inc(dec_done, 1)

            for n in range(NEARLY):
                decode(n, 0)
                decode(n, 1)
            late = 2 * NEARLY
            for g in range(NG):
                dve.wait_ge(sg_ready, g + 1)
                if g >= 2:
                    dve.wait_ge(down_mm, g - 1)
                dve.tensor_tensor(hidT[g % 2], sg[g % 2], bank[2 + g % 2][0:FI, 4 * CAP:8 * CAP], ALU.mult).then_inc(hid_ready, 1)
                while late < 2 * NQ and late < 2 * NEARLY + (g + 1) * PACE:
                    decode(late // 2, late % 2)
                    late += 1

            def combine(t):
                dve.wait_ge(gathered[t % 2], 16 * TOPK * (t // 2 + 1))
                g = gath[t % 2]
                link(dve.tensor_scalar(g[:, 0, :], g[:, 0, :], w8[:, t, 0:1], None, ALU.mult))
                for k in range(1, TOPK):
                    link(dve.scalar_tensor_tensor(g[:, 0, :], g[:, k, :], w8[:, t, k:k + 1], g[:, 0, :], ALU.mult, ALU.add))
                link(dve.tensor_tensor(g[:, 1, :], g[:, 0, :], mod[0][:, 5, :], ALU.mult))
                dve.tensor_tensor(x[:, t, :], x[:, t, :], g[:, 1, :], ALU.add).then_inc(x2_ready, 1)
                dve.wait_ge(x2_ready, t + 1)

            def shift_scale(dst, t, m, mean_var, rs):
                link(dve.tensor_scalar(dst, x[:, t, :], mean_var[:, 0:1], rs, ALU.subtract, ALU.mult))
                link(dve.tensor_tensor(dst, dst, mod[1][:, m + 1, :], ALU.mult))
                return dve.tensor_tensor(dst, dst, mod[1][:, m, :], ALU.add)

            def combine_moments(t):
                combine(t)
                link(dve.bn_stats(st1, x[:, t, :]))
                dve.bn_aggr(mv1, st1).then_inc(mom_ready, 1)

            def norm_a(t):
                dve.wait_ge(mom_rstd, t + 1)
                if t >= 2:
                    dve.wait_ge(haT_mm, t - 1)
                shift_scale(h[:, t % 2, :], t, 0, mv1, rs1).then_inc(ha_ready, 1)

            def residual(t):
                dve.wait_ge(out_mm, t + 1)
                link(dve.tensor_tensor(tmp2, bank[4][:, 0:DM], mod[1][:, 2, :], ALU.mult))
                link(dve.tensor_tensor(x[:, t, :], x[:, t, :], tmp2, ALU.add))
                link(dve.bn_stats(st4, x[:, t, :]))
                dve.bn_aggr(mv4, st4).then_inc(mom4_ready, 1)

            def norm_4(t):
                dve.wait_ge(mom4_rstd, t + 1)
                if t >= 2:
                    dve.wait_ge(h4T_mm, t - 1)
                shift_scale(h[:, 2 + t % 2, :], t, 3, mv4, rs4).then_inc(h4_ready, 1)

            def maxima(b):
                m, e = mx[b % 2], es[b % 2]
                dve.wait_ge(s_mm, b + 1)
                for i in range(2):
                    ins = dve.tensor_reduce(m[:, 4 * i:4 * i + 4], bank[2 * (b % 2) + i][:, :].rearrange("p (a b) -> p a b", b=P), AX, ALU.max)
                link(ins)
                link(dve.tensor_tensor(m, m, sinks_s, ALU.max))
                link(dve.tensor_scalar(m, m, -1.0, None, ALU.mult))
                dve.tensor_tensor(e, sinks_s, m, ALU.add).then_inc(mx_ready, 1)

            def over_sums(b):
                d = den[b % 2]
                dve.wait_ge(p_ready, b + 1)
                link(dve.tensor_tensor(d, d, es[b % 2], ALU.add))
                link(dve.reciprocal(d, d))
                dve.tensor_tensor(Pb[b % 2], Pb[b % 2], over(d, P), ALU.mult).then_inc(pn_ready, 1)

            def high(dst, src):
                return dve.tensor_copy(rounded(dst), src)

            def split_rows(t, n):
                dve.wait_ge(h4T_ready, t + n)
                dst = h4_hi[t // 4][:, :, (t % 4) * P:(t % 4 + n) * P]
                src = hT[:, :, WIN + t * P:WIN + (t + n) * P]
                link(high(dst, src))
                for j in range(KC):
                    dve.tensor_tensor(rounded(src[:, j]), src[:, j], rounded(dst[:, j]), ALU.subtract).then_inc(h4_split, n)

            def weights_high(i):
                cols = slice(i * P, (i + 1) * P)
                high(gu_hi[i][:, 0], wg_s[:, :, cols])
                high(gu_hi[i][:, 1], wu_s[:, :, cols])
                high(dn_hi[i], wdn_s[:, i, :]).then_inc(w_hi_ready, 1)

            combine_moments(0)
            norm_a(0)
            for s in range(-1, T + 1):
                nxt, done = s + 1, s - 2
                if 0 <= s < T:
                    maxima(2 * s)
                    maxima(2 * s + 1)
                    over_sums(2 * s)
                if s == -1:
                    combine_moments(1)
                elif s + 2 < T:
                    norm_a(s + 2)
                if done >= 0:
                    norm_4(done)
                if nxt < T:
                    dve.wait_ge(sq_pool, nxt + 1)
                    dve.tensor_reduce(ssq[:, 0:NH // 2], tmp[:, 0:NH // 2, :], AX, ALU.add)
                    dve.wait_ge(sq_ready, nxt + 1)
                    dve.tensor_reduce(ssq[:, NH // 2:], tmp[:, NH // 2:, :], AX, ALU.add).then_inc(ssq_ready, 1)
                    dve.wait_ge(rq_ready, nxt + 1)
                    dve.tensor_tensor(qk, qk, over(rq, P), ALU.mult).then_inc(qn_ready, 1)
                if 0 <= s < T:
                    over_sums(2 * s + 1)
                if nxt < T:
                    dve.wait_ge(qn_ready, nxt + 1)
                    cos, sin = under(rope_s[:, nxt, 0:32], NH + 1), under(rope_s[:, nxt, 32:64], NH + 1)
                    dve.tensor_tensor(tmp[:, :, 0:32], qk[:, :, 0:32], cos, ALU.mult)
                    dve.tensor_tensor(tmp[:, :, 32:64], qk[:, :, 32:64], sin, ALU.mult)
                    dve.tensor_tensor(tmp[:, :, 96:128], qk[:, :, 32:64], cos, ALU.mult).then_inc(rope_dve, 1)
                    dve.wait_ge(rope_dve, 2 * nxt + 1)
                    dve.wait_ge(rope_pool, nxt + 1)
                    dve.tensor_tensor(qk[:, :, 0:32], tmp[:, :, 0:32], tmp[:, :, 32:64], ALU.subtract)
                    dve.tensor_tensor(qk[:, :, 32:64], tmp[:, :, 64:96], tmp[:, :, 96:128], ALU.add).then_inc(rope_dve, 1)
                if s == -1:
                    norm_a(1)
                if 0 <= s - 2 < 4:
                    split_rows(s - 2, 1)
                if s + 3 < T:
                    combine_moments(s + 3)
                if s == T - 1:
                    for i in range(3):
                        weights_high(i)
                if 1 <= s <= T:
                    residual(s - 1)
            norm_4(T - 1)
            for n in range(2 * NT):
                dve.wait_ge(gl_ready, n + 1)
                if n >= 3:
                    dve.wait_ge(dn_mm, n - 2)
                link(dve.tensor_tensor(it[n % 3], gl[n % 3], bank[2 * (n % 3) + 1][:, :], ALU.mult))
                link(high(it_hi[n % 3], it[n % 3]))
                dve.tensor_tensor(rounded(it[n % 3]), it[n % 3], rounded(it_hi[n % 3]), ALU.subtract).then_inc(it_ready, 1)
                if n + 3 < NT:
                    weights_high(n + 3)
                if n == 8:
                    split_rows(4, 4)
                if n % NT == NT - 1:
                    half = n // NT
                    dve.wait_ge(dn_mm, n + 1)
                    for i in range(4):
                        t = 4 * half + i
                        if t >= 1:
                            dve.wait_ge(fin_ready, t)
                        link(dve.tensor_tensor(tmp2, bank[6 + i // 2][:, (i % 2) * DM:(i % 2 + 1) * DM], mod[1][:, 5, :], ALU.mult))
                        dve.tensor_tensor(x[:, t, :], x[:, t, :], tmp2, ALU.add).then_inc(fin_ready, 1)
        @block.tensor
        def _(pe):
            def mm(o, lhsT, rhs, start=True, stop=True, **kw):
                return pe.matmul(o, lhsT, rhs, start=start, stop=stop, **kw)

            def modulation(n):
                if n >= 2:
                    pe.wait_ge(mod_copied, n - 1)
                for j in range(KC):
                    ins = mm(bank[4 + n % 2][:, :], scb[:, 2 * (n // 3) + j, :], wmod_s[:, n // 3, j, (n % 3) * 512:(n % 3 + 1) * 512],
                             start=j == 0, stop=j == KC - 1)
                ins.then_inc(mod_mm, 1)

            def project(t, o, lo, hi, done):
                for j in range(KC):
                    ins = mm(o[:, 0:hi - lo], uT[:, j, t * P:(t + 1) * P], w_in_s[:, j, lo:hi], start=j == 0, stop=j == KC - 1)
                ins.then_inc(done, 1)

            pe.wait_ge(silu_ready, 1)
            pe.wait_ge(ld_mod, 16)
            modulation(0)
            pe.wait_ge(ld_con, 16)
            for s in range(T + 1):
                if s < T:
                    pe.wait_ge(un_ready, s + 1)
                    if s >= 2:
                        pe.wait_ge(uT_ready, 2 * (s - 1))
                    for j in range(KC):
                        ins = pe.transpose(bank[6 + s % 2][:, j * P:(j + 1) * P], un[:, s, j * P:(j + 1) * P], ident)
                    ins.then_inc(uT_mm, 1)
                if s >= 1:
                    t = s - 1
                    if t == 0:
                        pe.wait_ge(ld_win, 16)
                    pe.wait_ge(uT_ready, 2 * (t + 1))
                    if t >= 2:
                        pe.wait_ge(bc_ready, t - 1)
                        pe.wait_ge(xs_ready, t - 1)
                    project(t, bank[t % 2], 2 * DI, 2 * DI + 2 * N + H, proj_bc)
                    project(t, bank[2 + t % 2], DI, 2 * DI, proj_x)
                if 3 <= s < 8:
                    if s == 3:
                        pe.wait_ge(ld_mod_rest, 32)
                    modulation(s - 2)
            pe.wait_ge(uT_ready, 2 * T)
            pe.wait_ge(mod_copied, 6)
            for t in range(4):
                if t == 3:
                    pe.wait_ge(xs_ready, T)
                project(t, bank[(6, 7, 5, 3)[t]], 0, DI, proj_z)
            pe.wait_ge(dA_ready, 1)
            pe.wait_ge(pool_consts, 10)
            dAf = dA.rearrange("p a b -> p (a b)")
            mm(bank[4][:, 0:T * H], tri, dAf)
            mm(bank[4][:, T * H:2 * T * H], ones, dAf).then_inc(cs_mm, 1)

            def cs_rows(t):
                if t >= 1:
                    pe.wait_ge(L_ready, t)
                for i in range(H):
                    mm(bank[i // 4][:, (i % 4) * P:(i % 4 + 1) * P], dA[:, t, i:i + 1].to_broadcast([P, P]), tri,
                       start=i % 4 == 0, stop=False, skip_group_check=True)
                for i in range(2):
                    ins = mm(bank[i][:, :], ident_b, mask_ssd_b, start=False, stop=True, skip_group_check=True)
                ins.then_inc(csrow_mm, 1)

            cs_rows(0)
            for q in range(T // 2):
                pe.wait_ge(bcn_ready, 4 * q + 4)
                if q >= 1:
                    pe.wait_ge(bcT_ready, q)
                for i in range(2):
                    pe.transpose(bank[2][:, 2 * i * P:(2 * i + 1) * P], bn[:, 2 * q + i, :], ident)
                    ins = pe.transpose(bank[2][:, (2 * i + 1) * P:(2 * i + 2) * P], bc[:, 2 * q + i, N:2 * N], ident)
                ins.then_inc(bcT_mm, 1)
                t = 4 + q
                pe.wait_ge(z_ready, t - 3)
                project(t, bank[(6, 7, 5, 3)[q]], 0, DI, proj_z)
            pe.wait_ge(bcT_ready, T // 2)
            mm(bank[2][:, 0:P], bT[:, 0, :], cT[:, 0, :]).then_inc(G_mm, 1)
            pe.wait_ge(decs_ready, 3)

            def places(s):
                if s - 4 in LAST:
                    q = LAST.index(s - 4)
                    lo, hi = BATCHES[q]
                    pe.wait_ge(mask_ready, q + 1)
                    pe.wait_ge(M_ready, min(s + 1, T))
                    if q >= 1:
                        pe.wait_ge(slots_ready, q)
                    for t in range(lo, hi):
                        o = bank[2][:, P + (t - lo) * E:P + (t - lo + 1) * E]
                        mm(o, strict_b, mask_b[:, t, :], stop=False)
                        ins = mm(o, ones_b, run_b[:, t, :], start=False)
                    ins.then_inc(pos_mm, 1)

            for s in range(T + 4):
                if s + 1 < T:
                    cs_rows(s + 1)
                if s < T:
                    if s == 0:
                        pe.wait_ge(z_ready, T)
                    if s < T - 1:
                        pe.wait_ge(xdec_ready, s + 1)
                        if s >= 1:
                            pe.wait_ge(state_ready, s)
                        mm(bank[5][:, :], bn[:, s, :], xdec[s]).then_inc(st_mm, 1)
                    if s >= 1:
                        pe.wait_ge(state_ready, s)
                        if s >= 2:
                            pe.wait_ge(yo_ready, s - 1)
                        mm(bank[4][:, :], cT[:, s, :], state[:, s % 2, :]).then_inc(Yo_mm, 1)
                    if s >= 1:
                        pe.wait_ge(y_ready, s)
                    pe.wait_ge(xD_ready, s + 1)
                    mm(bank[3][:, :], ident, xD[s], start=True, stop=False, skip_group_check=True)
                    places(s)
                    if s + 1 < T:
                        pe.wait_ge(M_ready, s + 1)
                        if s >= 5:
                            pe.wait_ge(slots_ready, sum(t <= s - 5 for t in LAST))
                        mm(bank[2][:, 0:P], bT[:, s + 1, :], cT[:, s + 1, :]).then_inc(G_mm, 1)
                    pe.wait_ge(M_ready, s + 1)
                    for i in range(H):
                        ins = mm(bank[3][:, i * HD:(i + 1) * HD], Lm[:, s % 2, i * P:(i + 1) * P], xs[:, s, i * HD:(i + 1) * HD],
                                 start=False, stop=True, skip_group_check=True)
                    ins.then_inc(Yd_mm, 1)
                else:
                    places(s)
                if 0 <= s - 1 < T:
                    t = s - 1
                    pe.wait_ge(y_ready, t + 1)
                    if t >= 2:
                        pe.wait_ge(h2T_ready, t - 1)
                        pe.wait_ge(lmax_ready, t - 1)
                    for j in range(4):
                        ins = pe.transpose(bank[6][:, j * P:(j + 1) * P], zs[:, t, j * P:(j + 1) * P], ident)
                    ins.then_inc(yT_mm, 1)
                    if t == 0:
                        pe.wait_ge(ld_wout, 16)
                    pe.wait_ge(yT_ready, t + 1)
                    if t >= 1:
                        pe.wait_ge(x1_ready, t)
                    for j in range(4):
                        ins = mm(bank[7][:, 0:DM], yT[:, t % 2, j * P:(j + 1) * P], w_out_s[:, j, :], start=j == 0, stop=j == 3)
                    ins.then_inc(o_mm, 1)
                if 0 <= s - 2 < T:
                    t = s - 2
                    pe.wait_ge(h2_ready, t + 1)
                    if t >= 1:
                        pe.wait_ge(lmax_ready, t)
                    for j in range(KC):
                        ins = pe.transpose(bank[6][:, j * P:(j + 1) * P], h[:, t, j * P:(j + 1) * P], ident)
                    ins.then_inc(h2T_mm, 1)
                    if t == 0:
                        pe.wait_ge(ld_gate, 16)
                    pe.wait_ge(h2T_ready, t + 1)
                    for j in range(KC):
                        ins = mm(bank[6][:, 2 * P:2 * P + E], h2T[t % 2][:, j, :], gate_s[:, j, :], start=j == 0, stop=j == KC - 1)
                    ins.then_inc(logits_mm, 1)
            def rows_T(g):
                pe.wait_ge(xg_loaded[g % NX], 16 * (g // NX + 1))
                if g >= 2:
                    pe.wait_ge(xgT_ready, g - 1)
                for q in range(2):
                    for j in range(KC):
                        ins = pe.transpose(bank[g % 2][:, (2 * q + j) * P:(2 * q + j + 1) * P], xg[g % NX][:, q, j * P:(j + 1) * P], ident)
                ins.then_inc(xgT_mm, 1)

            def gate_up(g):
                pe.wait_ge(xgT_ready, g + 1)
                if g >= 2:
                    pe.wait_ge(hid_ready, g - 1)
                for e in range(4):
                    q = 2 * g + e // 2
                    if e % 2 == 0:
                        pe.wait_ge(w_loaded[q % NS], 32 * (q // NS + 1))
                    w = wgu_s[q % NS][:, e % 2, :].rearrange("p (a j f) -> p a j f", a=2, j=KC)
                    for a in range(2):
                        for j in range(KC):
                            ins = mm(bank[2 + g % 2][0:FI, (4 * a + e) * CAP:(4 * a + e + 1) * CAP], w[:, a, j, :],
                                     xgT[g % 2][:, 2 * (e // 2) + j, (e % 2) * CAP:(e % 2 + 1) * CAP], start=j == 0, stop=j == KC - 1)
                ins.then_inc(gu_mm, 1)

            def down(g):
                pe.wait_ge(hid_ready, g + 1)
                if g >= 2:
                    pe.wait_ge(ob_ready, 2 * (g - 1))
                for e in range(4):
                    q = 2 * g + e // 2
                    ins = mm(bank[4 + 2 * (g % 2) + e // 2][0:CAP, (e % 2) * DM:(e % 2 + 1) * DM],
                             hidT[g % 2][:, e * CAP:(e + 1) * CAP], wd_s[q % NS][:, e % 2, :])
                ins.then_inc(down_mm, 1)

            pe.wait_ge(slots_ready, len(BATCHES))
            rows_T(0)
            for g in range(NG):
                if g + 1 < NG:
                    rows_T(g + 1)
                gate_up(g)
                if g >= 1:
                    down(g - 1)
            down(NG - 1)
            def scores(b):
                keys = kT[:, 64 * b:64 * b + P]
                for i in range(2):
                    o = bank[2 * (b % 2) + i]
                    mm(o[:, :], ident_b, mask_first_b if b == 0 else mask_win_b, start=True, stop=False, skip_group_check=True)
                    for j in range(4):
                        p = 4 * i + j
                        ins = mm(o[:, j * P:(j + 1) * P], qT[:, b % 2, 2 * p:2 * p + 2, :].rearrange("p a b -> p (a b)"), keys,
                                 start=False, stop=True, skip_group_check=True)
                ins.then_inc(s_mm, 1)

            def probs_T(b):
                pe.wait_ge(pn_ready, b + 1)
                for i in range(PR):
                    o = bank[6 + i // 4]
                    ins = pe.transpose(o[:, (i % 4) * P:(i % 4 + 1) * P], Pb[b % 2][:, i, :], ident)
                ins.then_inc(PT_mm, 1)

            def attend(b):
                pe.wait_ge(PT_ready, 2 * b + 2)
                for i in range(2):
                    ins = mm(bank[(1, 5, 2, 3)[2 * (b % 2) + i]][:, :], Vw[b % 4], PT[:, 4 * i:4 * i + 4, :])
                ins.then_inc(av_mm, 1)

            def mlp_rows_T(t, o):
                pe.wait_ge(h4_ready, t + 1)
                pair = h[:, 2 + t % 2, :].rearrange("p (k two) -> p two k", two=2)
                for j in range(2):
                    ins = pe.transpose(o[:, j * P:(j + 1) * P], pair[:, j, :], ident)
                ins.then_inc(h4T_mm, 1)

            pe.wait_ge(ob_ready, 2 * NG)
            pe.wait_ge(ld_w12, 32)
            for i in range(NH):
                if i % 2 == 0 and i >= 8:
                    pe.wait_ge(w12_ready, i // 2 - 3)
                for j in range(2):
                    ins = mm(bank[(i // 2) % 4][:, (i % 2) * DM:(i % 2 + 1) * DM], w12_s[:, i, j * P:(j + 1) * P],
                             w2_s[:, 2 * (i // 4) + j, :], start=j == 0, stop=j == 1)
                if i % 2:
                    ins.then_inc(w12_mm, 1)
            pe.wait_ge(w12_ready, NH // 2)

            def states_T(t):
                pe.wait_ge(ha_ready, t + 1)
                if t >= 1:
                    pe.wait_ge(qT_ready, 5 * t - 1)
                for j in range(KC):
                    ins = pe.transpose(bank[6][:, j * P:(j + 1) * P], h[:, t % 2, j * P:(j + 1) * P], ident)
                ins.then_inc(haT_mm, 1)

            def queries_narrow(t):
                pe.wait_ge(haT_ready, t + 1)
                if t >= 1:
                    pe.wait_ge(qT_ready, 5 * t)
                    pe.wait_ge(q_mm, 4 * t)
                for j in range(KC):
                    ins = mm(bank[7][0:QD, 0:P], wqc_s[:, j, :], hT[:, j, WIN + t * P:WIN + (t + 1) * P], start=j == 0, stop=j == KC - 1)
                ins.then_inc(qcT_mm, 1)

            def queries(t, i):
                pe.wait_ge(qcT_ready, t + 1)
                if i >= 2:
                    pe.wait_ge(q_copied, 4 * t + i - 1)
                mm(bank[6 + i % 2][:, :], qcT, wqup_s[:, i * 512:(i + 1) * 512]).then_inc(q_mm, 1)

            def project_out(t, heads):
                for i in heads:
                    ins = mm(bank[4][:, 0:DM], aT[t % 2][:, i, :], w12_s[:, i, :], start=i == 0, stop=i == NH - 1, skip_group_check=True)
                if i == NH - 1:
                    ins.then_inc(out_mm, 1)

            states_T(0)
            pe.wait_ge(ld_wq, 32)
            pe.wait_ge(ld_wqup, 16)
            pe.wait_ge(pads, 2)
            queries_narrow(0)
            for s in range(-1, T + 1):
                nxt, last, done = s + 1, s - 1, s - 2
                if 0 <= s < T:
                    if s >= 1:
                        pe.wait_ge(av_ready, 4 * s)
                    scores(2 * s + 1)
                if nxt < T:
                    now = slice(WIN + nxt * P, WIN + (nxt + 1) * P)
                    queries(nxt, 0)
                    queries(nxt, 1)
                    if nxt >= 1:
                        pe.wait_ge(qT_ready, 5 * nxt)
                    for j in range(KC):
                        mm(bank[5][:, 0:2 * P], hT[:, j, now], wkv_s[:, j, :], start=j == 0, stop=j == KC - 1)
                    for j in range(KC):
                        ins = mm(bank[5][:, 2 * P:3 * P], hT[:, j, nxt * P:(nxt + 1) * P], wkv_s[:, j, P:2 * P], start=j == 0, stop=j == KC - 1)
                    ins.then_inc(kv_mm, 1)
                    queries(nxt, 2)
                    queries(nxt, 3)
                if 0 <= s < T:
                    if nxt < T:
                        pe.wait_ge(q_copied, 4 * (nxt + 1))
                    probs_T(2 * s)
                if last >= 0:
                    pe.wait_ge(av_ready, 4 * s)
                    if done >= 0:
                        pe.wait_ge(mom4_ready, done + 1)
                    project_out(last, range(0, 5))
                if 0 <= s < T:
                    pe.wait_ge(v_ready, min(nxt + 1, T))
                    pe.wait_ge(p_ready, 2 * s + 1)
                    attend(2 * s)
                if done >= 0:
                    mlp_rows_T(done, bank[0])
                if last >= 0:
                    project_out(last, range(5, 11))
                if 0 <= s < T:
                    pe.wait_ge(PT_ready, 4 * s + 2)
                    probs_T(2 * s + 1)
                if last >= 0:
                    project_out(last, range(11, 13))
                if 0 <= s < T:
                    attend(2 * s + 1)
                if nxt < T:
                    pe.wait_ge(rope_dve, 2 * nxt + 2)
                    pe.wait_ge(q_copied, 4 * (nxt + 1))
                    pe.wait_ge(v_ready, nxt + 1)
                    if done >= 0:
                        pe.wait_ge(h4T_ready, done + 1)
                    if s >= 0:
                        pe.wait_ge(PT_ready, 4 * s + 4)
                        pe.wait_ge(av_ready, 4 * s + 2)
                    for i in range(4):
                        for j in range(4):
                            ins = pe.transpose(bank[(0, 1, 5, 6)[i]][:, j * P:(j + 1) * P], qk[:, 4 * i + j, :], ident)
                        ins.then_inc(qT_mm, 1)
                    pe.transpose(bank[7][:, 0:P], qk[:, NH, :], ident).then_inc(qT_mm, 1)
                if last >= 0:
                    project_out(last, range(13, NH))
                if s + 2 < T:
                    states_T(s + 2)
                    queries_narrow(s + 2)
                if nxt < T:
                    pe.wait_ge(qT_ready, 5 * (nxt + 1))
                    scores(2 * nxt)
            pe.wait_ge(dec_done, NQ)
            pe.wait_ge(h4T_ready, T - 1)

            def mlp_down(n):
                half, i = n // NT, n % NT
                pe.wait_ge(it_ready, n + 1)
                if i == 0 and half == 1:
                    pe.wait_ge(fin_ready, 4)
                for j in range(4):
                    hi, lo = (v[n % 3][:, j * P:(j + 1) * P] for v in (it_hi, it))
                    for k, (l, r) in enumerate(((hi, dn_hi[i]), (hi, wdn_s[:, i, :]), (lo, dn_hi[i]))):
                        ins = mm(bank[6 + j // 2][:, (j % 2) * DM:(j % 2 + 1) * DM], rounded(l), rounded(r),
                                 start=i == 0 and j % 2 == 0 and k == 0, stop=i == NT - 1 and k == 2, skip_group_check=True)
                ins.then_inc(dn_mm, 1)

            for n in range(2 * NT):
                half, i = n // NT, n % NT
                if n == 2:
                    pe.wait_ge(mom4_ready, T)
                    mlp_rows_T(T - 1, bank[4])
                    pe.wait_ge(h4T_ready, T)
                if n >= 3:
                    pe.wait_ge(it_ready, n - 2)
                toks = slice(WIN + half * 512, WIN + half * 512 + 512)
                pe.wait_ge(w_split, i + 1)
                pe.wait_ge(h4_split, 4 * KC * (half + 1))
                for a, w in enumerate((wg_s, wu_s)):
                    for j in range(2):
                        hi, lo = gu_hi[i][:, a, j, :], w[:, j, i * P:(i + 1) * P]
                        xhi, xlo = h4_hi[half][:, j, :], hT[:, j, toks]
                        for k, (l, r) in enumerate(((hi, xhi), (hi, xlo), (lo, xhi))):
                            ins = mm(bank[2 * (n % 3) + a][:, :], rounded(l), rounded(r), start=j == 0 and k == 0,
                                     stop=j == 1 and k == 2)
                ins.then_inc(mgu_mm, 1)
                if n >= 1:
                    mlp_down(n - 1)
            mlp_down(2 * NT - 1)


def _layout(i):
    import numpy as np
    i = {k: np.asarray(v) for k, v in i.items()}
    P = 128
    fm = lambda w: np.ascontiguousarray(w.reshape(-1, P, w.shape[-1]).transpose(1, 0, 2))
    col = lambda v: v.reshape(-1, P).T
    f32 = np.float32
    r = np.arange(P)
    k, m = r[:, None], r[None, :]
    masks = [k == m, k <= m, k < m]
    big = f32(-1e30)
    q = k % 64
    window = (m > q) & (m <= q + 64)
    consts = np.stack([a.astype(f32) for a in masks] + [np.where(k > m, big, f32(0)),
                      np.where(window & (m >= 64), f32(0), big), np.where(window, f32(0), big)], 1)
    inv = f32(1.0) / (f32(10000.0) ** (np.arange(0, 64, 2, dtype=f32) / f32(64)))
    ang = np.arange(1024, dtype=f32)[:, None] * inv[None, :]
    rope = np.concatenate([np.cos(ang), np.sin(ang)], 1).astype(f32).reshape(8, P, 64).transpose(1, 0, 2)
    wg = i["L0_ffn_wg"].reshape(64, 2, P, 96)
    wu = i["L0_ffn_wu"].reshape(64, 2, P, 96)
    wgu = np.stack([wg, wu], 1).transpose(0, 3, 1, 2, 4).reshape(32, 2, P, 384).transpose(0, 2, 1, 3)
    wd = i["L0_ffn_wd"].reshape(32, 2, 96, 256).transpose(0, 2, 1, 3)
    perm = lambda w: w.reshape(8, P, 2, w.shape[-1]).transpose(0, 2, 1, 3).reshape(2048, w.shape[-1]).T
    down = i["L1_ffn_down_W_packed"]
    arrays = {
        "x": i["L0_attn_u"].reshape(1024, 256),
        "w_in": fm(i["L0_attn_in_proj_w"].T), "w_out": fm(i["L0_attn_out_proj_w"].T), "gate_w": fm(i["L0_ffn_gate_w"].T),
        "wgu": wgu.reshape(32, P, 768), "wd": wd.reshape(32, 96, 512),
        "wmod": np.stack([fm(i["L0_wmod"]), fm(i["L1_wmod"])]),
        "ccol": np.concatenate([col(i["L0_c"].reshape(-1)), col(i["L1_c"].reshape(-1))], 1),
        "cols": np.concatenate([col(i["L0_attn_ln_w"]), col(i["L0_attn_ln_b"]), col(i["L0_attn_bnorm_w"]), col(i["L0_attn_cnorm_w"]),
                                col(i["L1_attn_q_norm_w"]), col(i["L1_attn_k_norm_w"])], 1),
        "rows": np.concatenate([i["L0_attn_D"], i["L0_attn_dt_bias"], i["L0_attn_A_log"],
                                8192 - 64 * np.arange(64, dtype=f32)])[None],
        "sinks": i["L1_attn_sink_logit"].reshape(8, 2).T,
        "rope": rope, "consts": consts,
        "wqc": fm(i["L1_attn_wq_comp"]), "wqup": i["L1_attn_wq_up"],
        "wkv": np.concatenate([fm(i["L1_attn_wk"]), fm(i["L1_attn_wv"])], 2),
        "w1": i["L1_attn_out_w1"].reshape(4, 4, P, 2, P).transpose(4, 0, 1, 3, 2).reshape(P, 16, 256),
        "w2": fm(i["L1_attn_out_w2"]),
        "gpk": perm(i["L1_ffn_gate_W_packed"]), "upk": perm(i["L1_ffn_up_W_packed"]),
        "dpk": down.T.reshape(8, P, 256).transpose(1, 0, 2),
        "gsc": perm(i["L1_ffn_gate_scales"]), "usc": perm(i["L1_ffn_up_scales"]), "dsc": i["L1_ffn_down_scales"].T,
    }
    return {n: np.ascontiguousarray(a) for n, a in arrays.items()}


def kernel(**inputs):
    import concourse.bacc as _bacc
    from concourse import mybir as _mybir
    from concourse.bass_utils import run_bass_kernel_spmd as _run

    nc = _bacc.Bacc("TRN2", target_bir_lowering=False, num_devices=1)
    arrays = {f"in_{n}": a for n, a in _layout(inputs).items()}
    args = [nc.dram_tensor(n, a.shape, _mybir.dt.from_np(a.dtype), kind="ExternalInput").ap() for n, a in arrays.items()]
    args.append(nc.dram_tensor("out_0", (1024, 256), _mybir.dt.float32, kind="ExternalOutput").ap())
    adaln_two_layers(nc, *args)
    r = _run(nc, [arrays], core_ids=[0])
    return r.results[0]["out_0"].reshape(1, 1024, 256)
```
